# Optimizing a Trainium2 kernel written in Bass

```python
import numpy as np
import jax
import jax.numpy as jnp

def _softmax(x, axis=-1):
    return jax.nn.softmax(x, axis=axis)

def _gelu(x):
    return jax.nn.gelu(x, approximate=True)

def _silu(x):
    return jax.nn.silu(x)

def _sigmoid(x):
    return jax.nn.sigmoid(x)

def _layernorm(x, axis=-1, eps=1e-05):
    m = jnp.mean(x, axis=axis, keepdims=True)
    v = jnp.var(x, axis=axis, keepdims=True)
    return (x - m) / jnp.sqrt(v + eps)

def _scatter_add(tgt, idx, src, axis=0):
    return tgt.at[idx].add(src)

def _segment_sum(src, seg, n):
    return jax.ops.segment_sum(src, seg, n)
kernel_name = 'mk_hybrid_d1_jaxref_r8_850f54'

def setup_inputs(seed: int=0):
    np.random.seed(seed)
    _w = jnp.asarray

    def _L0_attn_a_setup():
        import jax, jax.numpy as jnp
        import numpy as np
        B, L, D = (4, 512, 128)
        DS, EXP, DC = (16, 2, 4)
        DI = EXP * D
        K_SYM = max(3, 2 * DC + 1)

        def _linear(x, w, b):
            return jnp.einsum('blc,oc->blo', x, w) + b

        def _dwconv(x, kernel, bias, pad_l, pad_r):
            y = jax.lax.conv_general_dilated(x.transpose(0, 2, 1), kernel, window_strides=(1,), padding=[(pad_l, pad_r)], dimension_numbers=('NCH', 'OIH', 'NCH'), feature_group_count=x.shape[-1])
            return y.transpose(0, 2, 1) + bias

        def _rmsnorm(x, w, eps=1e-06):
            scale = jax.lax.rsqrt(jnp.mean(x * x, axis=-1, keepdims=True) + eps)
            return w * x * scale
        key = jax.random.key(seed)
        ks = jax.random.split(key, 12)

        def n(k, shape, s=0.02):
            return jax.random.normal(k, shape, jnp.float32) * s
        return {'x': jax.random.normal(ks[0], (B, L, D), jnp.float32), 'norm_w': jnp.ones((D,), jnp.float32), 'in_w': n(ks[1], (2 * DI, D)), 'in_b': jnp.zeros((2 * DI,), jnp.float32), 'dwa_k': n(ks[2], (DI, 1, DC)), 'dwa_b': jnp.zeros((DI,), jnp.float32), 'A': n(ks[3], (DI, DS)), 'Bm': n(ks[4], (DS, DI)), 'sym_k': n(ks[5], (DI, 1, K_SYM)), 'sym_b': jnp.zeros((DI,), jnp.float32), 'pw_w': n(ks[6], (DI, DI)), 'pw_b': jnp.zeros((DI,), jnp.float32), 'ha_w': n(ks[7], (DI // 2, DI)), 'ha_b': jnp.zeros((DI // 2,), jnp.float32), 'hb_w': n(ks[8], (DI // 2, DI)), 'hb_b': jnp.zeros((DI // 2,), jnp.float32), 'fuse_w': n(ks[9], (DI, DI)), 'fuse_b': jnp.zeros((DI,), jnp.float32), 'out_w': n(ks[10], (D, DI)), 'out_b': jnp.zeros((D,), jnp.float32)}
    _L0_attn_a_in = _L0_attn_a_setup()

    def _L0_attn_b_setup():
        import jax, jax.numpy as jnp
        import numpy as np
        EMBED_DIM = 128
        NUM_HEADS = 16
        HEAD_DIM = EMBED_DIM // NUM_HEADS
        key = jax.random.key(seed)
        k_x, k_qw, k_qb, k_ow, k_ob = jax.random.split(key, 5)
        B, S, E = (2, 256, EMBED_DIM)
        scale = 1.0 / np.sqrt(E)
        return {'x': jax.random.normal(k_x, (B, S, E), dtype=jnp.float32), 'qkv_w': jax.random.uniform(k_qw, (3 * E, E), jnp.float32, -scale, scale), 'qkv_b': jax.random.uniform(k_qb, (3 * E,), jnp.float32, -scale, scale), 'out_w': jax.random.uniform(k_ow, (E, E), jnp.float32, -scale, scale), 'out_b': jax.random.uniform(k_ob, (E,), jnp.float32, -scale, scale)}
    _L0_attn_b_in = _L0_attn_b_setup()

    def _L0_ffn_setup():
        import jax, jax.numpy as jnp
        import numpy as np

        def _bitlinear(x, w_latent):
            scale = jax.lax.stop_gradient(jnp.clip(jnp.mean(jnp.abs(w_latent), axis=1, keepdims=True), 1e-05, None))
            tern = jnp.clip(jnp.round(w_latent / scale), -1.0, 1.0)
            w = w_latent + jax.lax.stop_gradient(tern - w_latent)
            return x @ (w * scale).T
        key = jax.random.key(seed)
        ks = jax.random.split(key, 6)
        dim, hidden, rank = (128, 512, 16)
        B, S = (4, 512)
        x = jax.random.normal(ks[0], (B, S, dim), dtype=jnp.float32)
        w_fc = 0.02 * jax.random.normal(ks[1], (hidden, dim), dtype=jnp.float32)
        w_proj = 0.02 * jax.random.normal(ks[2], (dim, hidden), dtype=jnp.float32)
        u = 0.02 * jax.random.normal(ks[3], (hidden, rank), dtype=jnp.float32)
        v = 0.02 * jax.random.normal(ks[4], (rank, dim), dtype=jnp.float32)
        fast_b = jax.random.normal(ks[5], (rank, rank), dtype=jnp.float32)
        gate = jnp.float32(0.05)
        return {'x': x, 'fast_b': fast_b, 'w_fc': w_fc, 'w_proj': w_proj, 'u': u, 'v': v, 'gate': gate}
    _L0_ffn_in = _L0_ffn_setup()
    _d = {'L0_attn_a_x': _L0_attn_a_in['x'], 'L0_attn_a_norm_w': _L0_attn_a_in['norm_w'], 'L0_attn_a_in_w': _L0_attn_a_in['in_w'], 'L0_attn_a_in_b': _L0_attn_a_in['in_b'], 'L0_attn_a_dwa_k': _L0_attn_a_in['dwa_k'], 'L0_attn_a_dwa_b': _L0_attn_a_in['dwa_b'], 'L0_attn_a_A': _L0_attn_a_in['A'], 'L0_attn_a_Bm': _L0_attn_a_in['Bm'], 'L0_attn_a_sym_k': _L0_attn_a_in['sym_k'], 'L0_attn_a_sym_b': _L0_attn_a_in['sym_b'], 'L0_attn_a_pw_w': _L0_attn_a_in['pw_w'], 'L0_attn_a_pw_b': _L0_attn_a_in['pw_b'], 'L0_attn_a_ha_w': _L0_attn_a_in['ha_w'], 'L0_attn_a_ha_b': _L0_attn_a_in['ha_b'], 'L0_attn_a_hb_w': _L0_attn_a_in['hb_w'], 'L0_attn_a_hb_b': _L0_attn_a_in['hb_b'], 'L0_attn_a_fuse_w': _L0_attn_a_in['fuse_w'], 'L0_attn_a_fuse_b': _L0_attn_a_in['fuse_b'], 'L0_attn_a_out_w': _L0_attn_a_in['out_w'], 'L0_attn_a_out_b': _L0_attn_a_in['out_b'], 'L0_attn_b_qkv_w': _L0_attn_b_in['qkv_w'], 'L0_attn_b_qkv_b': _L0_attn_b_in['qkv_b'], 'L0_attn_b_out_w': _L0_attn_b_in['out_w'], 'L0_attn_b_out_b': _L0_attn_b_in['out_b'], 'L0_ffn_fast_b': _L0_ffn_in['fast_b'], 'L0_ffn_w_fc': _L0_ffn_in['w_fc'], 'L0_ffn_w_proj': _L0_ffn_in['w_proj'], 'L0_ffn_u': _L0_ffn_in['u'], 'L0_ffn_v': _L0_ffn_in['v'], 'L0_ffn_gate': _L0_ffn_in['gate']}
    _x0 = _d['L0_attn_a_x']
    _d['L0_attn_a_x'] = jax.random.normal(jax.random.fold_in(jax.random.key(seed), 1), (2, 1024, 128), dtype=_x0.dtype)
    del _x0
    return _d

def reference(L0_attn_a_x, L0_attn_a_norm_w, L0_attn_a_in_w, L0_attn_a_in_b, L0_attn_a_dwa_k, L0_attn_a_dwa_b, L0_attn_a_A, L0_attn_a_Bm, L0_attn_a_sym_k, L0_attn_a_sym_b, L0_attn_a_pw_w, L0_attn_a_pw_b, L0_attn_a_ha_w, L0_attn_a_ha_b, L0_attn_a_hb_w, L0_attn_a_hb_b, L0_attn_a_fuse_w, L0_attn_a_fuse_b, L0_attn_a_out_w, L0_attn_a_out_b, L0_attn_b_qkv_w, L0_attn_b_qkv_b, L0_attn_b_out_w, L0_attn_b_out_b, L0_ffn_fast_b, L0_ffn_w_fc, L0_ffn_w_proj, L0_ffn_u, L0_ffn_v, L0_ffn_gate):

    def _L0_attn_a_ref(x, norm_w, in_w, in_b, dwa_k, dwa_b, A, Bm, sym_k, sym_b, pw_w, pw_b, ha_w, ha_b, hb_w, hb_b, fuse_w, fuse_b, out_w, out_b):
        import jax, jax.numpy as jnp
        import numpy as np
        B, L, D = (4, 512, 128)
        DS, EXP, DC = (16, 2, 4)
        DI = EXP * D
        K_SYM = max(3, 2 * DC + 1)

        def _linear(x, w, b):
            return jnp.einsum('blc,oc->blo', x, w) + b

        def _dwconv(x, kernel, bias, pad_l, pad_r):
            y = jax.lax.conv_general_dilated(x.transpose(0, 2, 1), kernel, window_strides=(1,), padding=[(pad_l, pad_r)], dimension_numbers=('NCH', 'OIH', 'NCH'), feature_group_count=x.shape[-1])
            return y.transpose(0, 2, 1) + bias

        def _rmsnorm(x, w, eps=1e-06):
            scale = jax.lax.rsqrt(jnp.mean(x * x, axis=-1, keepdims=True) + eps)
            return w * x * scale
        residual = x
        h = _rmsnorm(x, norm_w)
        h = _linear(h, in_w, in_b)
        gate, val = (h[..., :DI], h[..., DI:])
        gate = jax.nn.sigmoid(gate)
        a = _dwconv(val, dwa_k, dwa_b, 1, 2)
        a = jnp.einsum('bld,ds->bls', a, A)
        a = jnp.einsum('bls,sd->bld', a, Bm)
        b = _dwconv(val, sym_k, sym_b, K_SYM // 2, K_SYM // 2)
        b = jax.nn.silu(b)
        b = _linear(b, pw_w, pw_b)
        a = _linear(a, ha_w, ha_b)
        b = _linear(b, hb_w, hb_b)
        y = jnp.concatenate([a, b], axis=-1)
        y = _linear(y, fuse_w, fuse_b)
        y = gate * y
        y = _linear(y, out_w, out_b)
        return residual + y

    def _L0_attn_b_ref(x, qkv_w, qkv_b, out_w, out_b):
        import jax, jax.numpy as jnp
        import numpy as np
        EMBED_DIM = 128
        NUM_HEADS = 16
        HEAD_DIM = EMBED_DIM // NUM_HEADS
        B, S, E = x.shape
        H, hd = (NUM_HEADS, HEAD_DIM)
        qkv = x @ qkv_w.T + qkv_b
        qkv = qkv.reshape(B, S, H, 3 * hd)
        qkv = jnp.transpose(qkv, (2, 0, 3, 1))
        q, k, v = jnp.split(qkv, 3, axis=2)
        scores = jnp.einsum('hbds,hbdt->hbst', q, k) / jnp.sqrt(jnp.float32(hd))
        w = jax.nn.softmax(scores, axis=-1)
        attn = jnp.einsum('hbst,hbdt->hbsd', w, v)
        attn = jnp.transpose(attn, (1, 3, 0, 2)).reshape(B, S, E)
        return attn @ out_w.T + out_b

    def _L0_ffn_ref(x, fast_b, w_fc, w_proj, u, v, gate):
        import jax, jax.numpy as jnp
        import numpy as np

        def _bitlinear(x, w_latent):
            scale = jax.lax.stop_gradient(jnp.clip(jnp.mean(jnp.abs(w_latent), axis=1, keepdims=True), 1e-05, None))
            tern = jnp.clip(jnp.round(w_latent / scale), -1.0, 1.0)
            w = w_latent + jax.lax.stop_gradient(tern - w_latent)
            return x @ (w * scale).T
        h = _bitlinear(x, w_fc) + gate * (x @ v.T @ fast_b.T @ u.T)
        r = jnp.maximum(h, 0.0)
        return _bitlinear(r * r, w_proj)
    x = L0_attn_a_x
    x = x + _L0_attn_a_ref(_layernorm(x, axis=-1), L0_attn_a_norm_w, L0_attn_a_in_w, L0_attn_a_in_b, L0_attn_a_dwa_k, L0_attn_a_dwa_b, L0_attn_a_A, L0_attn_a_Bm, L0_attn_a_sym_k, L0_attn_a_sym_b, L0_attn_a_pw_w, L0_attn_a_pw_b, L0_attn_a_ha_w, L0_attn_a_ha_b, L0_attn_a_hb_w, L0_attn_a_hb_b, L0_attn_a_fuse_w, L0_attn_a_fuse_b, L0_attn_a_out_w, L0_attn_a_out_b)
    x = x + _L0_ffn_ref(_layernorm(x, axis=-1), L0_ffn_fast_b, L0_ffn_w_fc, L0_ffn_w_proj, L0_ffn_u, L0_ffn_v, L0_ffn_gate)
    x = x + _L0_attn_b_ref(_layernorm(x, axis=-1), L0_attn_b_qkv_w, L0_attn_b_qkv_b, L0_attn_b_out_w, L0_attn_b_out_b)
    x = x + _L0_ffn_ref(_layernorm(x, axis=-1), L0_ffn_fast_b, L0_ffn_w_fc, L0_ffn_w_proj, L0_ffn_u, L0_ffn_v, L0_ffn_gate)
    return x

_drawn_inputs = setup_inputs


def setup_inputs(seed=0):
    import zlib

    import numpy as np

    out = dict(_drawn_inputs(seed))
    spreads = {'L0_attn_a_norm_w': (1.0, 0.6),
     'L0_attn_a_in_b': (0.0, 0.8),
     'L0_attn_a_dwa_b': (0.0, 0.8),
     'L0_attn_a_sym_b': (0.0, 0.8),
     'L0_attn_a_pw_b': (0.0, 0.8),
     'L0_attn_a_ha_b': (0.0, 0.8),
     'L0_attn_a_hb_b': (0.0, 0.8),
     'L0_attn_a_fuse_b': (0.0, 0.8),
     'L0_attn_a_out_b': (0.0, 0.8)}
    factors = {'L0_attn_a_in_w': 8.0,
     'L0_attn_a_dwa_k': 8.0,
     'L0_attn_a_A': 8.0,
     'L0_attn_a_Bm': 8.0,
     'L0_attn_a_sym_k': 8.0,
     'L0_attn_a_pw_w': 8.0,
     'L0_attn_a_ha_w': 8.0,
     'L0_attn_a_hb_w': 8.0,
     'L0_attn_a_fuse_w': 8.0,
     'L0_attn_a_out_w': 5.922,
     'L0_attn_b_qkv_w': 4.129,
     'L0_attn_b_qkv_b': 20.451,
     'L0_ffn_fast_b': 8.0,
     'L0_ffn_w_fc': 4.272,
     'L0_ffn_w_proj': 3.249,
     'L0_ffn_u': 8.0,
     'L0_ffn_v': 8.0,
     'L0_attn_b_out_b': 8.0}
    for name, (base, spread) in spreads.items():
        noise = np.random.default_rng([zlib.crc32(name.encode()), seed]).standard_normal(out[name].shape)
        drawn = base * np.exp(spread * noise) if base else spread * noise
        out[name] = jnp.asarray(drawn.astype(out[name].dtype))
    for name, factor in factors.items():
        out[name] = (out[name] * factor).astype(out[name].dtype)
    return out
```

```python
from contextlib import ExitStack

import concourse.bass as bass
from concourse import mybir

F32 = mybir.dt.float32
BF16 = mybir.dt.bfloat16
ALU = mybir.AluOpType
ACT = mybir.ActivationFunctionType
AX = mybir.AxisListType

P = 128
B, L, D = 2, 1024, 128
NT = B * L // P
BT = L // P
CH = 512
NCH = B * L // CH
TC = CH // P
DI = 2 * D
KC = DI // P
DS = 16
DC = 4
KS = 9
PAD = 4
LP = L + 2 * PAD
HID = 512
KH = HID // P
RANK = 16
H, HD = 16, 8
QH = 4
GQ = H // QH
NQ = B * GQ
PARTS = 3
QK_ROWS = PARTS * PARTS * HD
SHIFT_ROW = QK_ROWS
ROWS = 96
NBUF = 3
VW = 32
EPS_LN, EPS_RMS = 1e-5, 1e-6
SCALE = float(HD) ** -0.5
UNITS = [3, 2] * 6 + [2, 0, 0, 0]
STEPS = 2 * BT
NPB = 4
assert len(UNITS) == STEPS and sum(UNITS) == QH * BT and STEPS % NPB == 0

IN_B, SYM_B, DWA_B, PW_B, HA_B, HB_B, FU_B, NORM, BQ, BK = 0, 4, 6, 8, 10, 11, 12, 14, 15, 16
NVEC = 17
TURN_MIX, TURN_F1, TURN_QKV, TURN_F2 = (NCH * i for i in range(4))
TOK_MIX, TOK_F1, TOK_V, TOK_AO, TOK_F2 = (NCH * i for i in range(5))
VAR0 = (0, 2, 2 + NCH, 2 + 2 * NCH)
SETUP_VCOL = 1
WIDE_IN = 0
WIDE_Y = WIDE_IN + 4 * NCH
WIDE_F1 = WIDE_Y + KC * NCH
WIDE_QK = WIDE_F1 + KH * NCH
WIDE_F2 = WIDE_QK + 2 * NCH


def build(nc, ins, out):
    x_d, norm_w, in_w, in_b, dwa_k, dwa_b, A_d, Bm_d, sym_k, sym_b, pw_w, pw_b, ha_w, ha_b, hb_w, hb_b, \
        fuse_w, fuse_b, out_w, out_b, qkv_w, qkv_b, ao_w, ao_b, fb_d, wfc_d, wproj_d, u_d, v_d, gate_d = ins
    ctx = ExitStack()
    with ctx:
        def sb(name, shape, dt=F32):
            return ctx.enter_context(nc.sbuf_tensor(name, shape, dt))

        def sem(name):
            return ctx.enter_context(nc.semaphore(name))

        in_n = sb("in_n", [P, 4, D])
        hb_n = sb("hb_n", [P, DI])
        ha_n = sb("ha_n", [P, DI])
        fu_n = sb("fu_n", [P, KC, DI])
        ow_n = sb("ow_n", [P, DI])
        bm_n = sb("bm_n", [DS, DI])
        pw_n = sb("pw_n", [P, KC, DI])
        a_n = sb("a_n", [P, KC, DS])
        kdwa = sb("kdwa", [P, KC, DC])
        ksym = sb("ksym", [P, KC, KS])
        qkv_n = sb("qkv_n", [P, 3, D])
        ao_n = sb("ao_n", [P, D])
        wfc_n = sb("wfc_n", [P, KH, D])
        wpr_n = sb("wpr_n", [P, HID])
        u_n = sb("u_n", [P, KH, RANK])
        v_n = sb("v_n", [RANK, D])
        fb_n = sb("fb_n", [RANK, RANK])
        gate_n = sb("gate_n", [RANK, 1])
        vec_n = sb("vec_n", [NVEC, P])
        ob_bc = sb("ob_bc", [P, D])
        bv_bc = sb("bv_bc", [P, D])
        aob_bc = sb("aob_bc", [P, D])
        ident = sb("ident", [P, P])
        vcol = sb("vcol", [P, NVEC])
        in_T = sb("in_T", [P, 4, D])
        hh_T = sb("hh_T", [P, 4, P])
        fu_T = sb("fu_T", [P, 2, DI])
        ob_T = sb("ob_T", [P, 2 * P + 2 * DS])
        att_T = sb("att_T", [P, 4, P])
        u_T = sb("u_T", [RANK, HID])
        wp_T = sb("wp_T", [P, KH, D])
        fc_T = sb("fc_T", [P, HID])
        lowrank = sb("lowrank", [P, HID])
        z_s = sb("z_s", [RANK, HID])
        xy = sb("xy", [P, DI + DS])
        y1rep = sb("y1rep", [P, P])
        wb_T = sb("wb_T", [P, KC, DI])
        g_T = sb("g_T", [P, DI])
        ua = sb("ua", [P, KC, P])
        v1 = sb("v1", [DS, 1])
        v2 = sb("v2", [P, KC])
        v3 = sb("v3", [P, 1])
        w1 = sb("w1", [P, 1])
        cb = sb("cb", [P, KC])
        tern_fc = sb("tern_fc", [P, KH, D])
        tern_lo = sb("tern_lo", [P, HID])
        tern_pr = sb("tern_pr", [P, HID])
        tern_pl = sb("tern_pl", [P, HID])
        sc = sb("sc", [P, 4, KH + 1])
        x = sb("x", [P, NT, D])
        xr = sb("xr", [P, NT, D])
        h = sb("h", [P, NT, D])
        hT = sb("hT", [P, B * L])
        gate = sb("gate", [P, B, KC, L])
        val = sb("val", [P, B, KC, LP])
        acc = sb("acc", [P, B, KC, L])
        us = sb("us", [P, B, LP])
        st = sb("st", [P, 4, NT, 6])
        mv = sb("mv", [P, 4, NT, 2])
        small = sb("small", [P, 4, 8, NT])
        xr_c = sb("xr_c", [P, 2, NT])
        r_buf = gate[:, :, :, :].rearrange("p b k l -> p b (k l)").rearrange("p b (m c) -> p b m c", m=KH)
        r2_buf = acc[:, :, :, :].rearrange("p b k l -> p b (k l)").rearrange("p b (m c) -> p b m c", m=KH)
        gate_f = gate[:, :, :, :].rearrange("p b k l -> p (b k l)")
        acc_f = acc[:, :, :, :].rearrange("p b k l -> p (b k l)")
        val_h = val[:, :, :, :].rearrange("p b k l -> p (b k l)").bitcast(BF16)
        qk_f = gate_f[:, 0:4 * CH].rearrange("p (a w c) -> p a w c", a=2, w=2)
        qk_r = gate_f[:, 4 * CH:8 * CH].rearrange("p (a w c) -> p a w c", a=2, w=2)
        qk_s = acc_f.bitcast(BF16)[:, 0:4 * PARTS * CH].rearrange("p (a w i c) -> p a w i c", a=2, w=2, i=PARTS)
        v_tok = us[:, :, :].rearrange("p b l -> p (b l)")[:, 0:NT * H * HD].rearrange("p (i d) -> p i d", i=NT)
        qt = [sb(f"qt{r}", [ROWS, QH, L], BF16)[:, :, :] for r in range(NBUF - 1)]
        kt = [sb(f"kt{r}", [ROWS, QH, L], BF16)[:, :, :] for r in range(NBUF - 1)]
        for i, buf in enumerate((qt, kt)):
            buf.append(val_h[0:ROWS, i * QH * L:(i + 1) * QH * L].rearrange("p (j t) -> p j t", j=QH))
        v4 = [sb(f"v4_{r}", [P, BT, QH, VW]) for r in range(NBUF)]
        ones_rows = xr[:, :, :].rearrange("p i d -> p (i d)").bitcast(BF16)[0:PARTS, :]
        pexp = [gate[:, 0, :, :], gate[:, 1, :, :], acc[:, 0, :, :], acc[:, 1, :, :]]
        pexp = [b.rearrange("p k l -> p (k l)").rearrange("p (j c) -> p j c", j=QH) for b in pexp]
        o_sb = sb("o_sb", [P, CH])
        o_rc = sb("o_rc", [P, TC, QH])
        attn = sb("attn", [P, NQ, HD, QH * BT])
        mx = sb("mx", [P, QH * BT])
        nm = sb("nm", [QH * BT, P])
        nr = sb("nr", [QH * BT, P])
        nm_s = sb("nm_s", [QH * BT, PARTS, P], BF16)

        ps = [ctx.enter_context(nc.psum_tensor(f"ps{i}", [P, CH], F32)) for i in range(4)]
        pm = [ctx.enter_context(nc.psum_tensor(f"pm{i}", [P, 2, CH], F32)) for i in range(2)]
        ps = ps + [pm[0][:, 0, :], pm[0][:, 1, :], pm[1][:, 0, :], pm[1][:, 1, :]]

        def bank(i):
            return ps[i][:, :] if i < 4 else ps[i]

        q_scr = nc.dram_tensor("q_scr", [PARTS, P, B * L], BF16, kind="Internal").ap()
        k_scr = nc.dram_tensor("k_scr", [PARTS, P, B * L], BF16, kind="Internal").ap()

        s_x, s_w_in, s_w_mix, s_vec = sem("s_x"), sem("s_w_in"), sem("s_w_mix"), sem("s_vec")
        s_w_ffn, s_w_att = sem("s_w_ffn"), sem("s_w_att")
        ident_zero, ident_ready, pads_ready = sem("ident_zero"), sem("ident_ready"), sem("pads_ready")
        consts_ready, v4_zero, v4_ones = sem("consts_ready"), sem("v4_zero"), sem("v4_ones")
        dve_step, rc_ready, shift_step, xr_step = sem("dve_step"), sem("rc_ready"), sem("shift_step"), sem("xr_step")
        setup_mm, setup_ev, tern_ready, ua_ready = sem("setup_mm"), sem("setup_ev"), sem("tern_ready"), sem("ua_ready")
        var_ready, std_ready, xn_ready = sem("var_ready"), sem("std_ready"), sem("xn_ready")
        xr_coef, xr_ready = sem("xr_coef"), sem("xr_ready")
        turn_mm, turned = sem("turn_mm"), sem("turned")
        wide_mm, wide_read = sem("wide_mm"), sem("wide_read")
        tok_mm, tok_read = sem("tok_mm"), sem("tok_read")
        u_mm, u_read, conv_done, silu_done = sem("u_mm"), sem("u_read"), sem("conv_done"), sem("silu_done")
        sq_ready, relu_ready = sem("sq_ready"), sem("relu_ready")
        qk_ready, split_ready = sem("qk_ready"), sem("split_ready")
        scr_done = [sem(f"scr_done{i}") for i in range(2)]
        qk_in = [sem(f"qk_in{r}") for r in range(NBUF)]
        shift_in, v4_ready = sem("shift_in"), sem("v4_ready")
        exp_mm, exp_done, pv_mm = sem("exp_mm"), sem("exp_done"), sem("pv_mm")
        o_copied, o_turned, o_normed = sem("o_copied"), sem("o_turned"), sem("o_normed")
        max_mm, max_done = sem("max_mm"), sem("max_done")
        mx_turned, shift_split = sem("mx_turned"), sem("shift_split")
        attn_flat = sem("attn_flat")
        ao_biased, stored = sem("ao_biased"), sem("stored")

        x_src = x_d.rearrange("b (i p) d -> p (b i) d", p=P)
        out_dst = out.rearrange("b (i p) d -> p (b i) d", p=P)
        block = ctx.enter_context(nc.Block())

        def row(v):
            return v.rearrange("(m p) -> m p", p=P)

        @block.sync
        def _(sp):
            for c in range(NCH):
                sp.dma_start(x[:, TC * c:TC * c + TC, :], x_src[:, TC * c:TC * c + TC, :]).then_inc(s_x, 16)
            sp.dma_start(in_n[:, :, :], in_w.rearrange("(m p) d -> p m d", p=P)).then_inc(s_w_in, 16)
            sp.dma_start(wfc_n[:, :, :], wfc_d.rearrange("(m p) d -> p m d", p=P)).then_inc(s_w_ffn, 16)
            sp.dma_start(wpr_n[:, :], wproj_d).then_inc(s_w_ffn, 16)
            sp.dma_start(u_n[:, :, :], u_d.rearrange("(m p) r -> p m r", p=P)).then_inc(s_w_ffn, 16)
            sp.dma_start(v_n[:, :], v_d).then_inc(s_w_ffn, 16)
            sp.dma_start(fb_n[:, :], fb_d).then_inc(s_w_ffn, 16)
            sp.dma_start(gate_n[:, :], gate_d.broadcast_to([RANK, 1])).then_inc(s_w_ffn, 16)
            for c in range(NCH):
                for w, scr in ((0, q_scr), (1, k_scr)):
                    sp.wait_ge(split_ready, 2 * c + w + 1)
                    sp.dma_start(scr[:, :, c * CH:(c + 1) * CH].rearrange("i p t -> p i t"),
                                 qk_s[:, c % 2, w, :, :]).then_inc(scr_done[c % 2], 16)

            def load_quad(n):
                b, g = divmod(n, GQ)
                cols = slice(b * L, (b + 1) * L)
                rows = slice(g * QH * HD, (g + 1) * QH * HD)
                for i in range(PARTS):
                    for rep in range(PARTS):
                        at_q = (i * PARTS + rep) * HD
                        at_k = (rep * PARTS + i) * HD
                        for buf, scr, at in ((qt, q_scr, at_q), (kt, k_scr, at_k)):
                            src = scr[i, rows, cols].rearrange("(j d) t -> d j t", d=HD)
                            sp.dma_start(buf[n % NBUF][at:at + HD, :, :], src).then_inc(qk_in[n % NBUF], 16)

            def load_shift(n):
                sp.wait_ge(shift_split, n + 1)
                for i in range(PARTS):
                    dst = qt[n % NBUF][SHIFT_ROW + i:SHIFT_ROW + i + 1, :, :]
                    sp.dma_start(dst.rearrange("a j (k p) -> a (j k) p", p=P),
                                 nm_s[:, i, :]).then_inc(shift_in, 16)

            sp.wait_ge(consts_ready, 2 * NBUF + 1)
            for r in range(NBUF):
                sp.dma_start(kt[r][SHIFT_ROW:SHIFT_ROW + PARTS, :, :].rearrange("i j t -> i (j t)"),
                             ones_rows).then_inc(qk_in[r], 16)
            for i in range(2):
                sp.wait_ge(scr_done[i], 16 * 2 * NCH // 2)
            for n in range(NBUF):
                load_quad(n)
            load_shift(0)
            for n in range(NQ - 1):
                if 1 <= n and n + 2 < NQ:
                    sp.wait_ge(exp_mm, STEPS * QH * n)
                    load_quad(n + 2)
                load_shift(n + 1)
            for c in range(NCH):
                sp.wait_ge(tok_read, TOK_F2 + c + 1)
                sp.dma_start(out_dst[:, TC * c:TC * c + TC, :], x[:, TC * c:TC * c + TC, :]).then_inc(stored, 16)
            sp.wait_ge(stored, 16 * NCH)

        @block.gpsimd
        def _(pool):
            pool.memset(ident[:, :], 0.0).then_inc(ident_zero, 1)
            pool.wait_ge(ident_zero, 1)
            pool.affine_select(out=ident[:, :], in_=ident[:, :], compare_op=ALU.not_equal, fill=1.0, base=0,
                               pattern=[[-1, P]], channel_multiplier=1).then_inc(ident_ready, 1)
            for w in range(3):
                src = qkv_w.rearrange("(h w d) e -> w h d e", w=3, d=HD)[w]
                pool.dma_start(qkv_n[:, w, :], src).then_inc(s_w_att, 16)
            pool.dma_start(ao_n[:, :], ao_w).then_inc(s_w_att, 16)
            pool.dma_start(aob_bc[:, :], ao_b.rearrange("(a d) -> a d", a=1).broadcast_to([P, D])).then_inc(s_w_att, 16)
            pool.dma_start(ob_bc[:, :], out_b.rearrange("(a d) -> a d", a=1).broadcast_to([P, D])).then_inc(s_w_att, 16)
            src = qkv_b.rearrange("(a h w d) -> w a h d", a=1, w=3, d=HD)[2].broadcast_to([P, H, HD])
            pool.dma_start(bv_bc[:, :].rearrange("p (h d) -> p h d", d=HD), src).then_inc(s_w_att, 16)
            edges = val[:, :, :, :].rearrange("p b k l -> p (b k) l")
            pool.memset(edges[:, :, 0:PAD], 0.0).then_inc(pads_ready, 1)
            pool.memset(edges[:, :, PAD + L:LP], 0.0).then_inc(pads_ready, 1)
            pool.memset(us[:, :, :], 0.0).then_inc(pads_ready, 1)
            pool.memset(ua[:, :, :], 0.0).then_inc(pads_ready, 1)
            pool.memset(y1rep[:, :], 0.0).then_inc(pads_ready, 1)
            pool.wait_ge(xr_coef, 2)
            for i in range(NT):
                pool.tensor_scalar(xr[:, i, :], x[:, i, :], xr_c[:, 0, i:i + 1], xr_c[:, 1, i:i + 1],
                                   ALU.mult, ALU.add).then_inc(xr_step, 1)
            pool.wait_ge(s_w_att, 16 * 7)
            for i in range(NT):
                pool.wait_ge(xr_step, i + 1)
                pool.tensor_tensor(xr[:, i, :], xr[:, i, :], ob_bc[:, :], ALU.add).then_inc(xr_ready, 1)
            pool.wait_ge(tok_read, TOK_MIX + NCH)
            for r in range(NBUF):
                pool.memset(v4[r][:, :, :, :], 0.0).then_inc(v4_zero, 1)
            pool.wait_ge(v4_zero, NBUF)
            for r in range(NBUF):
                pool.memset(qt[r][64:ROWS, :, :].bitcast(F32), 0.0).then_inc(consts_ready, 1)
                pool.memset(kt[r][64:ROWS, :, :].bitcast(F32), 0.0).then_inc(consts_ready, 1)
            pool.wait_ge(consts_ready, 2 * NBUF)
            pool.memset(ones_rows, 1.0).then_inc(consts_ready, 1)
            pool.wait_ge(consts_ready, 2 * NBUF + 1)
            for r in range(NBUF):
                pool.memset(v4[r][:, :, :, HD:HD + 1], 1.0).then_inc(v4_ones, 1)
            pool.wait_ge(v4_ones, NBUF)
            for i in range(NT):
                pool.wait_ge(xn_ready, NCH * 2 + i // TC + 1)
                pool.tensor_tensor(x[:, i, :], x[:, i, :], aob_bc[:, :], ALU.add).then_inc(ao_biased, 1)
            pool.wait_ge(tok_read, TOK_V + NCH)
            for n in range(NQ):
                b, g = divmod(n, GQ)
                if n >= NBUF:
                    pool.wait_ge(pv_mm, STEPS * (n - NBUF + 1))
                src = v_tok[:, b * BT:(b + 1) * BT, g * QH * HD:(g + 1) * QH * HD]
                pool.tensor_copy(v4[n % NBUF][:, :, :, 0:HD],
                                 src.rearrange("p c (j d) -> p c j d", d=HD)).then_inc(v4_ready, 1)

        @block.scalar
        def _(act):
            for dst, src in ((pw_n[:, :, :], pw_w.rearrange("(k p) c -> p k c", p=P)), (hb_n[:, :], hb_w),
                             (ha_n[:, :], ha_w), (fu_n[:, :, :], fuse_w.rearrange("(k p) c -> p k c", p=P)),
                             (ow_n[:, :], out_w), (bm_n[:, :], Bm_d),
                             (a_n[:, :, :], A_d.rearrange("(k p) s -> p k s", p=P)),
                             (kdwa[:, :, :], dwa_k.rearrange("(k p) o t -> p k (o t)", p=P)),
                             (ksym[:, :, :], sym_k.rearrange("(k p) o t -> p k (o t)", p=P))):
                act.dma_start(dst, src).then_inc(s_w_mix, 16)
            for at, v in ((IN_B, in_b), (SYM_B, sym_b), (DWA_B, dwa_b), (PW_B, pw_b), (HA_B, ha_b), (HB_B, hb_b),
                          (FU_B, fuse_b), (NORM, norm_w)):
                rows = v.rearrange("(m p) -> m p", p=P)
                act.dma_start(vec_n[at:at + rows.shape[0], :], rows).then_inc(s_vec, 16)
            for at, w in ((BQ, 0), (BK, 1)):
                src = qkv_b.rearrange("(a h w d) -> w a h d", a=1, w=3, d=HD)[w]
                act.dma_start(vec_n[at:at + 1, :].rearrange("a (h d) -> a h d", d=HD), src).then_inc(s_vec, 16)

            def root(f, lo, hi, k=0):
                act.activation(small[:, f, k + 1, lo:hi], small[:, f, k, lo:hi], ACT.Sqrt).then_inc(std_ready, 1)

            def turn_copy(i):
                c = i % NCH
                act.wait_ge(turn_mm, i + 1)
                act.activation(hT[:, c * CH:(c + 1) * CH], bank(i % 2), ACT.Copy).then_inc(turned, 1)

            for k in range(2):
                act.wait_ge(var_ready, k + 1)
                root(0, 0, NT, 4 * k)
            act.wait_ge(pads_ready, 5)
            act.wait_ge(setup_ev, SETUP_VCOL)
            for b in range(B):
                for q in range(2):
                    turn_copy(TURN_MIX + 2 * b + q)
                for q in range(2):
                    for m in range(4):
                        i = WIDE_IN + (2 * b + q) * 4 + m
                        act.wait_ge(wide_mm, i + 1)
                        src, bias = bank(2 + i % 4), vcol[:, IN_B + m:IN_B + m + 1]
                        if m < KC:
                            act.activation(gate[:, b, m, q * CH:(q + 1) * CH], src, ACT.Sigmoid,
                                           bias=bias).then_inc(wide_read, 1)
                        else:
                            act.activation(val[:, b, m - KC, PAD + q * CH:PAD + (q + 1) * CH], src, ACT.Identity,
                                           bias=bias).then_inc(wide_read, 1)
            for b in range(B):
                for q in range(2):
                    act.wait_ge(u_mm, 2 * b + q + 1)
                    for t in range(DC):
                        at = PAD + q * CH + 1 - t
                        act.activation(us[32 * t:32 * t + 32, b, at:at + CH], bank(6 + q)[32 * t:32 * t + 32, :],
                                       ACT.Copy).then_inc(u_read, 1)
            for b in range(B):
                for k in range(KC):
                    act.wait_ge(conv_done, KC * b + k + 1)
                    act.activation(acc[:, b, k, :], acc[:, b, k, :], ACT.Silu).then_inc(silu_done, 1)

            def ffn(f, turn0, wide0, sq0):
                act.wait_ge(var_ready, VAR0[f] + 1)
                root(f, 0, TC)
                turn_copy(turn0)
                for c in range(NCH):
                    if c + 1 < NCH:
                        act.wait_ge(var_ready, VAR0[f] + c + 2)
                        root(f, TC * (c + 1), TC * (c + 2))
                    for m in range(KH):
                        i = wide0 + KH * c + m
                        act.wait_ge(wide_mm, i + 1)
                        if c >= 2:
                            act.wait_ge(sq_ready, sq0 + KH * (c - 2) + m + 1)
                        act.activation(r_buf[:, c % 2, m, :], bank(2 + i % 4), ACT.Relu).then_inc(wide_read, 1)
                    if c + 1 < NCH:
                        turn_copy(turn0 + c + 1)

            ffn(1, TURN_F1, WIDE_F1, 0)

            act.wait_ge(var_ready, VAR0[2] + 1)
            root(2, 0, TC)
            turn_copy(TURN_QKV)
            for c in range(NCH):
                if c + 1 < NCH:
                    act.wait_ge(var_ready, VAR0[2] + c + 2)
                    root(2, TC * (c + 1), TC * (c + 2))
                for w in range(2):
                    i = WIDE_QK + 2 * c + w
                    act.wait_ge(wide_mm, i + 1)
                    if c >= 2:
                        act.wait_ge(split_ready, 2 * (c - 2) + w + 1)
                        act.wait_ge(scr_done[c % 2], 16 * 2 * (c // 2))
                    bias = vcol[:, BQ + w:BQ + w + 1]
                    act.activation(qk_f[:, c % 2, w, :], bank(2 + i % 4), ACT.Identity, bias=bias).then_inc(qk_ready, 1)
                    act.activation(qk_s[:, c % 2, w, 0, :], bank(2 + i % 4), ACT.Identity,
                                   bias=bias).then_inc(wide_read, 1)
                if c + 1 < NCH:
                    turn_copy(TURN_QKV + c + 1)

            def copy_o(hn):
                act.wait_ge(pv_mm, BT * hn + BT)
                if not isinstance(hn, int) or hn >= 1:
                    act.wait_ge(o_turned, hn)
                act.activation(o_sb[:, :], bank(2), ACT.Copy).then_inc(o_copied, 1)

            def quad(n, first):
                for s in range(STEPS):
                    if not (first and s < NPB):
                        act.wait_ge(pv_mm, n * STEPS + (s - NPB + 1))
                    for j in range(QH):
                        act.wait_ge(exp_mm, n * (STEPS * QH) + (s * QH + j + 1))
                        act.activation(pexp[s % NPB][:, j, :], bank(j % 2), ACT.Exp,
                                       scale=SCALE).then_inc(exp_done, 1)
                    if s == 0 and not first:
                        copy_o(n * 2 - 1)
                    if s == BT:
                        copy_o(n * 2)

            quad(0, True)
            with act.Fori(0, 2) as i:
                for q in range(NBUF):
                    quad(i * NBUF + (1 + q), False)
            quad(NQ - 1, False)
            copy_o(2 * NQ - 1)
            ffn(3, TURN_F2, WIDE_F2, KH * NCH)

        @block.vector
        def _(dve):
            steps = [0]

            def settled(ins):
                steps[0] += 1
                ins.then_inc(dve_step, 1)
                dve.wait_ge(dve_step, steps[0])

            def stats(f, lo, hi):
                for i in range(lo, hi):
                    ins = dve.bn_stats(st[:, f, i, :], x[:, i, :])
                    ins.then_inc(dve_step, 1)
                steps[0] += hi - lo
                dve.wait_ge(dve_step, steps[0])
                for i in range(lo, hi):
                    ins = dve.bn_aggr(mv[:, f, i, :], st[:, f, i, :])
                    ins.then_inc(dve_step, 1)
                steps[0] += hi - lo
                dve.wait_ge(dve_step, steps[0])
                dve.tensor_scalar(small[:, f, 0, lo:hi], mv[:, f, lo:hi, 1], EPS_LN, None,
                                  ALU.add).then_inc(var_ready, 1)

            def norm(f, c):
                lo, hi = TC * c, TC * (c + 1)
                stats(f, lo, hi)
                dve.wait_ge(std_ready, VAR0[f] + c + 1)
                settled(dve.reciprocal(small[:, f, 2, lo:hi], small[:, f, 1, lo:hi]))
                settled(dve.scalar_tensor_tensor(out=small[:, f, 3, lo:hi], in0=mv[:, f, lo:hi, 0], scalar=-1.0,
                                                 in1=small[:, f, 2, lo:hi], op0=ALU.mult, op1=ALU.mult))
                for i in range(lo, hi):
                    ins = dve.tensor_scalar(h[:, i, :], x[:, i, :], small[:, f, 2, i:i + 1],
                                            small[:, f, 3, i:i + 1], ALU.mult, ALU.add)
                    if i == hi - 1:
                        ins.then_inc(xn_ready, 1)

            dve.wait_ge(s_x, 16 * NCH)
            stats(0, 0, NT)
            dve.wait_ge(std_ready, 1)
            rstd, nmr = small[:, 0, 2, :], small[:, 0, 3, :]
            settled(dve.reciprocal(rstd, small[:, 0, 1, :]))
            dve.tensor_scalar(xr_c[:, 0, :], rstd, 1.0, None, ALU.add).then_inc(xr_coef, 1)
            settled(dve.scalar_tensor_tensor(out=nmr, in0=mv[:, 0, :, 0], scalar=-1.0, in1=rstd,
                                             op0=ALU.mult, op1=ALU.mult))
            dve.tensor_copy(xr_c[:, 1, :], nmr).then_inc(xr_coef, 1)
            settled(dve.tensor_tensor(small[:, 0, 6, :], rstd, rstd, ALU.mult))
            settled(dve.tensor_tensor(small[:, 0, 7, :], small[:, 0, 6, :], mv[:, 0, :, 1], ALU.mult))
            dve.tensor_scalar(small[:, 0, 4, :], small[:, 0, 7, :], EPS_RMS, None, ALU.add).then_inc(var_ready, 1)
            dve.wait_ge(std_ready, 2)
            settled(dve.reciprocal(small[:, 1, 4, :], small[:, 0, 5, :]))
            dve.tensor_tensor(small[:, 1, 5, :], small[:, 1, 4, :], rstd, ALU.mult).then_inc(dve_step, 1)
            steps[0] += 1
            settled(dve.tensor_tensor(small[:, 1, 6, :], small[:, 1, 4, :], nmr, ALU.mult))
            for c in range(NCH):
                for i in range(TC * c, TC * (c + 1)):
                    ins = dve.tensor_scalar(h[:, i, :], x[:, i, :], small[:, 1, 5, i:i + 1],
                                            small[:, 1, 6, i:i + 1], ALU.mult, ALU.add)
                ins.then_inc(xn_ready, 1)

            dve.wait_ge(s_w_ffn, 16 * 6)
            wfc = wfc_n[:, :, :]
            dve.tensor_reduce(sc[:, 0, 0:KH], wfc, AX.X, ALU.add,
                              apply_absolute_value=True).then_inc(dve_step, 1)
            steps[0] += 1
            settled(dve.tensor_reduce(sc[:, 0, KH:KH + 1], wpr_n[:, :], AX.X, ALU.add, apply_absolute_value=True))
            dve.tensor_scalar(sc[:, 1, 0:KH], sc[:, 0, 0:KH], 1.0 / D, 1e-5, ALU.mult, ALU.max).then_inc(dve_step, 1)
            steps[0] += 1
            settled(dve.tensor_scalar(sc[:, 1, KH:KH + 1], sc[:, 0, KH:KH + 1], 1.0 / HID, 1e-5, ALU.mult, ALU.max))
            dve.tensor_scalar(sc[:, 2, :], sc[:, 1, :], 0.5, None, ALU.mult).then_inc(dve_step, 1)
            dve.tensor_scalar(sc[:, 3, :], sc[:, 1, :], -0.5, None, ALU.mult).then_inc(dve_step, 1)
            steps[0] += 2
            dve.wait_ge(dve_step, steps[0])
            pairs = [(wfc_n[:, m, :], tern_fc[:, m, :], tern_lo[:, m * D:(m + 1) * D], m) for m in range(KH)]
            pairs.append((wpr_n[:, :], tern_pr[:, :], tern_pl[:, :], KH))
            for w, hi, lo, m in pairs:
                dve.tensor_scalar(hi, w, sc[:, 2, m:m + 1], sc[:, 1, m:m + 1], ALU.is_gt,
                                  ALU.mult).then_inc(dve_step, 1)
                dve.tensor_scalar(lo, w, sc[:, 3, m:m + 1], sc[:, 1, m:m + 1], ALU.is_lt,
                                  ALU.mult).then_inc(dve_step, 1)
            steps[0] += 2 * len(pairs)
            dve.wait_ge(dve_step, steps[0])
            dve.tensor_tensor(tern_fc[:, :, :].rearrange("p m d -> p (m d)"),
                              tern_fc[:, :, :].rearrange("p m d -> p (m d)"), tern_lo[:, :],
                              ALU.subtract).then_inc(tern_ready, 1)
            dve.tensor_tensor(tern_pr[:, :], tern_pr[:, :], tern_pl[:, :], ALU.subtract).then_inc(tern_ready, 1)

            def ev(ins):
                ins.then_inc(setup_ev, 1)

            def made(k):
                dve.wait_ge(setup_mm, k)

            made(1)
            ev(dve.tensor_copy(vcol[:, :], bank(0)[:, 0:NVEC]))
            made(2)
            dve.wait_ge(setup_ev, 1)
            ev(dve.tensor_scalar(in_T[:, :, :].rearrange("p m o -> p (m o)"), bank(1), vcol[:, NORM:NORM + 1],
                                 None, ALU.mult))
            made(3)
            ev(dve.tensor_copy(hh_T[:, :, :].rearrange("p m o -> p (m o)"), bank(2)))
            made(4)
            ev(dve.tensor_copy(fu_T[:, :, :].rearrange("p m o -> p (m o)"), bank(3)))
            made(5)
            ev(dve.tensor_copy(ob_T[:, :], bank(4)[:, 0:2 * P + 2 * DS]))
            made(6)
            ev(dve.tensor_copy(att_T[:, :, :].rearrange("p m o -> p (m o)"), bank(5)))
            made(7)
            ev(dve.tensor_copy(u_T[:, :], bank(6)[0:RANK, :]))
            made(8)
            ev(dve.tensor_copy(wp_T[:, :, :].rearrange("p m o -> p (m o)"), bank(7)))
            made(9)
            ev(dve.tensor_copy(xy[:, :], bank(0)[:, 0:DI + DS]))
            made(10)
            ev(dve.tensor_scalar(z_s[:, :], bank(1)[0:RANK, :], gate_n[:, 0:1], None, ALU.mult))
            made(11)
            ev(dve.tensor_copy(v1[:, :], bank(4)[0:DS, 0:1]))
            dve.wait_ge(setup_ev, 9)
            dve.wait_ge(pads_ready, 5)
            for t in range(DC):
                ins = dve.tensor_copy(y1rep[:, 32 * t:32 * t + DS], xy[:, DI:DI + DS])
            ev(ins)
            made(12)
            ev(dve.tensor_copy(wb_T[:, :, :].rearrange("p m o -> p (m o)"), bank(2)))
            made(13)
            ev(dve.tensor_copy(g_T[:, :], bank(3)[:, 0:DI]))
            made(14)
            ev(dve.tensor_copy(lowrank[:, :], bank(6)))
            made(15)
            dve.wait_ge(setup_ev, 15)
            ev(dve.tensor_tensor(fc_T[:, :], bank(5), lowrank[:, :], ALU.add))
            made(16)
            ev(dve.tensor_copy(v2[:, :], bank(0)[:, 0:KC]))
            made(17)
            ev(dve.tensor_tensor(w1[:, :], bank(1)[:, 0:1], vcol[:, HB_B:HB_B + 1], ALU.add))
            made(18)
            ev(dve.tensor_tensor(v3[:, :], bank(2)[:, 0:1], vcol[:, HA_B:HA_B + 1], ALU.add))
            made(19)
            ev(dve.tensor_tensor(cb[:, :], bank(3)[:, 0:KC], vcol[:, FU_B:FU_B + KC], ALU.add))
            dve.wait_ge(s_w_mix, 16 * 9)
            for k in range(KC):
                for t in range(DC):
                    ins = dve.tensor_scalar(ua[:, k, 32 * t:32 * t + DS], a_n[:, k, :], kdwa[:, k, t:t + 1], None,
                                            ALU.mult)
            ins.then_inc(ua_ready, 1)

            def conv(b):
                tap = {}
                for j in range(KS):
                    for k in range(KC):
                        if j == 0:
                            if k == 0:
                                dve.wait_ge(wide_read, WIDE_IN + 8 * (b + 1))
                            ins = dve.tensor_scalar(acc[:, b, k, :], val[:, b, k, 0:L], ksym[:, k, 0:1],
                                                    vcol[:, SYM_B + k:SYM_B + k + 1], ALU.mult, ALU.add)
                        else:
                            dve.wait_ge(dve_step, tap[k])
                            ins = dve.scalar_tensor_tensor(out=acc[:, b, k, :], in0=val[:, b, k, j:j + L],
                                                           scalar=ksym[:, k, j:j + 1], in1=acc[:, b, k, :],
                                                           op0=ALU.mult, op1=ALU.add)
                        if j < KS - 1:
                            steps[0] += 1
                            tap[k] = steps[0]
                            ins.then_inc(dve_step, 1)
                        else:
                            ins.then_inc(conv_done, 1)

            def mix_out(b):
                for q in range(2):
                    for m in range(KC):
                        i = WIDE_Y + (2 * b + q) * KC + m
                        dve.wait_ge(wide_mm, i + 1)
                        dve.scalar_tensor_tensor(out=gate[:, b, m, q * CH:(q + 1) * CH], in0=bank(2 + i % 4),
                                                 scalar=cb[:, m:m + 1], in1=gate[:, b, m, q * CH:(q + 1) * CH],
                                                 op0=ALU.add, op1=ALU.mult).then_inc(wide_read, 1)
                for q in range(2):
                    c = 2 * b + q
                    dve.wait_ge(tok_mm, TOK_MIX + c + 1)
                    dve.wait_ge(xr_ready, TC * (c + 1))
                    add_tokens(TOK_MIX + c, xr)

            def add_tokens(i, base):
                c = i % NCH
                tiles = slice(TC * c, TC * (c + 1))
                dve.tensor_tensor(x[:, tiles, :].rearrange("p i d -> p (i d)"), bank(6 + i % 2),
                                  base[:, tiles, :].rearrange("p i d -> p (i d)"), ALU.add).then_inc(tok_read, 1)

            dve.wait_ge(setup_ev, 20)
            conv(0)
            conv(1)
            mix_out(0)
            mix_out(1)

            def ffn(f, wide0, tok0, sq0):
                norm(f, 0)
                for c in range(NCH):
                    if c + 1 < NCH:
                        norm(f, c + 1)
                    for m in range(KH):
                        dve.wait_ge(wide_read, wide0 + KH * c + m + 1)
                        if c >= 2:
                            dve.wait_ge(tok_mm, tok0 + c - 1)
                        dve.tensor_tensor(r2_buf[:, c % 2, m, :], r_buf[:, c % 2, m, :], r_buf[:, c % 2, m, :],
                                          ALU.mult).then_inc(sq_ready, 1)
                    dve.wait_ge(tok_mm, tok0 + c + 1)
                    add_tokens(tok0 + c, x)

            dve.wait_ge(tok_read, TOK_MIX + NCH)
            ffn(1, WIDE_F1, TOK_F1, 0)

            dve.wait_ge(tok_read, TOK_F1 + NCH)
            norm(2, 0)
            for c in range(NCH):
                if c + 1 < NCH:
                    norm(2, c + 1)
                tiles = slice(TC * c, TC * (c + 1))
                dve.wait_ge(tok_mm, TOK_V + c + 1)
                dve.tensor_tensor(v_tok[:, tiles, :], bank(6 + c % 2).rearrange("p (i d) -> p i d", d=D),
                                  bv_bc[:, :].unsqueeze(1).broadcast_to([P, TC, D]), ALU.add).then_inc(tok_read, 1)
                for w in range(2):
                    dve.wait_ge(wide_read, WIDE_QK + 2 * c + w + 1)
                    parts, rest = qk_s[:, c % 2, w, :, :], qk_r[:, c % 2, w, :]
                    settled(dve.tensor_tensor(rest, qk_f[:, c % 2, w, :], parts[:, 0, :], ALU.subtract))
                    settled(dve.tensor_copy(parts[:, 1, :], rest))
                    dve.tensor_tensor(parts[:, 2, :], rest, parts[:, 1, :], ALU.subtract).then_inc(split_ready, 1)

            def unit_max(n, u):
                dve.wait_ge(max_mm, n * (QH * BT) + (u + 1))
                dve.tensor_reduce(mx[:, u:u + 1], pm[u % 2][:, :, :], AX.XY, ALU.max).then_inc(max_done, 1)

            def split_shift(n):
                dve.wait_ge(mx_turned, n + 1)
                if not isinstance(n, int) or n >= 1:
                    dve.wait_ge(shift_in, n * (16 * PARTS))
                src = bank(3)[0:QH * BT, 0:P]
                dve.tensor_scalar(nm_s[:, 0, :], src, -1.0, None, ALU.mult).then_inc(shift_step, 1)
                dve.tensor_scalar(nm[:, :], src, -1.0, None, ALU.mult).then_inc(shift_step, 1)
                dve.wait_ge(shift_step, n * 4 + 2)
                dve.tensor_tensor(nr[:, :], nm[:, :], nm_s[:, 0, :], ALU.subtract).then_inc(shift_step, 1)
                dve.wait_ge(shift_step, n * 4 + 3)
                dve.tensor_copy(nm_s[:, 1, :], nr[:, :]).then_inc(shift_step, 1)
                dve.wait_ge(shift_step, n * 4 + 4)
                dve.tensor_tensor(nm_s[:, 2, :], nr[:, :], nm_s[:, 1, :], ALU.subtract).then_inc(shift_split, 1)

            def norm_o(n, half):
                hn = n * 2 + half
                dve.wait_ge(o_turned, hn + 1)
                o = bank(3).rearrange("p (c j w) -> p c j w", c=TC, j=QH)
                dve.reciprocal(o_rc[:, :, :], o[:, :, :, HD]).then_inc(rc_ready, 1)
                dve.wait_ge(rc_ready, hn + 1)
                quad_out = attn[:, n, :, :] if isinstance(n, int) else attn[:, bass.ds(n, 1), :, :].rearrange(
                    "p a d w -> p (a d) w")
                dst = quad_out.rearrange("p d (j c) -> p c j d", j=QH)[:, TC * half:TC * (half + 1), :, :]
                dve.tensor_tensor(dst, o[:, :, :, 0:HD], o_rc[:, :, :].unsqueeze(3).broadcast_to([P, TC, QH, HD]),
                                  ALU.mult).then_inc(o_normed, 1)

            def quad(n, first, last):
                u = 0
                for s in range(STEPS):
                    if not last:
                        for _ in range(UNITS[s]):
                            if u == 0:
                                dve.wait_ge(mx_turned, n + 1)
                            unit_max(n + 1, u)
                            u += 1
                    if s == 3 and not first:
                        norm_o(n - 1, 1)
                    if s == 11:
                        norm_o(n, 0)
                if not last:
                    split_shift(n + 1)

            for u in range(QH * BT):
                unit_max(0, u)
            split_shift(0)
            quad(0, True, False)
            with dve.Fori(0, 2) as i:
                for q in range(NBUF):
                    quad(i * NBUF + (1 + q), False, False)
            quad(NQ - 1, False, True)
            norm_o(NQ - 1, 1)

            dve.wait_ge(o_normed, 2 * NQ)
            for c in range(NCH):
                b, q = divmod(c, 2)
                dst = h[:, TC * c:TC * (c + 1), :].rearrange("p d (g w) -> p d g w", g=GQ)
                src = attn[:, GQ * b:GQ * (b + 1), TC * q:TC * (q + 1), :].rearrange("p g d w -> p d g w")
                dve.tensor_copy(dst, src).then_inc(attn_flat, 1)

            dve.wait_ge(ao_biased, NT)
            for c in range(NCH):
                dve.wait_ge(tok_mm, TOK_AO + c + 1)
                add_tokens(TOK_AO + c, x)
            dve.wait_ge(tok_read, TOK_AO + NCH)
            ffn(3, WIDE_F2, TOK_F2, KH * NCH)

        @block.tensor
        def _(pe):
            pe.wait_ge(ident_ready, 1)
            pe.wait_ge(s_vec, 16 * 10)
            pe.transpose(bank(0)[:, 0:NVEC], vec_n[:, :], ident[0:NVEC, 0:NVEC]).then_inc(setup_mm, 1)
            pe.wait_ge(s_w_in, 16)
            for m in range(4):
                mm = pe.transpose(bank(1)[:, m * P:(m + 1) * P], in_n[:, m, :], ident[:, :])
            mm.then_inc(setup_mm, 1)
            pe.wait_ge(s_w_mix, 16 * 9)
            for i, src in enumerate((hb_n, ha_n)):
                for k in range(KC):
                    at = (2 * i + k) * P
                    mm = pe.transpose(bank(2)[:, at:at + P], src[:, k * P:(k + 1) * P], ident[:, :])
            mm.then_inc(setup_mm, 1)
            for a in range(2):
                for o in range(KC):
                    at = a * DI + o * P
                    mm = pe.transpose(bank(3)[:, at:at + P], fu_n[:, o, a * P:(a + 1) * P], ident[:, :])
            mm.then_inc(setup_mm, 1)
            for k in range(KC):
                pe.transpose(bank(4)[:, k * P:(k + 1) * P], ow_n[:, k * P:(k + 1) * P], ident[:, :])
                at = 2 * P + k * DS
                mm = pe.transpose(bank(4)[:, at:at + DS], bm_n[:, k * P:(k + 1) * P], ident[0:DS, 0:DS])
            mm.then_inc(setup_mm, 1)
            pe.wait_ge(s_w_att, 16 * 7)
            for w in range(3):
                pe.transpose(bank(5)[:, w * P:(w + 1) * P], qkv_n[:, w, :], ident[:, :])
            pe.transpose(bank(5)[:, 3 * P:4 * P], ao_n[:, :], ident[:, :]).then_inc(setup_mm, 1)
            pe.wait_ge(s_w_ffn, 16 * 6)
            for m in range(KH):
                mm = pe.transpose(bank(6)[0:RANK, m * P:(m + 1) * P], u_n[:, m, :], ident[:, :])
            mm.then_inc(setup_mm, 1)
            pe.wait_ge(tern_ready, 2)
            for m in range(KH):
                mm = pe.transpose(bank(7)[:, m * P:(m + 1) * P], tern_pr[:, m * P:(m + 1) * P], ident[:, :])
            mm.then_inc(setup_mm, 1)
            pe.wait_ge(setup_ev, 5)
            for k in range(KC):
                pe.matmul(bank(0)[:, 0:DI], hh_T[:, k, :], pw_n[:, k, :], start=(k == 0), stop=(k == KC - 1))
            for k in range(KC):
                mm = pe.matmul(bank(0)[:, DI:DI + DS], hh_T[:, KC + k, :], ob_T[:, DI + k * DS:DI + (k + 1) * DS],
                               start=(k == 0), stop=(k == KC - 1))
            mm.then_inc(setup_mm, 1)
            pe.wait_ge(setup_ev, 7)
            pe.matmul(bank(1)[0:RANK, :], fb_n[:, :], u_T[:, :], start=True, stop=True).then_inc(setup_mm, 1)
            for k in range(KC):
                mm = pe.matmul(bank(4)[0:DS, 0:1], a_n[:, k, :], vcol[:, DWA_B + k:DWA_B + k + 1],
                               start=(k == 0), stop=(k == KC - 1))
            mm.then_inc(setup_mm, 1)
            pe.wait_ge(setup_ev, 9)
            for k in range(KC):
                mm = pe.matmul(bank(2)[:, k * DI:(k + 1) * DI], xy[:, k * P:(k + 1) * P], fu_T[:, 1, :],
                               start=True, stop=True)
            mm.then_inc(setup_mm, 1)
            pe.wait_ge(setup_ev, 12)
            pe.matmul(bank(3)[:, 0:DI], y1rep[:, :], fu_T[:, 0, :], start=True, stop=True).then_inc(setup_mm, 1)
            pe.matmul(bank(6), v_n[:, :], z_s[:, :], start=True, stop=True).then_inc(setup_mm, 1)
            for m in range(KH):
                mm = pe.transpose(bank(5)[:, m * P:(m + 1) * P], tern_fc[:, m, :], ident[:, :])
            mm.then_inc(setup_mm, 1)
            for k in range(KC):
                mm = pe.matmul(bank(0)[:, k:k + 1], bm_n[:, k * P:(k + 1) * P], v1[:, :], start=True, stop=True)
            mm.then_inc(setup_mm, 1)
            for k in range(KC):
                mm = pe.matmul(bank(1)[:, 0:1], hh_T[:, k, :], vcol[:, PW_B + k:PW_B + k + 1],
                               start=(k == 0), stop=(k == KC - 1))
            mm.then_inc(setup_mm, 1)
            pe.wait_ge(setup_ev, 17)
            for k in range(KC):
                mm = pe.matmul(bank(2)[:, 0:1], hh_T[:, KC + k, :], v2[:, k:k + 1],
                               start=(k == 0), stop=(k == KC - 1))
            mm.then_inc(setup_mm, 1)
            pe.wait_ge(setup_ev, 19)
            for o in range(KC):
                pe.matmul(bank(3)[:, o:o + 1], fu_T[:, 0, o * P:(o + 1) * P], v3[:, :], start=True, stop=False)
                mm = pe.matmul(bank(3)[:, o:o + 1], fu_T[:, 1, o * P:(o + 1) * P], w1[:, :], start=False, stop=True)
            mm.then_inc(setup_mm, 1)
            pe.wait_ge(setup_ev, 20)

            def turn(i, src):
                if i >= 2:
                    pe.wait_ge(turned, i - 1)
                for t in range(TC):
                    mm = pe.transpose(bank(i % 2)[:, t * P:(t + 1) * P], src(t), ident[:, :])
                mm.then_inc(turn_mm, 1)

            def turn_h(f, i):
                c = i % NCH
                pe.wait_ge(xn_ready, f * NCH + c + 1)
                turn(i, lambda t: h[:, TC * c + t, :])

            def wide(i, pairs):
                if i >= 4:
                    pe.wait_ge(wide_read, i - 3)
                for k, (w, a) in enumerate(pairs):
                    mm = pe.matmul(bank(2 + i % 4), w, a, start=(k == 0), stop=(k == len(pairs) - 1))
                mm.then_inc(wide_mm, 1)

            def tokens(i, pairs):
                if i >= 2:
                    pe.wait_ge(tok_read, i - 1)
                for t in range(TC):
                    group = pairs(t)
                    for k, (a, w) in enumerate(group):
                        mm = pe.matmul(bank(6 + i % 2)[:, t * P:(t + 1) * P], a, w,
                                       start=(k == 0), stop=(k == len(group) - 1))
                mm.then_inc(tok_mm, 1)

            for b in range(B):
                for q in range(2):
                    turn_h(0, TURN_MIX + 2 * b + q)
                for q in range(2):
                    c = 2 * b + q
                    pe.wait_ge(turned, TURN_MIX + c + 1)
                    for m in range(4):
                        wide(WIDE_IN + 4 * c + m, [(in_T[:, m, :], hT[:, c * CH:(c + 1) * CH])])
            pe.wait_ge(ua_ready, 1)
            for b in range(B):
                pe.wait_ge(wide_read, WIDE_IN + 8 * (b + 1))
                for q in range(2):
                    if b:
                        pe.wait_ge(u_read, DC * (2 * (b - 1) + q + 1))
                    for k in range(KC):
                        mm = pe.matmul(bank(6 + q), ua[:, k, :], val[:, b, k, PAD + q * CH:PAD + (q + 1) * CH],
                                       start=(k == 0), stop=(k == KC - 1))
                    mm.then_inc(u_mm, 1)
            for b in range(B):
                pe.wait_ge(silu_done, KC * (b + 1))
                pe.wait_ge(u_read, DC * 4)
                for q in range(2):
                    for m in range(KC):
                        cols = slice(q * CH, (q + 1) * CH)
                        wide(WIDE_Y + (2 * b + q) * KC + m,
                             [(wb_T[:, k, m * P:(m + 1) * P], acc[:, b, k, cols]) for k in range(KC)]
                             + [(g_T[:, m * P:(m + 1) * P], us[:, b, PAD + q * CH:PAD + (q + 1) * CH])])
                for q in range(2):
                    pe.wait_ge(wide_read, WIDE_Y + (2 * b + q + 1) * KC)
                    tokens(TOK_MIX + 2 * b + q,
                           lambda t: [(gate[:, b, k, q * CH + t * P:q * CH + (t + 1) * P], ob_T[:, k * P:(k + 1) * P])
                                      for k in range(KC)])

            def ffn(f, turn0, wide0, tok0, sq0):
                turn_h(f, turn0)
                for c in range(NCH):
                    pe.wait_ge(turned, turn0 + c + 1)
                    for m in range(KH):
                        wide(wide0 + KH * c + m, [(fc_T[:, m * P:(m + 1) * P], hT[:, c * CH:(c + 1) * CH])])
                    if c + 1 < NCH:
                        turn_h(f, turn0 + c + 1)
                    pe.wait_ge(sq_ready, sq0 + KH * (c + 1))
                    tokens(tok0 + c, lambda t: [(r2_buf[:, c % 2, m, t * P:(t + 1) * P], wp_T[:, m, :])
                                                for m in range(KH)])

            ffn(1, TURN_F1, WIDE_F1, TOK_F1, 0)

            turn_h(2, TURN_QKV)
            for c in range(NCH):
                cols = slice(c * CH, (c + 1) * CH)
                pe.wait_ge(turned, TURN_QKV + c + 1)
                for w in range(2):
                    wide(WIDE_QK + 2 * c + w, [(att_T[:, w, :], hT[:, cols])])
                tokens(TOK_V + c, lambda t: [(hT[:, c * CH + t * P:c * CH + (t + 1) * P], att_T[:, 2, :])])
                if c + 1 < NCH:
                    turn_h(2, TURN_QKV + c + 1)

            def max_mms(r, n, u):
                j, k = divmod(u, BT)
                ops = []
                for half in range(2):
                    def op(half=half):
                        if half == 0 and not (isinstance(n, int) and n == 0 and u < 2):
                            pe.wait_ge(max_done, n * (QH * BT) + (u - 1))
                        mm = pe.matmul(pm[u % 2][:, half, :], qt[r][0:QK_ROWS, j, k * P:(k + 1) * P],
                                       kt[r][0:QK_ROWS, j, half * CH:(half + 1) * CH], start=True, stop=True)
                        if half == 1:
                            mm.then_inc(max_mm, 1)
                    ops.append(op)
                return ops

            def turn_max(n):
                pe.wait_ge(max_done, n * (QH * BT) + QH * BT)
                if not (isinstance(n, int) and n == 0):
                    pe.wait_ge(o_normed, n * 2 - 1)
                pe.transpose(bank(3)[0:QH * BT, 0:P], mx[:, :], ident[:, :]).then_inc(mx_turned, 1)

            def pv(r, n, s):
                pe.wait_ge(exp_done, n * (STEPS * QH) + QH * (s + 1))
                if s == 0:
                    pe.wait_ge(v4_ready, n + 1)
                hn = n * 2 + s // BT
                if s % BT == 0 and not (isinstance(n, int) and hn == 0):
                    pe.wait_ge(o_copied, hn)
                for j in range(QH):
                    mm = pe.matmul(bank(2)[VW * j:VW * (j + 1), :], v4[r][:, s % BT, j, :], pexp[s % NPB][:, j, :],
                                   start=(s % BT == 0), stop=(s % BT == BT - 1), tile_position=(0, VW * j))
                mm.then_inc(pv_mm, 1)

            def turn_o(hn, n):
                pe.wait_ge(o_copied, hn + 1)
                pe.wait_ge(shift_split, n + 1)
                if not (isinstance(hn, int) and hn == 0):
                    pe.wait_ge(o_normed, hn)
                for t in range(TC):
                    mm = pe.transpose(bank(3)[:, t * P:(t + 1) * P], o_sb[:, t * P:(t + 1) * P], ident[:, :])
                mm.then_inc(o_turned, 1)

            def loads(n0, trip):
                return (trip + n0 // NBUF + 1) * (16 * 2 * PARTS * PARTS) + 16

            def quad(n0, trip, first, last):
                n = trip * NBUF + n0
                r, nxt, prev = n0 % NBUF, (n0 + 1) % NBUF, (n0 - 1) % NBUF
                if not last:
                    pe.wait_ge(qk_in[nxt], loads(n0 + 1, trip))
                pe.wait_ge(shift_in, n * (16 * PARTS) + 16 * PARTS)
                u = 0
                for s in range(STEPS):
                    half, tile = divmod(s, BT)
                    ahead = []
                    if not last:
                        for _ in range(UNITS[s]):
                            ahead += max_mms(nxt, n + 1, u)
                            u += 1
                    share = [ahead[i::QH] for i in range(QH)]
                    share = [ahead[len(ahead) * i // QH:len(ahead) * (i + 1) // QH] for i in range(QH)]
                    for j in range(QH):
                        if not (first and s == 0 and j < 2):
                            pe.wait_ge(exp_done, n * (STEPS * QH) + (s * QH + j - 1))
                        pe.matmul(bank(j % 2), kt[r][:, j, tile * P:(tile + 1) * P],
                                  qt[r][:, j, half * CH:(half + 1) * CH], start=True, stop=True).then_inc(exp_mm, 1)
                        for op in share[j]:
                            op()
                        if j == 1:
                            if s:
                                pv(r, n, s - 1)
                            elif not first:
                                pv(prev, n - 1, STEPS - 1)
                    if s == 2 and not first:
                        turn_o(n * 2 - 1, n)
                    if s == BT + 2:
                        turn_o(n * 2, n)
                    if s == STEPS - 2 and not last:
                        turn_max(n + 1)

            pe.wait_ge(turned, TURN_QKV + NCH)
            pe.wait_ge(wide_read, WIDE_QK + 2 * NCH)
            pe.wait_ge(tok_read, TOK_V + NCH)
            pe.wait_ge(qk_in[0], loads(0, 0))
            for u in range(QH * BT):
                for op in max_mms(0, 0, u):
                    op()
            turn_max(0)
            quad(0, 0, True, False)
            with pe.Fori(0, 2) as i:
                for q in range(NBUF):
                    quad(1 + q, i, False, False)
            quad(NQ - 1, 0, False, True)
            pv((NQ - 1) % NBUF, NQ - 1, STEPS - 1)
            turn_o(2 * NQ - 1, NQ - 1)

            for c in range(NCH):
                pe.wait_ge(attn_flat, c + 1)
                tokens(TOK_AO + c, lambda t: [(h[:, TC * c + t, :], att_T[:, 3, :])])
            ffn(3, TURN_F2, WIDE_F2, TOK_F2, KH * NCH)


_INS = ['L0_attn_a_x', 'L0_attn_a_norm_w', 'L0_attn_a_in_w', 'L0_attn_a_in_b', 'L0_attn_a_dwa_k', 'L0_attn_a_dwa_b',
        'L0_attn_a_A', 'L0_attn_a_Bm', 'L0_attn_a_sym_k', 'L0_attn_a_sym_b', 'L0_attn_a_pw_w', 'L0_attn_a_pw_b',
        'L0_attn_a_ha_w', 'L0_attn_a_ha_b', 'L0_attn_a_hb_w', 'L0_attn_a_hb_b', 'L0_attn_a_fuse_w',
        'L0_attn_a_fuse_b', 'L0_attn_a_out_w', 'L0_attn_a_out_b', 'L0_attn_b_qkv_w', 'L0_attn_b_qkv_b',
        'L0_attn_b_out_w', 'L0_attn_b_out_b', 'L0_ffn_fast_b', 'L0_ffn_w_fc', 'L0_ffn_w_proj', 'L0_ffn_u',
        'L0_ffn_v', 'L0_ffn_gate']


def kernel(**inputs):
    import numpy as np
    import concourse.bacc as bacc
    from concourse.bass_utils import run_bass_kernel_spmd

    nc = bacc.Bacc("TRN2", target_bir_lowering=False, num_devices=1)
    arrays, args = {}, []
    for name in _INS:
        a = np.ascontiguousarray(inputs[name])
        if a.ndim == 0:
            a = a.reshape(1, 1)
        arrays[f"in_{name}"] = a
        args.append(nc.dram_tensor(f"in_{name}", a.shape, mybir.dt.from_np(a.dtype), kind="ExternalInput").ap())
    out = nc.dram_tensor("out", (B, L, D), F32, kind="ExternalOutput").ap()
    build(nc, args, out)
    r = run_bass_kernel_spmd(nc, [arrays], core_ids=[0])
    return r.results[0]["out"]
```

```python
from contextlib import ExitStack

import concourse.bass as bass
from concourse import mybir

F32 = mybir.dt.float32
BF16 = mybir.dt.bfloat16
ALU = mybir.AluOpType
ACT = mybir.ActivationFunctionType
AX = mybir.AxisListType

P = 128
B, L, D = 2, 1024, 128
NT = B * L // P
BT = L // P
CH = 512
NCH = B * L // CH
TC = CH // P
DI = 2 * D
KC = DI // P
DS = 16
DC = 4
KS = 9
PAD = 4
LP = L + 2 * PAD
HID = 512
KH = HID // P
RANK = 16
H, HD = 16, 8
QH = 4
GQ = H // QH
NQ = B * GQ
PARTS = 3
QK_ROWS = PARTS * PARTS * HD
SHIFT_ROW = QK_ROWS
ROWS = 96
NBUF = 3
VW = 32
EPS_LN, EPS_RMS = 1e-5, 1e-6
SCALE = float(HD) ** -0.5
STEPS = 2 * BT
NR = 3
NPB = 4
ORDER = "memememev"
EBANKS = (0, 1, 3)
MBANKS = (4, 5, 6, 7)
COPY_O_AFTER = 1
MS = ORDER.count("m")
HT = QH * TC
NU = 2 * HT
LEAD = 12
MQ = 2 * (NU + 2)
M0 = NU + LEAD
TURN_MAX_AT = 2
TURN_O_AT = 2
O_NUMBER = (TURN_O_AT * MS, (BT + TURN_O_AT) * MS + 2)
O_NUMBER_LAST = (TURN_O_AT * MS, NU - LEAD + 2)
O_LAST = M0 + (NQ - 1) * MQ + NU - LEAD + 3
STORED = 16 * 2 * PARTS
SHIFT = 16 * PARTS
assert MQ % len(MBANKS) == 0 and M0 % len(MBANKS) == 0 and MS * BT == NU and LEAD % MS == 0
assert STEPS % NPB == 0 and QH * STEPS % len(EBANKS) == 1

IN_B, SYM_B, DWA_B, PW_B, HA_B, HB_B, FU_B, NORM, BQ, BK = 0, 4, 6, 8, 10, 11, 12, 14, 15, 16
NVEC = 17
TURN_MIX, TURN_F1, TURN_QKV, TURN_F2 = (NCH * i for i in range(4))
TOK_MIX, TOK_F1, TOK_V, TOK_AO, TOK_F2 = (NCH * i for i in range(5))
VAR0 = (0, 1, 1 + NCH, 1 + 2 * NCH)
WIDE_IN = 0
WIDE_Y = WIDE_IN + 4 * NCH
WIDE_F1 = WIDE_Y + KC * NCH
WIDE_QK = WIDE_F1 + KH * NCH
WIDE_F2 = WIDE_QK + 2 * NCH


def build(nc, ins, out):
    x_d, norm_w, in_w, in_b, dwa_k, dwa_b, A_d, Bm_d, sym_k, sym_b, pw_w, pw_b, ha_w, ha_b, hb_w, hb_b, \
        fuse_w, fuse_b, out_w, out_b, qkv_w, qkv_b, ao_w, ao_b, fb_d, wfc_d, wproj_d, u_d, v_d, gate_d = ins
    ctx = ExitStack()
    with ctx:
        def sb(name, shape, dt=F32):
            return ctx.enter_context(nc.sbuf_tensor(name, shape, dt))

        def sem(name):
            return ctx.enter_context(nc.semaphore(name))

        in_n = sb("in_n", [P, 4, D])
        hb_n = sb("hb_n", [P, DI])
        ha_n = sb("ha_n", [P, DI])
        fu_n = sb("fu_n", [P, KC, DI])
        ow_n = sb("ow_n", [P, DI])
        bm_n = sb("bm_n", [DS, DI])
        pw_n = sb("pw_n", [P, KC, DI])
        a_n = sb("a_n", [P, KC, DS])
        kdwa = sb("kdwa", [P, KC, DC])
        ksym = sb("ksym", [P, KC, KS])
        qkv_n = sb("qkv_n", [P, 3, D])
        ao_n = sb("ao_n", [P, D])
        wfc_n = sb("wfc_n", [P, KH, D])
        wpr_n = sb("wpr_n", [P, HID])
        u_n = sb("u_n", [P, KH, RANK])
        v_n = sb("v_n", [RANK, D])
        fb_n = sb("fb_n", [RANK, RANK])
        gate_n = sb("gate_n", [RANK, 1])
        vec_n = sb("vec_n", [NVEC, P])
        ob_bc = sb("ob_bc", [P, D])
        bv_bc = sb("bv_bc", [P, D])
        aob_bc = sb("aob_bc", [P, D])
        ident = sb("ident", [P, P])
        vcol = sb("vcol", [P, NVEC])
        in_T = sb("in_T", [P, 4, D])
        hh_T = sb("hh_T", [P, 4, P])
        fu_T = sb("fu_T", [P, 2, DI])
        ob_T = sb("ob_T", [P, 2 * P + 2 * DS])
        att_T = sb("att_T", [P, 4, P])
        u_T = sb("u_T", [RANK, HID])
        wp_T = sb("wp_T", [P, KH, D])
        fc_T = sb("fc_T", [P, HID])
        z_s = sb("z_s", [RANK, HID])
        xy = sb("xy", [P, DI + DS])
        y1rep = sb("y1rep", [P, P])
        wb_T = sb("wb_T", [P, KC, DI])
        g_T = sb("g_T", [P, DI])
        ua = sb("ua", [P, KC, P])
        v1 = sb("v1", [DS, 1])
        v2 = sb("v2", [P, KC])
        v3 = sb("v3", [P, 1])
        w1 = sb("w1", [P, 1])
        cb = sb("cb", [P, KC])
        tern_fc = sb("tern_fc", [P, KH, D])
        tern_lo = sb("tern_lo", [P, HID])
        tern_pr = sb("tern_pr", [P, HID])
        tern_pl = sb("tern_pl", [P, HID])
        sc = sb("sc", [P, 4, KH + 1])
        x = sb("x", [P, NT, D])
        xr = sb("xr", [P, NT, D])
        h = sb("h", [P, NT, D])
        hT = sb("hT", [P, B * L])
        gate = sb("gate", [P, B, KC, L])
        val = sb("val", [P, B, KC, LP])
        acc = sb("acc", [P, B, KC, L])
        us = sb("us", [P, B, LP])
        st = sb("st", [P, 4, NT, 6])
        mv = sb("mv", [P, 4, NT, 2])
        small = sb("small", [P, 4, 8, NT])
        xr_c = sb("xr_c", [P, NT])
        r2_buf = acc[:, :, :, :].rearrange("p b k l -> p b (k l)").rearrange("p b (m c) -> p b m c", m=KH)
        gate_f = gate[:, :, :, :].rearrange("p b k l -> p (b k l)")
        val_h = val[:, :, :, :].rearrange("p b k l -> p (b k l)").bitcast(BF16)
        v_tok = us[:, :, :].rearrange("p b l -> p (b l)")[:, 0:NT * H * HD].rearrange("p (i d) -> p i d", i=NT)
        qt = [sb(f"qt{r}", [ROWS, 2, QH, CH], BF16)[:, :, :, :] for r in range(NBUF - 1)]
        kt = [sb(f"kt{r}", [ROWS, 2, QH, CH], BF16)[:, :, :, :] for r in range(NBUF - 1)]
        for i, buf in enumerate((qt, kt)):
            buf.append(val_h[0:ROWS, i * QH * L:(i + 1) * QH * L].rearrange("p (h j t) -> p h j t", h=2, j=QH))
        v4 = [sb(f"v4_{r}", [P, BT, QH, VW]) for r in range(NBUF)]
        ones_rows = xr[:, :, :].rearrange("p i d -> p (i d)").bitcast(BF16)[0:PARTS, :]
        pexp = [gate[:, 0, :, :], gate[:, 1, :, :], acc[:, 0, :, :], acc[:, 1, :, :]]
        pexp = [b.rearrange("p k l -> p (k l)").rearrange("p (j c) -> p j c", j=QH) for b in pexp]
        o_sb = sb("o_sb", [P, CH])
        o_rc = sb("o_rc", [P, TC, QH])
        attn = sb("attn", [P, NQ, HD, QH * BT])
        relu = gate_f[:, 0:NR * CH].rearrange("p (i c) -> p i c", i=NR)
        qk_r = gate_f[:, NR * CH:(NR + 2) * CH].rearrange("p (w c) -> p w c", w=2)
        attn_f = attn[:, :, :, :].rearrange("p n d w -> p (n d w)")
        qk_s = [attn_f[:, 0:PARTS * CH], gate_f[:, (NR + 2) * CH:(NR + 2 + PARTS) * CH]]
        qk_s = [b.bitcast(BF16).rearrange("p (w i c) -> p w i c", w=2, i=PARTS) for b in qk_s]
        hT_f = hT[:, :]
        u_rows = h[:, :, :].rearrange("p i d -> p (i d)").rearrange("p (b l) -> p b l", b=B)
        tap_bufs = [attn_f[:, 0:L], attn_f[:, L:2 * L], hT_f[:, 0:L], hT_f[:, L:2 * L]]
        mx = sb("mx", [P, HT, 2])
        mx_row = sb("mx_row", [P, HT])
        nm = sb("nm", [HT, P])
        nr = sb("nr", [HT, P])
        nm_s = sb("nm_s", [HT, PARTS, P], BF16)

        ps = [ctx.enter_context(nc.psum_tensor(f"ps{i}", [P, CH], F32)) for i in range(8)]

        def bank(i):
            return ps[i][:, :]

        def tap_buf(j):
            return tap_bufs[(j - 1) % 4]

        q_scr = nc.dram_tensor("q_scr", [PARTS, GQ * HD, NCH, QH, CH], BF16, kind="Internal").ap()
        k_scr = nc.dram_tensor("k_scr", [PARTS, GQ * HD, NCH, QH, CH], BF16, kind="Internal").ap()

        s_x = [sem(f"s_x{c}") for c in range(NCH)]
        s_w_in, s_w_taps, s_w_mix, s_vec = sem("s_w_in"), sem("s_w_taps"), sem("s_w_mix"), sem("s_vec")
        s_w_tern, s_w_ffn, s_w_att = sem("s_w_tern"), sem("s_w_ffn"), sem("s_w_att")
        ident_zero, ident_ready, pads_ready = sem("ident_zero"), sem("ident_ready"), sem("pads_ready")
        consts_ready, v4_zero, v4_ones = sem("consts_ready"), sem("v4_zero"), sem("v4_ones")
        dve_step, rc_ready, shift_step, xr_step = sem("dve_step"), sem("rc_ready"), sem("shift_step"), sem("xr_step")
        setup_mm, setup_ev, tern_ready, ua_ready = sem("setup_mm"), sem("setup_ev"), sem("tern_ready"), sem("ua_ready")
        us_in = [sem(f"us_in{b}") for b in range(B)]
        var_ready, std_ready, xn_ready = sem("var_ready"), sem("std_ready"), sem("xn_ready")
        xr_coef, xr_ready = sem("xr_coef"), sem("xr_ready")
        turn_mm, turned = sem("turn_mm"), sem("turned")
        wide_mm, wide_read = sem("wide_mm"), sem("wide_read")
        tok_mm, tok_read = sem("tok_mm"), sem("tok_read")
        u_mm, u_read, conv_done, silu_done = sem("u_mm"), sem("u_read"), sem("conv_done"), sem("silu_done")
        tap_ready, tap_added = sem("tap_ready"), sem("tap_added")
        sq_ready = sem("sq_ready")
        part0_ready, part1_ready, split_ready = sem("part0_ready"), sem("part1_ready"), sem("split_ready")
        scr_done = [sem(f"scr_done{i}") for i in range(2)]
        qk_in = [sem(f"qk_in{r}") for r in range(NBUF)]
        shift_in, v4_ready = sem("shift_in"), sem("v4_ready")
        exp_mm, exp_done, pv_mm = sem("exp_mm"), sem("exp_done"), sem("pv_mm")
        o_copied = sem("o_copied")
        m_mm, m_read, rows_ready, max_step = sem("m_mm"), sem("m_read"), sem("rows_ready"), sem("max_step")
        shift_split = sem("shift_split")
        attn_flat = sem("attn_flat")
        ao_biased, stored = sem("ao_biased"), sem("stored")

        x_src = x_d.rearrange("b (i p) d -> p (b i) d", p=P)
        out_dst = out.rearrange("b (i p) d -> p (b i) d", p=P)
        block = ctx.enter_context(nc.Block())

        @block.sync
        def _(sp):
            for c in range(NCH):
                sp.dma_start(x[:, TC * c:TC * c + TC, :], x_src[:, TC * c:TC * c + TC, :]).then_inc(s_x[c], 16)
            for dst, src in ((ksym[:, :, :], sym_k.rearrange("(k p) o t -> p k (o t)", p=P)),
                             (a_n[:, :, :], A_d.rearrange("(k p) s -> p k s", p=P)),
                             (kdwa[:, :, :], dwa_k.rearrange("(k p) o t -> p k (o t)", p=P))):
                sp.dma_start(dst, src).then_inc(s_w_taps, 16)
            sp.dma_start(wfc_n[:, :, :], wfc_d.rearrange("(m p) d -> p m d", p=P)).then_inc(s_w_tern, 16)
            sp.dma_start(wpr_n[:, :], wproj_d).then_inc(s_w_tern, 16)
            for dst, src in ((pw_n[:, :, :], pw_w.rearrange("(k p) c -> p k c", p=P)), (hb_n[:, :], hb_w),
                             (ha_n[:, :], ha_w), (fu_n[:, :, :], fuse_w.rearrange("(k p) c -> p k c", p=P)),
                             (ow_n[:, :], out_w), (bm_n[:, :], Bm_d)):
                sp.dma_start(dst, src).then_inc(s_w_mix, 16)
            sp.dma_start(u_n[:, :, :], u_d.rearrange("(m p) r -> p m r", p=P)).then_inc(s_w_ffn, 16)
            sp.dma_start(v_n[:, :], v_d).then_inc(s_w_ffn, 16)
            sp.dma_start(fb_n[:, :], fb_d).then_inc(s_w_ffn, 16)
            sp.dma_start(gate_n[:, :], gate_d.broadcast_to([RANK, 1])).then_inc(s_w_ffn, 16)
            sp.wait_ge(pads_ready, 5)
            for b in range(B):
                sp.wait_ge(u_read, 2 * (b + 1))
                for t in range(DC):
                    at = PAD + 1 - t
                    sp.dma_start(us[32 * t:32 * t + 32, b, at:at + L],
                                 u_rows[32 * t:32 * t + 32, b, :]).then_inc(us_in[b], 16)

            def store_parts(c):
                for w, scr in ((0, q_scr), (1, k_scr)):
                    sp.wait_ge(split_ready, 2 * c + w + 1)
                    for i in range(PARTS):
                        sp.dma_start(scr[i, :, c, :, :].rearrange("x j t -> j x t"),
                                     qk_s[c % 2][:, w, i, :]).then_inc(scr_done[c % 2], 16)

            def load_quad(n):
                b, g = divmod(n, GQ)
                for i in range(PARTS):
                    for rep in range(PARTS):
                        at_q = (i * PARTS + rep) * HD
                        at_k = (rep * PARTS + i) * HD
                        for buf, scr, at in ((qt, q_scr, at_q), (kt, k_scr, at_k)):
                            src = scr[i, g * HD:(g + 1) * HD, 2 * b:2 * b + 2, :, :]
                            sp.dma_start(buf[n % NBUF][at:at + HD, :, :, :], src).then_inc(qk_in[n % NBUF], 16)

            def load_shift(hn):
                sp.wait_ge(shift_split, hn + 1)
                n, half = divmod(hn, 2)
                for i in range(PARTS):
                    dst = qt[n % NBUF][SHIFT_ROW + i:SHIFT_ROW + i + 1, half, :, :]
                    sp.dma_start(dst.rearrange("a j (k p) -> a (j k) p", p=P),
                                 nm_s[:, i, :]).then_inc(shift_in, 16)

            sp.wait_ge(consts_ready, 2 * NBUF + 1)
            for r in range(NBUF):
                sp.dma_start(kt[r][SHIFT_ROW:SHIFT_ROW + PARTS, :, :, :].rearrange("i h j t -> i (h j t)"),
                             ones_rows).then_inc(qk_in[r], 16)
            store_parts(0)
            store_parts(1)
            for i in range(2):
                sp.wait_ge(scr_done[i], STORED)
            load_quad(0)
            store_parts(2)
            store_parts(3)
            for n in range(1, NBUF):
                load_quad(n)
            load_shift(0)
            for n in range(NQ):
                if 1 <= n and n + 2 < NQ:
                    sp.wait_ge(exp_mm, STEPS * QH * n)
                    if n + 2 == GQ:
                        for i in range(2):
                            sp.wait_ge(scr_done[i], 2 * STORED)
                    load_quad(n + 2)
                load_shift(2 * n + 1)
                if n + 1 < NQ:
                    load_shift(2 * n + 2)
            for c in range(NCH):
                sp.wait_ge(tok_read, TOK_F2 + c + 1)
                sp.dma_start(out_dst[:, TC * c:TC * c + TC, :], x[:, TC * c:TC * c + TC, :]).then_inc(stored, 16)
            sp.wait_ge(stored, 16 * NCH)

        @block.gpsimd
        def _(pool):
            pool.memset(ident[:, :], 0.0).then_inc(ident_zero, 1)
            pool.wait_ge(ident_zero, 1)
            pool.affine_select(out=ident[:, :], in_=ident[:, :], compare_op=ALU.not_equal, fill=1.0, base=0,
                               pattern=[[-1, P]], channel_multiplier=1).then_inc(ident_ready, 1)
            for w in range(3):
                src = qkv_w.rearrange("(h w d) e -> w h d e", w=3, d=HD)[w]
                pool.dma_start(qkv_n[:, w, :], src).then_inc(s_w_att, 16)
            pool.dma_start(ao_n[:, :], ao_w).then_inc(s_w_att, 16)
            pool.dma_start(aob_bc[:, :], ao_b.rearrange("(a d) -> a d", a=1).broadcast_to([P, D])).then_inc(s_w_att, 16)
            pool.dma_start(ob_bc[:, :], out_b.rearrange("(a d) -> a d", a=1).broadcast_to([P, D])).then_inc(s_w_att, 16)
            src = qkv_b.rearrange("(a h w d) -> w a h d", a=1, w=3, d=HD)[2].broadcast_to([P, H, HD])
            pool.dma_start(bv_bc[:, :].rearrange("p (h d) -> p h d", d=HD), src).then_inc(s_w_att, 16)
            edges = val[:, :, :, :].rearrange("p b k l -> p (b k) l")
            pool.memset(edges[:, :, 0:PAD], 0.0).then_inc(pads_ready, 1)
            pool.memset(edges[:, :, PAD + L:LP], 0.0).then_inc(pads_ready, 1)
            pool.memset(us[:, :, :], 0.0).then_inc(pads_ready, 1)
            pool.memset(ua[:, :, :], 0.0).then_inc(pads_ready, 1)
            pool.memset(y1rep[:, :], 0.0).then_inc(pads_ready, 1)
            pool.wait_ge(xr_coef, 2)
            for i in range(NT):
                pool.tensor_scalar(xr[:, i, :], x[:, i, :], xr_c[:, i:i + 1], small[:, 0, 6, i:i + 1],
                                   ALU.mult, ALU.add).then_inc(xr_step, 1)
            pool.wait_ge(s_w_att, 16 * 7)
            for i in range(NT):
                pool.wait_ge(xr_step, i + 1)
                pool.tensor_tensor(xr[:, i, :], xr[:, i, :], ob_bc[:, :], ALU.add).then_inc(xr_ready, 1)
            for j in range(1, KS):
                pool.wait_ge(tap_ready, j + 1)
                if j > 1:
                    pool.wait_ge(tap_added, j - 1)
                dst = acc[:, B - 1, KC - 1, :]
                pool.tensor_tensor(dst, dst, tap_buf(j), ALU.add).then_inc(tap_added, 1)
            pool.wait_ge(tok_read, TOK_MIX + NCH)
            for r in range(NBUF):
                pool.memset(v4[r][:, :, :, :], 0.0).then_inc(v4_zero, 1)
            pool.wait_ge(v4_zero, NBUF)
            for r in range(NBUF):
                pool.memset(qt[r][64:ROWS, :, :, :].bitcast(F32), 0.0).then_inc(consts_ready, 1)
                pool.memset(kt[r][64:ROWS, :, :, :].bitcast(F32), 0.0).then_inc(consts_ready, 1)
            pool.wait_ge(consts_ready, 2 * NBUF)
            pool.memset(ones_rows, 1.0).then_inc(consts_ready, 1)
            pool.wait_ge(consts_ready, 2 * NBUF + 1)
            for r in range(NBUF):
                pool.memset(v4[r][:, :, :, HD:HD + 1], 1.0).then_inc(v4_ones, 1)
            pool.wait_ge(v4_ones, NBUF)
            for c in range(NCH):
                tiles = slice(TC * c, TC * (c + 1))
                pool.wait_ge(xn_ready, NCH * 2 + c + 1)
                pool.tensor_tensor(x[:, tiles, :], x[:, tiles, :],
                                   aob_bc[:, :].unsqueeze(1).broadcast_to([P, TC, D]), ALU.add).then_inc(ao_biased, 1)
                for w in range(2):
                    pool.wait_ge(part1_ready, 2 * c + w + 1)
                    parts = qk_s[c % 2][:, w, :, :]
                    pool.tensor_tensor(parts[:, 2, :], qk_r[:, w, :], parts[:, 1, :],
                                       ALU.subtract).then_inc(split_ready, 1)
            pool.wait_ge(tok_read, TOK_V + NCH)
            for n in range(NQ):
                b, g = divmod(n, GQ)
                if n >= NBUF:
                    pool.wait_ge(pv_mm, STEPS * (n - NBUF + 1))
                src = v_tok[:, b * BT:(b + 1) * BT, :].rearrange("p c (j g d) -> p g c j d", g=GQ, d=HD)
                pool.tensor_copy(v4[n % NBUF][:, :, :, 0:HD], src[:, g, :, :, :]).then_inc(v4_ready, 1)

        @block.scalar
        def _(act):
            act.dma_start(in_n[:, :, :], in_w.rearrange("(m p) d -> p m d", p=P)).then_inc(s_w_in, 16)
            for at, v in ((IN_B, in_b), (SYM_B, sym_b), (DWA_B, dwa_b), (PW_B, pw_b), (HA_B, ha_b), (HB_B, hb_b),
                          (FU_B, fuse_b), (NORM, norm_w)):
                rows = v.rearrange("(m p) -> m p", p=P)
                act.dma_start(vec_n[at:at + rows.shape[0], :], rows).then_inc(s_vec, 16)
            for at, w in ((BQ, 0), (BK, 1)):
                src = qkv_b.rearrange("(a h w d) -> w a h d", a=1, w=3, d=HD)[w]
                act.dma_start(vec_n[at:at + 1, :].rearrange("a (h d) -> a h d", d=HD), src).then_inc(s_vec, 16)

            def root(f, lo, hi, k=0):
                act.activation(small[:, f, k + 1, lo:hi], small[:, f, k, lo:hi], ACT.Sqrt).then_inc(std_ready, 1)

            def turn_copy(i):
                c = i % NCH
                act.wait_ge(turn_mm, i + 1)
                act.activation(hT[:, c * CH:(c + 1) * CH], bank(i % 2), ACT.Copy).then_inc(turned, 1)

            def ev(k, dst, src, func=ACT.Copy, **kw):
                act.wait_ge(setup_mm, k)
                act.activation(dst, src, func, **kw).then_inc(setup_ev, 1)

            def flat(w):
                return w[:, :, :].rearrange("p m o -> p (m o)")

            act.wait_ge(var_ready, 1)
            act.activation(small[:, 0, 2:4, :], small[:, 0, 0:2, :], ACT.Sqrt).then_inc(std_ready, 1)
            ev(1, vcol[:, :], bank(0)[:, 0:NVEC])
            act.wait_ge(setup_ev, 1)
            ev(2, flat(in_T), bank(1), ACT.Identity, scale=vcol[:, NORM:NORM + 1])
            for b in range(B):
                for q in range(2):
                    turn_copy(TURN_MIX + 2 * b + q)
                for q in range(2):
                    for m in range(4):
                        i = WIDE_IN + (2 * b + q) * 4 + m
                        act.wait_ge(wide_mm, i + 1)
                        src, bias = bank(2 + i % 4), vcol[:, IN_B + m:IN_B + m + 1]
                        if m < KC:
                            act.activation(gate[:, b, m, q * CH:(q + 1) * CH], src, ACT.Sigmoid,
                                           bias=bias).then_inc(wide_read, 1)
                        else:
                            act.activation(val[:, b, m - KC, PAD + q * CH:PAD + (q + 1) * CH], src, ACT.Identity,
                                           bias=bias).then_inc(wide_read, 1)

            def causal_out(b):
                for q in range(2):
                    act.wait_ge(u_mm, 2 * b + q + 1)
                    act.activation(u_rows[:, b, q * CH:(q + 1) * CH], bank(6 + q), ACT.Copy).then_inc(u_read, 1)

            def tap(j):
                k, src = KC - 1, val[:, B - 1, KC - 1, j:j + L]
                if j == 0:
                    act.activation(acc[:, B - 1, k, :], src, ACT.Identity, scale=ksym[:, k, 0:1],
                                   bias=vcol[:, SYM_B + k:SYM_B + k + 1]).then_inc(tap_ready, 1)
                else:
                    if j > 4:
                        act.wait_ge(tap_added, j - 4)
                    act.activation(tap_buf(j), src, ACT.Identity, scale=ksym[:, k, j:j + 1]).then_inc(tap_ready, 1)

            def silu(b):
                for k in range(KC):
                    if (b, k) == (B - 1, KC - 1):
                        act.wait_ge(tap_added, KS - 1)
                    else:
                        act.wait_ge(conv_done, 2 * (KC * b + k + 1))
                    act.activation(acc[:, b, k, :], acc[:, b, k, :], ACT.Silu).then_inc(silu_done, 1)

            act.wait_ge(pads_ready, 5)
            act.wait_ge(s_w_taps, 16 * 3)
            act.wait_ge(wide_read, WIDE_IN + 8 * B)
            causal_out(0)
            ev(3, flat(hh_T), bank(2))
            ev(4, flat(fu_T), bank(3))
            ev(5, ob_T[:, :], bank(4)[:, 0:2 * P + 2 * DS])
            ev(6, flat(att_T), bank(5))
            tap(0)
            tap(1)
            causal_out(1)
            tap(2)
            ev(7, u_T[:, :], bank(6)[0:RANK, :])
            ev(8, flat(wp_T), bank(7))
            tap(3)
            ev(9, xy[:, :], bank(0)[:, 0:DI + DS])
            ev(10, z_s[:, :], bank(1)[0:RANK, :], ACT.Identity, scale=gate_n[:, 0:1])
            ev(11, v1[:, :], bank(4)[0:DS, 0:1])
            act.wait_ge(setup_ev, 9)
            for t in range(DC):
                ins = act.activation(y1rep[:, 32 * t:32 * t + DS], xy[:, DI:DI + DS], ACT.Copy)
            ins.then_inc(setup_ev, 1)
            tap(4)
            ev(12, flat(wb_T), bank(2))
            ev(13, g_T[:, :], bank(3)[:, 0:DI])
            silu(0)
            tap(5)
            tap(6)
            ev(14, fc_T[:, :], bank(6))
            ev(15, v2[:, :], bank(0)[:, 0:KC])
            tap(7)
            ev(16, w1[:, :], bank(1)[:, 0:1], ACT.Identity, bias=vcol[:, HB_B:HB_B + 1])
            ev(17, v3[:, :], bank(7)[:, 0:1], ACT.Identity, bias=vcol[:, HA_B:HA_B + 1])
            tap(8)
            for o in range(KC):
                act.wait_ge(setup_mm, 18)
                act.activation(cb[:, o:o + 1], bank(0)[:, o:o + 1], ACT.Identity,
                               bias=vcol[:, FU_B + o:FU_B + o + 1]).then_inc(setup_ev, 1)
            silu(1)

            def stds(f, c):
                act.wait_ge(var_ready, VAR0[f] + c + 1)
                root(f, TC * c, TC * (c + 1))

            def first_parts(c):
                for w in range(2):
                    i = WIDE_QK + 2 * c + w
                    act.wait_ge(wide_mm, i + 1)
                    if c >= 2:
                        act.wait_ge(scr_done[c % 2], STORED * (c // 2))
                    act.activation(qk_s[c % 2][:, w, 0, :], bank(2 + i % 4), ACT.Identity,
                                   bias=vcol[:, BQ + w:BQ + w + 1]).then_inc(part0_ready, 1)

            def second_parts(c):
                for w in range(2):
                    act.wait_ge(wide_read, WIDE_QK + 2 * c + w + 1)
                    act.activation(qk_s[c % 2][:, w, 1, :], qk_r[:, w, :], ACT.Copy).then_inc(part1_ready, 1)

            def rectify(c, wide0, sq0):
                for m in range(KH):
                    i, n = wide0 + KH * c + m, KH * c + m
                    act.wait_ge(wide_mm, i + 1)
                    if sq0 + n >= NR:
                        act.wait_ge(sq_ready, sq0 + n - NR + 1)
                    act.activation(relu[:, n % NR, :], bank(2 + i % 4), ACT.Relu).then_inc(wide_read, 1)

            stds(1, 0)
            turn_copy(TURN_F1)
            stds(1, 1)
            turn_copy(TURN_F1 + 1)
            stds(1, 2)
            rectify(0, WIDE_F1, 0)
            turn_copy(TURN_F1 + 2)
            stds(1, 3)
            rectify(1, WIDE_F1, 0)
            turn_copy(TURN_F1 + 3)
            stds(2, 0)
            rectify(2, WIDE_F1, 0)
            stds(2, 1)
            rectify(3, WIDE_F1, 0)
            for c in range(NCH):
                turn_copy(TURN_QKV + c)
                if c:
                    second_parts(c - 1)
                if c + 2 < NCH:
                    stds(2, c + 2)
                first_parts(c)
            second_parts(NCH - 1)

            def copy_o(hn, turned_at):
                act.wait_ge(pv_mm, hn * BT + BT)
                if turned_at is not None:
                    act.wait_ge(m_mm, turned_at)
                act.activation(o_sb[:, :], bank(2), ACT.Copy).then_inc(o_copied, 1)

            def quad(n0, trip, first, last):
                n = trip * NBUF + n0
                for s in range(STEPS):
                    if not (first and s < NPB):
                        act.wait_ge(pv_mm, n * STEPS + (s - NPB + 1))
                    for j in range(QH):
                        act.wait_ge(exp_mm, n * (STEPS * QH) + (s * QH + j + 1))
                        act.activation(pexp[s % NPB][:, j, :], bank(EBANKS[(n0 + s * QH + j) % 3]), ACT.Exp,
                                       scale=SCALE).then_inc(exp_done, 1)
                        if s == 1 and j == COPY_O_AFTER and not first:
                            copy_o(n * 2 - 1, n * MQ + (M0 - MQ + O_NUMBER[1] + 1))
                        if s == BT + 1 and j == COPY_O_AFTER:
                            copy_o(n * 2, None if first else n * MQ + (M0 + O_NUMBER[0] + 1))

            quad(0, 0, True, False)
            with act.Fori(0, 2) as i:
                for q in range(NBUF):
                    quad(1 + q, i, False, False)
            quad(NQ - 1, 0, False, True)
            copy_o(2 * NQ - 1, M0 + (NQ - 1) * MQ + O_NUMBER_LAST[1] + 1)
            for c in range(NCH):
                stds(3, c)
            turn_copy(TURN_F2)
            turn_copy(TURN_F2 + 1)
            for c in range(NCH):
                rectify(c, WIDE_F2, KH * NCH)
                if c + 2 < NCH:
                    turn_copy(TURN_F2 + c + 2)

        @block.vector
        def _(dve):
            steps = [0]

            def settled(ins):
                steps[0] += 1
                ins.then_inc(dve_step, 1)
                dve.wait_ge(dve_step, steps[0])

            def stats(f, lo, hi):
                for i in range(lo, hi):
                    ins = dve.bn_stats(st[:, f, i, :], x[:, i, :])
                    ins.then_inc(dve_step, 1)
                steps[0] += hi - lo
                dve.wait_ge(dve_step, steps[0])
                for i in range(lo, hi):
                    ins = dve.bn_aggr(mv[:, f, i, :], st[:, f, i, :])
                    ins.then_inc(dve_step, 1)
                steps[0] += hi - lo
                dve.wait_ge(dve_step, steps[0])
                dve.tensor_scalar(small[:, f, 0, lo:hi], mv[:, f, lo:hi, 1], EPS_LN, None,
                                  ALU.add).then_inc(var_ready, 1)

            def chunk_stats(f, c):
                stats(f, TC * c, TC * (c + 1))

            def norm(f, c):
                lo, hi = TC * c, TC * (c + 1)
                dve.wait_ge(std_ready, VAR0[f] + c + 1)
                settled(dve.reciprocal(small[:, f, 2, lo:hi], small[:, f, 1, lo:hi]))
                settled(dve.scalar_tensor_tensor(out=small[:, f, 3, lo:hi], in0=mv[:, f, lo:hi, 0], scalar=-1.0,
                                                 in1=small[:, f, 2, lo:hi], op0=ALU.mult, op1=ALU.mult))
                for i in range(lo, hi):
                    ins = dve.tensor_scalar(h[:, i, :], x[:, i, :], small[:, f, 2, i:i + 1],
                                            small[:, f, 3, i:i + 1], ALU.mult, ALU.add)
                    if i == hi - 1:
                        ins.then_inc(xn_ready, 1)

            for c in range(NCH):
                dve.wait_ge(s_x[c], 16)
                for i in range(TC * c, TC * (c + 1)):
                    dve.bn_stats(st[:, 0, i, :], x[:, i, :]).then_inc(dve_step, 1)
            steps[0] += NT
            for i in range(NT):
                dve.wait_ge(dve_step, steps[0] - NT + i + 1)
                dve.bn_aggr(mv[:, 0, i, :], st[:, 0, i, :]).then_inc(dve_step, 1)
            steps[0] += NT
            dve.wait_ge(dve_step, steps[0])
            settled(dve.tensor_scalar(small[:, 0, 0, :], mv[:, 0, :, 1], EPS_LN, None, ALU.add))
            dve.scalar_tensor_tensor(out=small[:, 0, 1, :], in0=small[:, 0, 0, :], scalar=EPS_RMS,
                                     in1=mv[:, 0, :, 1], op0=ALU.mult, op1=ALU.add).then_inc(var_ready, 1)
            dve.wait_ge(std_ready, 1)
            settled(dve.reciprocal(small[:, 0, 4:6, :], small[:, 0, 2:4, :]))
            settled(dve.scalar_tensor_tensor(out=small[:, 0, 7, :], in0=mv[:, 0, :, 0], scalar=-1.0,
                                             in1=small[:, 0, 5, :], op0=ALU.mult, op1=ALU.mult))
            for c in range(NCH):
                for i in range(TC * c, TC * (c + 1)):
                    ins = dve.tensor_scalar(h[:, i, :], x[:, i, :], small[:, 0, 5, i:i + 1],
                                            small[:, 0, 7, i:i + 1], ALU.mult, ALU.add)
                ins.then_inc(xn_ready, 1)
                if c == 1:
                    dve.tensor_scalar(xr_c[:, :], small[:, 0, 4, :], 1.0, None, ALU.add).then_inc(xr_coef, 1)
                    dve.scalar_tensor_tensor(out=small[:, 0, 6, :], in0=mv[:, 0, :, 0], scalar=-1.0,
                                             in1=small[:, 0, 4, :], op0=ALU.mult, op1=ALU.mult).then_inc(xr_coef, 1)

            dve.wait_ge(s_w_taps, 16 * 3)
            dve.wait_ge(pads_ready, 5)
            for k in range(KC):
                for t in range(DC):
                    ins = dve.tensor_scalar(ua[:, k, 32 * t:32 * t + DS], a_n[:, k, :], kdwa[:, k, t:t + 1], None,
                                            ALU.mult)
            ins.then_inc(ua_ready, 1)

            dve.wait_ge(s_w_tern, 16 * 2)
            wfc = wfc_n[:, :, :]
            dve.tensor_reduce(sc[:, 0, 0:KH], wfc, AX.X, ALU.add,
                              apply_absolute_value=True).then_inc(dve_step, 1)
            steps[0] += 1
            settled(dve.tensor_reduce(sc[:, 0, KH:KH + 1], wpr_n[:, :], AX.X, ALU.add, apply_absolute_value=True))
            dve.tensor_scalar(sc[:, 1, 0:KH], sc[:, 0, 0:KH], 1.0 / D, 1e-5, ALU.mult, ALU.max).then_inc(dve_step, 1)
            steps[0] += 1
            settled(dve.tensor_scalar(sc[:, 1, KH:KH + 1], sc[:, 0, KH:KH + 1], 1.0 / HID, 1e-5, ALU.mult, ALU.max))
            dve.tensor_scalar(sc[:, 2, :], sc[:, 1, :], 0.5, None, ALU.mult).then_inc(dve_step, 1)
            dve.tensor_scalar(sc[:, 3, :], sc[:, 1, :], -0.5, None, ALU.mult).then_inc(dve_step, 1)
            steps[0] += 2
            dve.wait_ge(dve_step, steps[0])
            pairs = [(wfc_n[:, m, :], tern_fc[:, m, :], tern_lo[:, m * D:(m + 1) * D], m) for m in range(KH)]
            pairs.append((wpr_n[:, :], tern_pr[:, :], tern_pl[:, :], KH))
            for w, hi, lo, m in pairs:
                dve.tensor_scalar(hi, w, sc[:, 2, m:m + 1], sc[:, 1, m:m + 1], ALU.is_gt,
                                  ALU.mult).then_inc(dve_step, 1)
                dve.tensor_scalar(lo, w, sc[:, 3, m:m + 1], sc[:, 1, m:m + 1], ALU.is_lt,
                                  ALU.mult).then_inc(dve_step, 1)
            steps[0] += 2 * len(pairs)
            dve.wait_ge(dve_step, steps[0])
            dve.tensor_tensor(tern_fc[:, :, :].rearrange("p m d -> p (m d)"),
                              tern_fc[:, :, :].rearrange("p m d -> p (m d)"), tern_lo[:, :],
                              ALU.subtract).then_inc(tern_ready, 1)
            dve.tensor_tensor(tern_pr[:, :], tern_pr[:, :], tern_pl[:, :], ALU.subtract).then_inc(tern_ready, 1)

            def conv(b, streams):
                tap = {}
                for j in range(KS):
                    for k, lo, w in streams:
                        src, dst = val[:, b, k, j + lo:j + lo + w], acc[:, b, k, lo:lo + w]
                        if j == 0:
                            ins = dve.tensor_scalar(dst, src, ksym[:, k, 0:1], vcol[:, SYM_B + k:SYM_B + k + 1],
                                                    ALU.mult, ALU.add)
                        else:
                            dve.wait_ge(dve_step, tap[k, lo])
                            ins = dve.scalar_tensor_tensor(out=dst, in0=src, scalar=ksym[:, k, j:j + 1], in1=dst,
                                                           op0=ALU.mult, op1=ALU.add)
                        if j < KS - 1:
                            steps[0] += 1
                            tap[k, lo] = steps[0]
                            ins.then_inc(dve_step, 1)
                        else:
                            ins.then_inc(conv_done, 2 * w // L)

            def gated(b):
                for q in range(2):
                    for m in range(KC):
                        i = WIDE_Y + (2 * b + q) * KC + m
                        dve.wait_ge(wide_mm, i + 1)
                        dve.scalar_tensor_tensor(out=gate[:, b, m, q * CH:(q + 1) * CH], in0=bank(2 + i % 4),
                                                 scalar=cb[:, m:m + 1], in1=gate[:, b, m, q * CH:(q + 1) * CH],
                                                 op0=ALU.add, op1=ALU.mult).then_inc(wide_read, 1)

            def mixed(c):
                dve.wait_ge(tok_mm, TOK_MIX + c + 1)
                dve.wait_ge(xr_ready, TC * (c + 1))
                add_tokens(TOK_MIX + c, xr)

            def add_tokens(i, base):
                c = i % NCH
                tiles = slice(TC * c, TC * (c + 1))
                dve.tensor_tensor(x[:, tiles, :].rearrange("p i d -> p (i d)"), bank(6 + i % 2),
                                  base[:, tiles, :].rearrange("p i d -> p (i d)"), ALU.add).then_inc(tok_read, 1)

            dve.wait_ge(setup_ev, 1)
            dve.wait_ge(wide_read, WIDE_IN + 8)
            conv(0, [(k, 0, L) for k in range(KC)])
            dve.wait_ge(wide_read, WIDE_IN + 8 * B)
            conv(1, [(0, 0, CH), (0, CH, CH)])
            dve.wait_ge(setup_ev, 20)
            gated(0)
            mixed(0)
            mixed(1)

            def squares(c, wide0, tok0):
                for m in range(KH):
                    i = wide0 + KH * c + m
                    dve.wait_ge(wide_read, i + 1)
                    if c >= 2 and m == 0:
                        dve.wait_ge(tok_mm, tok0 + c - 1)
                    r = relu[:, (KH * c + m) % NR, :]
                    dve.tensor_tensor(r2_buf[:, c % 2, m, :], r, r, ALU.mult).then_inc(sq_ready, 1)

            def take_tokens(i):
                dve.wait_ge(tok_mm, i + 1)
                add_tokens(i, x)

            def qkv_out(c):
                tiles = slice(TC * c, TC * (c + 1))
                for w in range(2):
                    i = WIDE_QK + 2 * c + w
                    dve.wait_ge(part0_ready, 2 * c + w + 1)
                    if c:
                        dve.wait_ge(split_ready, 2 * (c - 1) + w + 1)
                    dve.scalar_tensor_tensor(out=qk_r[:, w, :], in0=bank(2 + i % 4),
                                             scalar=vcol[:, BQ + w:BQ + w + 1], in1=qk_s[c % 2][:, w, 0, :],
                                             op0=ALU.add, op1=ALU.subtract).then_inc(wide_read, 1)
                dve.wait_ge(tok_mm, TOK_V + c + 1)
                dve.tensor_tensor(v_tok[:, tiles, :], bank(6 + c % 2).rearrange("p (i d) -> p i d", d=D),
                                  bv_bc[:, :].unsqueeze(1).broadcast_to([P, TC, D]), ALU.add).then_inc(tok_read, 1)

            def mix_stats(c):
                dve.wait_ge(tok_read, TOK_MIX + c + 1)
                chunk_stats(1, c)

            mix_stats(0)
            mix_stats(1)
            gated(1)
            norm(1, 0)
            norm(1, 1)
            mixed(2)
            mix_stats(2)
            norm(1, 2)
            mixed(3)
            mix_stats(3)
            squares(0, WIDE_F1, TOK_F1)
            norm(1, 3)
            for c in range(NCH):
                if c + 1 < NCH:
                    squares(c + 1, WIDE_F1, TOK_F1)
                take_tokens(TOK_F1 + c)
                dve.wait_ge(tok_read, TOK_F1 + c + 1)
                chunk_stats(2, c)
                if c == NCH - 1:
                    qkv_out(0)
                norm(2, c)
            for c in range(1, NCH):
                qkv_out(c)

            def unit_max(u, i, k):
                dve.wait_ge(m_mm, i + 1)
                dve.tensor_reduce(mx[:, u // 2, u % 2:u % 2 + 1], bank(MBANKS[k % 4]), AX.X,
                                  ALU.max).then_inc(m_read, 1)

            def row_max(hn, i):
                dve.wait_ge(m_read, i)
                dve.tensor_tensor(mx_row[:, :], mx[:, :, 0], mx[:, :, 1], ALU.max).then_inc(rows_ready, 1)
                dve.wait_ge(rows_ready, hn + 1)

            def split_shift(hn, i, k):
                dve.wait_ge(m_mm, i + 1)
                if not isinstance(hn, int) or hn >= 1:
                    dve.wait_ge(shift_in, hn * SHIFT)
                dve.tensor_scalar(nm[:, :], bank(MBANKS[k % 4])[0:HT, 0:P], -1.0, None,
                                  ALU.mult).then_inc(m_read, 1)
                dve.wait_ge(m_read, i + 1)
                dve.tensor_copy(nm_s[:, 0, :], nm[:, :]).then_inc(shift_step, 1)
                dve.wait_ge(shift_step, hn * 3 + 1)
                dve.tensor_tensor(nr[:, :], nm[:, :], nm_s[:, 0, :], ALU.subtract).then_inc(shift_step, 1)
                dve.wait_ge(shift_step, hn * 3 + 2)
                dve.tensor_copy(nm_s[:, 1, :], nr[:, :]).then_inc(shift_step, 1)
                dve.wait_ge(shift_step, hn * 3 + 3)
                dve.tensor_tensor(nm_s[:, 2, :], nr[:, :], nm_s[:, 1, :], ALU.subtract).then_inc(shift_split, 1)

            def norm_o(n, half, i, k):
                dve.wait_ge(m_read, i)
                dve.wait_ge(m_mm, i + 1)
                o = bank(MBANKS[k % 4]).rearrange("p (c j w) -> p c j w", c=TC, j=QH)
                dve.reciprocal(o_rc[:, :, :], o[:, :, :, HD]).then_inc(rc_ready, 1)
                dve.wait_ge(rc_ready, n * 2 + (half + 1))
                quad_out = attn[:, n, :, :] if isinstance(n, int) else attn[:, bass.ds(n, 1), :, :].rearrange(
                    "p a d w -> p (a d) w")
                dst = quad_out.rearrange("p d (j c) -> p c j d", j=QH)[:, TC * half:TC * (half + 1), :, :]
                dve.tensor_tensor(dst, o[:, :, :, 0:HD], o_rc[:, :, :].unsqueeze(3).broadcast_to([P, TC, QH, HD]),
                                  ALU.mult).then_inc(m_read, 1)

            def maxima(hn, u, i, k, exist):
                if u == 0:
                    row_max(hn - 1, i)
                if u == TURN_MAX_AT:
                    split_shift(hn - 1, i, k)
                    i, k = i + 1, k + 1
                if exist:
                    unit_max(u, i, k)
                    k = k + 1
                return k

            def quad(n, first, last):
                base = n * MQ + M0
                k = 1 if first else 0
                for s in range(STEPS):
                    half = s // BT
                    if s % BT == TURN_O_AT and not (first and half == 0):
                        norm_o(n if half else n - 1, 1 - half, base + k, k)
                        k += 1
                    for m in range(MS):
                        h, u = divmod(NU + LEAD + s * MS + m, NU)
                        if not (last and h > 2):
                            k = maxima(n * 2 + h, u, base + k, k, not (last and h == 2))

            for u in range(NU):
                unit_max(u, u, u)
            k = NU
            for u in range(LEAD):
                k = maxima(1, u, k, k, True)
            quad(0, True, False)
            with dve.Fori(0, 2) as i:
                for q in range(NBUF):
                    quad(i * NBUF + (1 + q), False, False)
            quad(NQ - 1, False, True)
            norm_o(NQ - 1, 1, O_LAST, O_LAST)

            dve.wait_ge(m_read, O_LAST + 1)
            for c in range(NCH):
                b, q = divmod(c, 2)
                dst = h[:, TC * c:TC * (c + 1), :].rearrange("p d (j g w) -> p g d j w", j=QH, g=GQ)
                for g in range(GQ):
                    src = attn[:, GQ * b + g, TC * q:TC * (q + 1), :].rearrange("p d (j w) -> p d j w", j=QH)
                    dve.tensor_copy(dst[:, g, :, :, :], src).then_inc(attn_flat, 1)

            for c in range(NCH):
                dve.wait_ge(ao_biased, c + 1)
                take_tokens(TOK_AO + c)
                dve.wait_ge(tok_read, TOK_AO + c + 1)
                chunk_stats(3, c)
                norm(3, c)
            squares(0, WIDE_F2, TOK_F2)
            for c in range(NCH):
                if c + 1 < NCH:
                    squares(c + 1, WIDE_F2, TOK_F2)
                take_tokens(TOK_F2 + c)

        @block.tensor
        def _(pe):
            pe.wait_ge(ident_ready, 1)
            pe.wait_ge(s_vec, 16 * 10)
            pe.transpose(bank(0)[:, 0:NVEC], vec_n[:, :], ident[0:NVEC, 0:NVEC]).then_inc(setup_mm, 1)
            pe.wait_ge(s_w_in, 16)
            for m in range(4):
                mm = pe.transpose(bank(1)[:, m * P:(m + 1) * P], in_n[:, m, :], ident[:, :])
            mm.then_inc(setup_mm, 1)
            def turn(i, src):
                if i >= 2:
                    pe.wait_ge(turned, i - 1)
                for t in range(TC):
                    mm = pe.transpose(bank(i % 2)[:, t * P:(t + 1) * P], src(t), ident[:, :])
                mm.then_inc(turn_mm, 1)

            def turn_h(f, i):
                c = i % NCH
                pe.wait_ge(xn_ready, f * NCH + c + 1)
                turn(i, lambda t: h[:, TC * c + t, :])

            def wide(i, pairs):
                if i >= 4:
                    pe.wait_ge(wide_read, i - 3)
                for k, (w, a) in enumerate(pairs):
                    mm = pe.matmul(bank(2 + i % 4), w, a, start=(k == 0), stop=(k == len(pairs) - 1))
                mm.then_inc(wide_mm, 1)

            def tokens(i, pairs):
                if i >= 2:
                    pe.wait_ge(tok_read, i - 1)
                for t in range(TC):
                    group = pairs(t)
                    for k, (a, w) in enumerate(group):
                        mm = pe.matmul(bank(6 + i % 2)[:, t * P:(t + 1) * P], a, w,
                                       start=(k == 0), stop=(k == len(group) - 1))
                mm.then_inc(tok_mm, 1)

            def causal(b):
                for q in range(2):
                    if b:
                        pe.wait_ge(u_read, 2 * (b - 1) + q + 1)
                    for k in range(KC):
                        mm = pe.matmul(bank(6 + q), ua[:, k, :], val[:, b, k, PAD + q * CH:PAD + (q + 1) * CH],
                                       start=(k == 0), stop=(k == KC - 1))
                    mm.then_inc(u_mm, 1)

            def y_mm(b, q, blocks=range(KC)):
                pe.wait_ge(us_in[b], 16 * DC)
                for m in blocks:
                    cols = slice(q * CH, (q + 1) * CH)
                    wide(WIDE_Y + (2 * b + q) * KC + m,
                         [(wb_T[:, k, m * P:(m + 1) * P], acc[:, b, k, cols]) for k in range(KC)]
                         + [(g_T[:, m * P:(m + 1) * P], us[:, b, PAD + q * CH:PAD + (q + 1) * CH])])

            pe.wait_ge(setup_ev, 2)
            for b in range(B):
                for q in range(2):
                    turn_h(0, TURN_MIX + 2 * b + q)
                for q in range(2):
                    c = 2 * b + q
                    pe.wait_ge(turned, TURN_MIX + c + 1)
                    for m in range(4):
                        wide(WIDE_IN + 4 * c + m, [(in_T[:, m, :], hT[:, c * CH:(c + 1) * CH])])
            pe.wait_ge(ua_ready, 1)
            pe.wait_ge(wide_read, WIDE_IN + 8 * B)
            causal(0)

            pe.wait_ge(s_w_mix, 16 * 6)
            for i, src in enumerate((hb_n, ha_n)):
                for k in range(KC):
                    at = (2 * i + k) * P
                    mm = pe.transpose(bank(2)[:, at:at + P], src[:, k * P:(k + 1) * P], ident[:, :])
            mm.then_inc(setup_mm, 1)
            for a in range(2):
                for o in range(KC):
                    at = a * DI + o * P
                    mm = pe.transpose(bank(3)[:, at:at + P], fu_n[:, o, a * P:(a + 1) * P], ident[:, :])
            mm.then_inc(setup_mm, 1)
            for k in range(KC):
                pe.transpose(bank(4)[:, k * P:(k + 1) * P], ow_n[:, k * P:(k + 1) * P], ident[:, :])
                at = 2 * P + k * DS
                mm = pe.transpose(bank(4)[:, at:at + DS], bm_n[:, k * P:(k + 1) * P], ident[0:DS, 0:DS])
            mm.then_inc(setup_mm, 1)
            pe.wait_ge(s_w_att, 16 * 7)
            for w in range(3):
                pe.transpose(bank(5)[:, w * P:(w + 1) * P], qkv_n[:, w, :], ident[:, :])
            pe.transpose(bank(5)[:, 3 * P:4 * P], ao_n[:, :], ident[:, :]).then_inc(setup_mm, 1)
            causal(1)
            pe.wait_ge(u_read, 2 * B)
            pe.wait_ge(s_w_ffn, 16 * 4)
            for m in range(KH):
                mm = pe.transpose(bank(6)[0:RANK, m * P:(m + 1) * P], u_n[:, m, :], ident[:, :])
            mm.then_inc(setup_mm, 1)
            pe.wait_ge(tern_ready, 2)
            for m in range(KH):
                mm = pe.transpose(bank(7)[:, m * P:(m + 1) * P], tern_pr[:, m * P:(m + 1) * P], ident[:, :])
            mm.then_inc(setup_mm, 1)
            pe.wait_ge(setup_ev, 5)
            for k in range(KC):
                pe.matmul(bank(0)[:, 0:DI], hh_T[:, k, :], pw_n[:, k, :], start=(k == 0), stop=(k == KC - 1))
            for k in range(KC):
                mm = pe.matmul(bank(0)[:, DI:DI + DS], hh_T[:, KC + k, :], ob_T[:, DI + k * DS:DI + (k + 1) * DS],
                               start=(k == 0), stop=(k == KC - 1))
            mm.then_inc(setup_mm, 1)
            pe.wait_ge(setup_ev, 7)
            pe.matmul(bank(1)[0:RANK, :], fb_n[:, :], u_T[:, :], start=True, stop=True).then_inc(setup_mm, 1)
            for k in range(KC):
                mm = pe.matmul(bank(4)[0:DS, 0:1], a_n[:, k, :], vcol[:, DWA_B + k:DWA_B + k + 1],
                               start=(k == 0), stop=(k == KC - 1))
            mm.then_inc(setup_mm, 1)
            pe.wait_ge(setup_ev, 9)
            for k in range(KC):
                mm = pe.matmul(bank(2)[:, k * DI:(k + 1) * DI], xy[:, k * P:(k + 1) * P], fu_T[:, 1, :],
                               start=True, stop=True)
            mm.then_inc(setup_mm, 1)
            pe.wait_ge(setup_ev, 12)
            pe.matmul(bank(3)[:, 0:DI], y1rep[:, :], fu_T[:, 0, :], start=True, stop=True).then_inc(setup_mm, 1)
            pe.wait_ge(setup_ev, 14)
            pe.wait_ge(silu_done, KC)
            y_mm(0, 0, [0])
            pe.matmul(bank(6), v_n[:, :], z_s[:, :], start=True, stop=False)
            for m in range(KH):
                mm = pe.matmul(bank(6)[:, m * P:(m + 1) * P], tern_fc[:, m, :], ident[:, :], start=False,
                               stop=(m == KH - 1))
            mm.then_inc(setup_mm, 1)
            y_mm(0, 0, [1])
            for k in range(KC):
                mm = pe.matmul(bank(0)[:, k:k + 1], bm_n[:, k * P:(k + 1) * P], v1[:, :], start=True, stop=True)
            mm.then_inc(setup_mm, 1)
            for k in range(KC):
                mm = pe.matmul(bank(1)[:, 0:1], hh_T[:, k, :], vcol[:, PW_B + k:PW_B + k + 1],
                               start=(k == 0), stop=(k == KC - 1))
            mm.then_inc(setup_mm, 1)
            y_mm(0, 1, [0])
            pe.wait_ge(setup_ev, 16)
            for k in range(KC):
                mm = pe.matmul(bank(7)[:, 0:1], hh_T[:, KC + k, :], v2[:, k:k + 1],
                               start=(k == 0), stop=(k == KC - 1))
            mm.then_inc(setup_mm, 1)
            y_mm(0, 1, [1])
            pe.wait_ge(setup_ev, 18)
            for o in range(KC):
                pe.matmul(bank(0)[:, o:o + 1], fu_T[:, 0, o * P:(o + 1) * P], v3[:, :], start=True, stop=False)
                mm = pe.matmul(bank(0)[:, o:o + 1], fu_T[:, 1, o * P:(o + 1) * P], w1[:, :], start=False, stop=True)
            mm.then_inc(setup_mm, 1)
            pe.wait_ge(setup_ev, 20)

            for b in range(B):
                if b:
                    pe.wait_ge(silu_done, KC * (b + 1))
                    for q in range(2):
                        y_mm(b, q)
                for q in range(2):
                    pe.wait_ge(wide_read, WIDE_Y + (2 * b + q + 1) * KC)
                    tokens(TOK_MIX + 2 * b + q,
                           lambda t: [(gate[:, b, k, q * CH + t * P:q * CH + (t + 1) * P], ob_T[:, k * P:(k + 1) * P])
                                      for k in range(KC)])

            def fc(c, turn0, wide0):
                pe.wait_ge(turned, turn0 + c + 1)
                for m in range(KH):
                    wide(wide0 + KH * c + m, [(fc_T[:, m * P:(m + 1) * P], hT[:, c * CH:(c + 1) * CH])])

            def proj(c, sq0, tok0):
                pe.wait_ge(sq_ready, sq0 + KH * (c + 1))
                tokens(tok0 + c, lambda t: [(r2_buf[:, c % 2, m, t * P:(t + 1) * P], wp_T[:, m, :])
                                            for m in range(KH)])

            def qk(c):
                pe.wait_ge(turned, TURN_QKV + c + 1)
                for w in range(2):
                    wide(WIDE_QK + 2 * c + w, [(att_T[:, w, :], hT[:, c * CH:(c + 1) * CH])])

            def v(c):
                tokens(TOK_V + c, lambda t: [(hT[:, c * CH + t * P:c * CH + (t + 1) * P], att_T[:, 2, :])])

            turn_h(1, TURN_F1)
            turn_h(1, TURN_F1 + 1)
            fc(0, TURN_F1, WIDE_F1)
            turn_h(1, TURN_F1 + 2)
            fc(1, TURN_F1, WIDE_F1)
            proj(0, 0, TOK_F1)
            turn_h(1, TURN_F1 + 3)
            fc(2, TURN_F1, WIDE_F1)
            proj(1, 0, TOK_F1)
            fc(3, TURN_F1, WIDE_F1)
            turn_h(2, TURN_QKV)
            proj(2, 0, TOK_F1)
            qk(0)
            turn_h(2, TURN_QKV + 1)
            proj(3, 0, TOK_F1)
            v(0)
            for c in range(1, NCH):
                qk(c)
                if c + 1 < NCH:
                    turn_h(2, TURN_QKV + c + 1)
                v(c)

            def m_free(i):
                if not isinstance(i, int) or i >= len(MBANKS):
                    pe.wait_ge(m_read, i - (len(MBANKS) - 1))

            def max_mm(r, half, u, i, k):
                (j, c), keys = divmod(u // 2, TC), u % 2
                m_free(i)
                pe.matmul(bank(MBANKS[k % 4]), qt[r][0:QK_ROWS, half, j, c * P:(c + 1) * P],
                          kt[r][0:QK_ROWS, keys, j, :], start=True, stop=True).then_inc(m_mm, 1)

            def turn_max(hn, i, k):
                pe.wait_ge(rows_ready, hn + 1)
                m_free(i)
                pe.transpose(bank(MBANKS[k % 4])[0:HT, 0:P], mx_row[:, :], ident[:, :]).then_inc(m_mm, 1)

            def turn_o(hn, i, k):
                pe.wait_ge(o_copied, hn + 1)
                m_free(i)
                for t in range(TC):
                    mm = pe.transpose(bank(MBANKS[k % 4])[:, t * P:(t + 1) * P], o_sb[:, t * P:(t + 1) * P],
                                      ident[:, :])
                mm.then_inc(m_mm, 1)

            def pv(r, n, s):
                pe.wait_ge(exp_done, n * (STEPS * QH) + QH * (s + 1))
                if s == 0:
                    pe.wait_ge(v4_ready, n + 1)
                hn = n * 2 + s // BT
                if s % BT == 0 and not (isinstance(n, int) and hn == 0):
                    pe.wait_ge(o_copied, hn)
                for j in range(QH):
                    mm = pe.matmul(bank(2)[VW * j:VW * (j + 1), :], v4[r][:, s % BT, j, :], pexp[s % NPB][:, j, :],
                                   start=(s % BT == 0), stop=(s % BT == BT - 1), tile_position=(0, VW * j))
                mm.then_inc(pv_mm, 1)

            def loads(n0, trip):
                return (trip + n0 // NBUF + 1) * (16 * 2 * PARTS * PARTS) + 16

            def quad(n0, trip, first, last):
                n = trip * NBUF + n0
                r, nxt, prev = n0 % NBUF, (n0 + 1) % NBUF, (n0 - 1) % NBUF
                base = n * MQ + M0
                k = 1 if first else 0
                for s in range(STEPS):
                    half, tile = divmod(s, BT)
                    j = 0
                    if tile == 0:
                        pe.wait_ge(shift_in, (n * 2 + half) * SHIFT + SHIFT)
                    if tile == TURN_O_AT and not (first and half == 0):
                        turn_o(n * 2 + half - 1, base + k, k)
                        k += 1
                    for at, kind in enumerate(ORDER):
                        if kind == "e":
                            e = s * QH + j
                            if not first or e >= len(EBANKS):
                                pe.wait_ge(exp_done, n * (STEPS * QH) + (e - len(EBANKS) + 1))
                            keys = kt[r][:, tile // TC, j, tile % TC * P:(tile % TC + 1) * P]
                            pe.matmul(bank(EBANKS[(n0 + e) % 3]), keys,
                                      qt[r][:, half, j, :], start=True, stop=True).then_inc(exp_mm, 1)
                            j += 1
                        elif kind == "v" and s:
                            pv(r, n, s - 1)
                        elif kind == "v" and not first:
                            pv(prev, n - 1, STEPS - 1)
                        elif kind == "m":
                            h, u = divmod(NU + LEAD + s * MS + ORDER[:at].count("m"), NU)
                            if u == TURN_MAX_AT and not (last and h > 2):
                                turn_max(n * 2 + h - 1, base + k, k)
                                k += 1
                            if last and h >= 2:
                                continue
                            if h == 2 and u == 0:
                                pe.wait_ge(qk_in[nxt], loads(n0 + 1, trip))
                            max_mm(nxt if h >= 2 else r, h % 2, u, base + k, k)
                            k += 1

            pe.wait_ge(turned, TURN_QKV + NCH)
            pe.wait_ge(wide_read, WIDE_QK + 2 * NCH)
            pe.wait_ge(tok_read, TOK_V + NCH)
            pe.wait_ge(qk_in[0], loads(0, 0))
            k = 0
            for u in range(NU + LEAD):
                if u == NU + TURN_MAX_AT:
                    turn_max(0, k, k)
                    k += 1
                max_mm(0, u // NU, u % NU, k, k)
                k += 1
            quad(0, 0, True, False)
            with pe.Fori(0, 2) as i:
                for q in range(NBUF):
                    quad(1 + q, i, False, False)
            quad(NQ - 1, 0, False, True)
            pv((NQ - 1) % NBUF, NQ - 1, STEPS - 1)
            turn_o(2 * NQ - 1, O_LAST, O_LAST)

            for c in range(NCH):
                pe.wait_ge(attn_flat, GQ * (c + 1))
                tokens(TOK_AO + c, lambda t: [(h[:, TC * c + t, :], att_T[:, 3, :])])
            turn_h(3, TURN_F2)
            turn_h(3, TURN_F2 + 1)
            fc(0, TURN_F2, WIDE_F2)
            for c in range(NCH):
                if c + 2 < NCH:
                    turn_h(3, TURN_F2 + c + 2)
                if c + 1 < NCH:
                    fc(c + 1, TURN_F2, WIDE_F2)
                proj(c, KH * NCH, TOK_F2)


_INS = ['L0_attn_a_x', 'L0_attn_a_norm_w', 'L0_attn_a_in_w', 'L0_attn_a_in_b', 'L0_attn_a_dwa_k', 'L0_attn_a_dwa_b',
        'L0_attn_a_A', 'L0_attn_a_Bm', 'L0_attn_a_sym_k', 'L0_attn_a_sym_b', 'L0_attn_a_pw_w', 'L0_attn_a_pw_b',
        'L0_attn_a_ha_w', 'L0_attn_a_ha_b', 'L0_attn_a_hb_w', 'L0_attn_a_hb_b', 'L0_attn_a_fuse_w',
        'L0_attn_a_fuse_b', 'L0_attn_a_out_w', 'L0_attn_a_out_b', 'L0_attn_b_qkv_w', 'L0_attn_b_qkv_b',
        'L0_attn_b_out_w', 'L0_attn_b_out_b', 'L0_ffn_fast_b', 'L0_ffn_w_fc', 'L0_ffn_w_proj', 'L0_ffn_u',
        'L0_ffn_v', 'L0_ffn_gate']


def kernel(**inputs):
    import numpy as np
    import concourse.bacc as bacc
    from concourse.bass_utils import run_bass_kernel_spmd

    nc = bacc.Bacc("TRN2", target_bir_lowering=False, num_devices=1)
    arrays, args = {}, []
    for name in _INS:
        a = np.ascontiguousarray(inputs[name])
        if a.ndim == 0:
            a = a.reshape(1, 1)
        arrays[f"in_{name}"] = a
        args.append(nc.dram_tensor(f"in_{name}", a.shape, mybir.dt.from_np(a.dtype), kind="ExternalInput").ap())
    out = nc.dram_tensor("out", (B, L, D), F32, kind="ExternalOutput").ap()
    build(nc, args, out)
    r = run_bass_kernel_spmd(nc, [arrays], core_ids=[0])
    return r.results[0]["out"]
```

```python
from contextlib import ExitStack

import concourse.bass as bass
from concourse import mybir

F32 = mybir.dt.float32
BF16 = mybir.dt.bfloat16
ALU = mybir.AluOpType
ACT = mybir.ActivationFunctionType
AX = mybir.AxisListType

P = 128
B, L, D = 2, 1024, 128
NT = B * L // P
BT = L // P
CH = 512
NCH = B * L // CH
TC = CH // P
DI = 2 * D
KC = DI // P
DS = 16
DC = 4
KS = 9
PAD = 4
LP = L + 2 * PAD
HID = 512
KH = HID // P
RANK = 16
H, HD = 16, 8
QH = 4
GQ = H // QH
NQ = B * GQ
PARTS = 3
QK_ROWS = PARTS * PARTS * HD
SHIFT_ROW = QK_ROWS
ROWS = 96
NBUF = 3
VW = 32
EPS_LN, EPS_RMS = 1e-5, 1e-6
SCALE = float(HD) ** -0.5
STEPS = 2 * BT
NR = 3
NPB = 4
ORDER = "emememevm"
EBANKS = (0, 1, 3)
E_MORE = 24
MBANKS = (4, 5, 6, 7)
COPY_O_AFTER = 0
MS = ORDER.count("m")
HT = QH * TC
NU = 2 * HT
LEAD = 16
MQ = 2 * (NU + 2)
M0 = NU + LEAD
ROW_MAX_AT = 1
TURN_MAX_AT = 3
TURN_O_AT = 2
O_NUMBER = (TURN_O_AT * MS, (BT + TURN_O_AT) * MS + 2)
O_NUMBER_LAST = (TURN_O_AT * MS, NU - LEAD + 2)
O_LAST = M0 + (NQ - 1) * MQ + NU - LEAD + 3
STORED = 16 * 2 * PARTS
NEGATED = [NU + TURN_MAX_AT]
for n in range(NQ):
    for half in range(2):
        units = (half + 1) * NU - LEAD + TURN_MAX_AT * (n < NQ - 1)
        outputs = sum(units > at * MS for at in (TURN_O_AT, BT + TURN_O_AT))
        NEGATED.append(M0 + n * MQ + units + outputs + half)
PROJECT_AT = (11, 12)
SHIFT = 16 * PARTS
assert MQ % len(MBANKS) == 0 and M0 % len(MBANKS) == 0 and MS * BT == NU and LEAD % MS == 0
assert STEPS % NPB == 0 and QH * STEPS % len(EBANKS) == 1

IN_B, SYM_B, DWA_B, PW_B, HA_B, HB_B, FU_B, NORM, BQ, BK = 0, 4, 6, 8, 10, 11, 12, 14, 15, 16
NVEC = 17
TURN_MIX, TURN_F1, TURN_QKV, TURN_F2 = (NCH * i for i in range(4))
TOK_MIX, TOK_F1, TOK_V, TOK_AO, TOK_F2 = [0, 1, 2, 3], [4, 5, 7, 9], [6, 8, 10, 11], [12, 13, 14, 15], [16, 17, 18, 19]
VAR0 = (0, 1, 1 + NCH, 1 + 2 * NCH)
WIDE_IN = 0
IN_ORDER = [(0, 2), (0, 3), (1, 2), (1, 3), (0, 0), (0, 1), (1, 0), (1, 1)]
WIDE_Y = WIDE_IN + 4 * NCH
WIDE_F1 = WIDE_Y + KC * NCH
WIDE_QK = WIDE_F1 + KH * NCH
WIDE_F2 = WIDE_QK + 2 * NCH


def exp_bank(n0, e, last):
    if not last or e < E_MORE:
        return EBANKS[(n0 + e) % 3], 3
    ring = [EBANKS[(n0 + E_MORE + i) % 3] for i in range(3)] + [4, 5]
    return ring[(e - E_MORE) % 5], 3 if e < E_MORE + 5 else 5


def build(nc, ins, out):
    x_d, norm_w, in_w, in_b, dwa_k, dwa_b, A_d, Bm_d, sym_k, sym_b, pw_w, pw_b, ha_w, ha_b, hb_w, hb_b, \
        fuse_w, fuse_b, out_w, out_b, qkv_w, qkv_b, ao_w, ao_b, fb_d, wfc_d, wproj_d, u_d, v_d, gate_d = ins
    ctx = ExitStack()
    with ctx:
        def sb(name, shape, dt=F32):
            return ctx.enter_context(nc.sbuf_tensor(name, shape, dt))

        def sem(name):
            return ctx.enter_context(nc.semaphore(name))

        in_n = sb("in_n", [P, 4, D])
        hb_n = sb("hb_n", [P, DI])
        ha_n = sb("ha_n", [P, DI])
        fu_n = sb("fu_n", [P, KC, DI])
        ow_n = sb("ow_n", [P, DI])
        bm_n = sb("bm_n", [DS, DI])
        pw_n = sb("pw_n", [P, KC, DI])
        a_n = sb("a_n", [P, KC, DS])
        kdwa = sb("kdwa", [P, KC, DC])
        ksym = sb("ksym", [P, KC, KS])
        qkv_n = sb("qkv_n", [P, 3, D])
        ao_n = sb("ao_n", [P, D])
        wfc_n = sb("wfc_n", [P, KH, D])
        wpr_n = sb("wpr_n", [P, HID])
        u_n = sb("u_n", [P, KH, RANK])
        v_n = sb("v_n", [RANK, D])
        fb_n = sb("fb_n", [RANK, RANK])
        gate_n = sb("gate_n", [RANK, 1])
        vec_n = sb("vec_n", [NVEC, P])
        ob_bc = sb("ob_bc", [P, D])
        bv_bc = sb("bv_bc", [P, D])
        aob_bc = sb("aob_bc", [P, D])
        ident = sb("ident", [P, P])
        vcol = sb("vcol", [P, NVEC])
        in_T = sb("in_T", [P, 4, D])
        hh_T = sb("hh_T", [P, 4, P])
        fu_T = sb("fu_T", [P, 2, DI])
        ob_T = sb("ob_T", [P, 2 * P + 2 * DS])
        att_T = sb("att_T", [P, 4, P])
        u_T = sb("u_T", [RANK, HID])
        wp_T = sb("wp_T", [P, KH, D])
        fc_T = sb("fc_T", [P, HID])
        z_s = sb("z_s", [RANK, HID])
        xy = sb("xy", [P, DI + DS])
        y1rep = sb("y1rep", [P, P])
        wb_T = sb("wb_T", [P, KC, DI])
        g_T = sb("g_T", [P, DI])
        ua = sb("ua", [P, KC, P])
        v1 = sb("v1", [DS, 1])
        v2 = sb("v2", [P, KC])
        v3 = sb("v3", [P, 1])
        w1 = sb("w1", [P, 1])
        cb = sb("cb", [P, KC])
        tern_fc = sb("tern_fc", [P, KH, D])
        tern_lo = sb("tern_lo", [P, HID])
        tern_pr = sb("tern_pr", [P, HID])
        tern_pl = sb("tern_pl", [P, HID])
        sc = sb("sc", [P, 4, KH + 1])
        x = sb("x", [P, NT, D])
        xr = sb("xr", [P, NT, D])
        h = sb("h", [P, NT, D])
        hT = sb("hT", [P, B * L])
        gate = sb("gate", [P, B, KC, L])
        val = sb("val", [P, B, KC, LP])
        acc = sb("acc", [P, B, KC, L])
        us = sb("us", [P, B, LP])
        st = sb("st", [P, 4, NT, 6])
        mv = sb("mv", [P, 4, NT, 2])
        small = sb("small", [P, 4, 8, NT])
        xr_c = sb("xr_c", [P, NT])
        r2_buf = acc[:, :, :, :].rearrange("p b k l -> p b (k l)").rearrange("p b (m c) -> p b m c", m=KH)
        gate_f = gate[:, :, :, :].rearrange("p b k l -> p (b k l)")
        val_h = val[:, :, :, :].rearrange("p b k l -> p (b k l)").bitcast(BF16)
        v_tok = us[:, :, :].rearrange("p b l -> p (b l)")[:, 0:NT * H * HD].rearrange("p (i d) -> p i d", i=NT)
        qt = [sb(f"qt{r}", [ROWS, 2, QH, CH], BF16)[:, :, :, :] for r in range(NBUF - 1)]
        kt = [sb(f"kt{r}", [ROWS, 2, QH, CH], BF16)[:, :, :, :] for r in range(NBUF - 1)]
        for i, buf in enumerate((qt, kt)):
            buf.append(val_h[0:ROWS, i * QH * L:(i + 1) * QH * L].rearrange("p (h j t) -> p h j t", h=2, j=QH))
        v4 = [sb(f"v4_{r}", [P, BT, QH, VW]) for r in range(NBUF)]
        ones_rows = xr[:, :, :].rearrange("p i d -> p (i d)").bitcast(BF16)[0:PARTS, :]
        pexp = [gate[:, 0, :, :], gate[:, 1, :, :], acc[:, 0, :, :], acc[:, 1, :, :]]
        pexp = [b.rearrange("p k l -> p (k l)").rearrange("p (j c) -> p j c", j=QH) for b in pexp]
        o_sb = sb("o_sb", [P, CH])
        o_rc = sb("o_rc", [P, TC, QH])
        attn = sb("attn", [P, NQ, HD, QH * BT])
        relu = gate_f[:, 0:NR * CH].rearrange("p (i c) -> p i c", i=NR)
        qk_r = gate_f[:, NR * CH:(NR + 2) * CH].rearrange("p (w c) -> p w c", w=2)
        attn_f = attn[:, :, :, :].rearrange("p n d w -> p (n d w)")
        qk_s = [attn_f[:, 0:PARTS * CH], gate_f[:, (NR + 2) * CH:(NR + 2 + PARTS) * CH]]
        qk_s = [b.bitcast(BF16).rearrange("p (w i c) -> p w i c", w=2, i=PARTS) for b in qk_s]
        u_rows = h[:, :, :].rearrange("p i d -> p (i d)").rearrange("p (b l) -> p b l", b=B)
        tap_bufs = [attn_f[:, i * CH:(i + 1) * CH] for i in range(4)]
        mx = sb("mx", [P, 2, HT, 2])
        mx_row = sb("mx_row", [P, HT])
        nm = sb("nm", [HT, P])
        nr = sb("nr", [HT, P])
        nm_s = sb("nm_s", [HT, PARTS, P], BF16)

        ps = [ctx.enter_context(nc.psum_tensor(f"ps{i}", [P, CH], F32)) for i in range(8)]

        def bank(i):
            return ps[i][:, :]

        def tap_buf(j):
            return tap_bufs[(j - 1) % 4]

        q_scr = nc.dram_tensor("q_scr", [PARTS, GQ * HD, NCH, QH, CH], BF16, kind="Internal").ap()
        k_scr = nc.dram_tensor("k_scr", [PARTS, GQ * HD, NCH, QH, CH], BF16, kind="Internal").ap()

        s_x = [sem(f"s_x{c}") for c in range(NCH)]
        s_w_in, s_w_taps, s_w_mix, s_vec = sem("s_w_in"), sem("s_w_taps"), sem("s_w_mix"), sem("s_vec")
        s_w_tern, s_w_ffn, s_w_att = sem("s_w_tern"), sem("s_w_ffn"), sem("s_w_att")
        ident_zero, ident_ready, pads_ready = sem("ident_zero"), sem("ident_ready"), sem("pads_ready")
        consts_ready, v4_zero, v4_ones = sem("consts_ready"), sem("v4_zero"), sem("v4_ones")
        dve_step, rc_ready, shift_step, xr_step = sem("dve_step"), sem("rc_ready"), sem("shift_step"), sem("xr_step")
        setup_mm, setup_ev, tern_ready, ua_ready = sem("setup_mm"), sem("setup_ev"), sem("tern_ready"), sem("ua_ready")
        us_in = [sem(f"us_in{b}") for b in range(B)]
        var_ready, std_ready, xn_ready = sem("var_ready"), sem("std_ready"), sem("xn_ready")
        xr_coef, xr_ready = sem("xr_coef"), sem("xr_ready")
        turn_mm, turned = sem("turn_mm"), sem("turned")
        wide_mm, wide_read = sem("wide_mm"), sem("wide_read")
        tok_mm, tok_read = sem("tok_mm"), sem("tok_read")
        u_mm, u_read, conv_done, silu_done = sem("u_mm"), sem("u_read"), sem("conv_done"), sem("silu_done")
        tap_ready, tap_added = sem("tap_ready"), sem("tap_added")
        sq_ready = sem("sq_ready")
        part0_ready, part1_ready, split_ready = sem("part0_ready"), sem("part1_ready"), sem("split_ready")
        scr_done = [sem(f"scr_done{i}") for i in range(2)]
        qk_in = [sem(f"qk_in{r}") for r in range(NBUF)]
        shift_in, v4_ready = sem("shift_in"), sem("v4_ready")
        exp_mm, exp_done, pv_mm = sem("exp_mm"), sem("exp_done"), sem("pv_mm")
        o_copied = sem("o_copied")
        m_mm, m_read, rows_ready = sem("m_mm"), sem("m_read"), sem("rows_ready")
        shift_split = sem("shift_split")
        attn_flat = sem("attn_flat")
        ao_biased, stored = sem("ao_biased"), sem("stored")

        x_src = x_d.rearrange("b (i p) d -> p (b i) d", p=P)
        out_dst = out.rearrange("b (i p) d -> p (b i) d", p=P)
        vectors = [(at, v.rearrange("(m p) -> m p", p=P)) for at, v in (
            (IN_B, in_b), (SYM_B, sym_b), (DWA_B, dwa_b), (PW_B, pw_b), (HA_B, ha_b), (HB_B, hb_b), (FU_B, fuse_b),
            (NORM, norm_w))]
        q_k_biases = [(at, qkv_b.rearrange("(a h w d) -> w a h d", a=1, w=3, d=HD)[w]) for at, w in ((BQ, 0), (BK, 1))]
        block = ctx.enter_context(nc.Block())

        @block.sync
        def _(sp):
            for c in range(NCH):
                sp.dma_start(x[:, TC * c:TC * c + TC, :], x_src[:, TC * c:TC * c + TC, :]).then_inc(s_x[c], 16)
            for at, v in vectors[5:]:
                sp.dma_start(vec_n[at:at + v.shape[0], :], v).then_inc(s_vec, 16)
            for at, v in q_k_biases:
                sp.dma_start(vec_n[at:at + 1, :].rearrange("a (h d) -> a h d", d=HD), v).then_inc(s_vec, 16)
            for dst, src in ((ksym[:, :, :], sym_k.rearrange("(k p) o t -> p k (o t)", p=P)),
                             (a_n[:, :, :], A_d.rearrange("(k p) s -> p k s", p=P)),
                             (kdwa[:, :, :], dwa_k.rearrange("(k p) o t -> p k (o t)", p=P))):
                sp.dma_start(dst, src).then_inc(s_w_taps, 16)
            sp.dma_start(wfc_n[:, :, :], wfc_d.rearrange("(m p) d -> p m d", p=P)).then_inc(s_w_tern, 16)
            sp.dma_start(wpr_n[:, :], wproj_d).then_inc(s_w_tern, 16)
            for dst, src in ((pw_n[:, :, :], pw_w.rearrange("(k p) c -> p k c", p=P)), (hb_n[:, :], hb_w),
                             (ha_n[:, :], ha_w), (fu_n[:, :, :], fuse_w.rearrange("(k p) c -> p k c", p=P)),
                             (ow_n[:, :], out_w), (bm_n[:, :], Bm_d)):
                sp.dma_start(dst, src).then_inc(s_w_mix, 16)
            sp.dma_start(u_n[:, :, :], u_d.rearrange("(m p) r -> p m r", p=P)).then_inc(s_w_ffn, 16)
            sp.dma_start(v_n[:, :], v_d).then_inc(s_w_ffn, 16)
            sp.dma_start(fb_n[:, :], fb_d).then_inc(s_w_ffn, 16)
            sp.dma_start(gate_n[:, :], gate_d.broadcast_to([RANK, 1])).then_inc(s_w_ffn, 16)
            sp.wait_ge(pads_ready, 5)
            for b in range(B):
                sp.wait_ge(u_read, 2 * (b + 1))
                for t in range(DC):
                    at = PAD + 1 - t
                    sp.dma_start(us[32 * t:32 * t + 32, b, at:at + L],
                                 u_rows[32 * t:32 * t + 32, b, :]).then_inc(us_in[b], 16)

            def store_parts(c):
                for w, scr in ((0, q_scr), (1, k_scr)):
                    sp.wait_ge(split_ready, 2 * c + w + 1)
                    for i in range(PARTS):
                        sp.dma_start(scr[i, :, c, :, :].rearrange("x j t -> j x t"),
                                     qk_s[c % 2][:, w, i, :]).then_inc(scr_done[c % 2], 16)

            def load_quad(n):
                b, g = divmod(n, GQ)
                rows = slice(g * HD, (g + 1) * HD)
                for i in range(PARTS):
                    at = i * PARTS * HD
                    src = q_scr[i, rows, 2 * b:2 * b + 2, :, :].rearrange("d h j t -> d (h j t)")
                    dst = qt[n % NBUF][at:at + PARTS * HD, :, :, :].rearrange("x h j t -> x (h j t)")
                    sp.dma_start(dst, src.unsqueeze(0).broadcast_to([PARTS, HD, QH * L])).then_inc(qk_in[n % NBUF], 16)
                    src = k_scr[:, rows, 2 * b:2 * b + 2, :, :].rearrange("i d h j t -> i d (h j t)")
                    dst = kt[n % NBUF][at:at + PARTS * HD, :, :, :].rearrange("x h j t -> x (h j t)")
                    sp.dma_start(dst, src).then_inc(qk_in[n % NBUF], 16)

            def load_shift(hn):
                sp.wait_ge(shift_split, hn + 1)
                n, half = divmod(hn, 2)
                for i in range(PARTS):
                    dst = qt[n % NBUF][SHIFT_ROW + i:SHIFT_ROW + i + 1, half, :, :]
                    sp.dma_start(dst.rearrange("a j (k p) -> a (j k) p", p=P),
                                 nm_s[:, i, :]).then_inc(shift_in, 16)

            sp.wait_ge(consts_ready, 2 * NBUF + 1)
            for r in range(NBUF):
                sp.dma_start(kt[r][SHIFT_ROW:SHIFT_ROW + PARTS, :, :, :].rearrange("i h j t -> i (h j t)"),
                             ones_rows).then_inc(qk_in[r], 16)
            store_parts(0)
            store_parts(1)
            for i in range(2):
                sp.wait_ge(scr_done[i], STORED)
            load_quad(0)
            store_parts(2)
            store_parts(3)
            for n in range(1, NBUF):
                load_quad(n)
            load_shift(0)
            for n in range(NQ):
                if 1 <= n and n + 2 < NQ:
                    sp.wait_ge(exp_mm, STEPS * QH * n)
                    if n + 2 == GQ:
                        for i in range(2):
                            sp.wait_ge(scr_done[i], 2 * STORED)
                    load_quad(n + 2)
                load_shift(2 * n + 1)
                if n + 1 < NQ:
                    load_shift(2 * n + 2)
            for c in range(NCH):
                sp.wait_ge(tok_read, TOK_F2[c] + 1)
                sp.dma_start(out_dst[:, TC * c:TC * c + TC, :], x[:, TC * c:TC * c + TC, :]).then_inc(stored, 16)
            sp.wait_ge(stored, 16 * NCH)

        @block.gpsimd
        def _(pool):
            pool.memset(ident[:, :], 0.0).then_inc(ident_zero, 1)
            pool.wait_ge(ident_zero, 1)
            pool.affine_select(out=ident[:, :], in_=ident[:, :], compare_op=ALU.not_equal, fill=1.0, base=0,
                               pattern=[[-1, P]], channel_multiplier=1).then_inc(ident_ready, 1)
            for w in range(3):
                src = qkv_w.rearrange("(h w d) e -> w h d e", w=3, d=HD)[w]
                pool.dma_start(qkv_n[:, w, :], src).then_inc(s_w_att, 16)
            pool.dma_start(ao_n[:, :], ao_w).then_inc(s_w_att, 16)
            pool.dma_start(aob_bc[:, :], ao_b.rearrange("(a d) -> a d", a=1).broadcast_to([P, D])).then_inc(s_w_att, 16)
            pool.dma_start(ob_bc[:, :], out_b.rearrange("(a d) -> a d", a=1).broadcast_to([P, D])).then_inc(s_w_att, 16)
            src = qkv_b.rearrange("(a h w d) -> w a h d", a=1, w=3, d=HD)[2].broadcast_to([P, H, HD])
            pool.dma_start(bv_bc[:, :].rearrange("p (h d) -> p h d", d=HD), src).then_inc(s_w_att, 16)
            edges = val[:, :, :, :].rearrange("p b k l -> p (b k) l")
            pool.memset(edges[:, :, 0:PAD], 0.0).then_inc(pads_ready, 1)
            pool.memset(edges[:, :, PAD + L:LP], 0.0).then_inc(pads_ready, 1)
            pool.memset(us[:, :, :], 0.0).then_inc(pads_ready, 1)
            pool.memset(ua[:, :, :], 0.0).then_inc(pads_ready, 1)
            pool.memset(y1rep[:, :], 0.0).then_inc(pads_ready, 1)
            pool.wait_ge(xr_coef, 2)
            for i in range(NT):
                pool.tensor_scalar(xr[:, i, :], x[:, i, :], xr_c[:, i:i + 1], small[:, 0, 6, i:i + 1],
                                   ALU.mult, ALU.add).then_inc(xr_step, 1)
            pool.wait_ge(s_w_att, 16 * 7)
            for i in range(NT):
                pool.wait_ge(xr_step, i + 1)
                pool.tensor_tensor(xr[:, i, :], xr[:, i, :], ob_bc[:, :], ALU.add).then_inc(xr_ready, 1)
            for j in range(1, KS):
                pool.wait_ge(tap_ready, j + 1)
                if j > 1:
                    pool.wait_ge(tap_added, j - 1)
                dst = acc[:, B - 1, KC - 1, CH:L]
                pool.tensor_tensor(dst, dst, tap_buf(j), ALU.add).then_inc(tap_added, 1)
            pool.wait_ge(tok_read, TOK_MIX[-1] + 1)
            for r in range(NBUF):
                pool.memset(v4[r][:, :, :, :], 0.0).then_inc(v4_zero, 1)
            pool.wait_ge(v4_zero, NBUF)
            for r in range(NBUF):
                pool.memset(qt[r][64:ROWS, :, :, :].bitcast(F32), 0.0).then_inc(consts_ready, 1)
                pool.memset(kt[r][64:ROWS, :, :, :].bitcast(F32), 0.0).then_inc(consts_ready, 1)
            pool.wait_ge(consts_ready, 2 * NBUF)
            pool.memset(ones_rows, 1.0).then_inc(consts_ready, 1)
            pool.wait_ge(consts_ready, 2 * NBUF + 1)
            for r in range(NBUF):
                pool.memset(v4[r][:, :, :, HD:HD + 1], 1.0).then_inc(v4_ones, 1)
            pool.wait_ge(v4_ones, NBUF)
            for c in range(NCH):
                tiles = slice(TC * c, TC * (c + 1))
                pool.wait_ge(xn_ready, NCH * 2 + c + 1)
                pool.tensor_tensor(x[:, tiles, :], x[:, tiles, :],
                                   aob_bc[:, :].unsqueeze(1).broadcast_to([P, TC, D]), ALU.add).then_inc(ao_biased, 1)
                for w in range(2):
                    pool.wait_ge(part1_ready, 2 * c + w + 1)
                    parts = qk_s[c % 2][:, w, :, :]
                    pool.tensor_tensor(parts[:, 2, :], qk_r[:, w, :], parts[:, 1, :],
                                       ALU.subtract).then_inc(split_ready, 1)
            pool.wait_ge(tok_read, TOK_V[-1] + 1)
            def quad_v(n):
                b, g = divmod(n, GQ)
                if n >= NBUF:
                    pool.wait_ge(pv_mm, STEPS * (n - NBUF + 1))
                src = v_tok[:, b * BT:(b + 1) * BT, :].rearrange("p c (j g d) -> p g c j d", g=GQ, d=HD)
                pool.tensor_copy(v4[n % NBUF][:, :, :, 0:HD], src[:, g, :, :, :]).then_inc(v4_ready, 1)

            def split_shift(hn):
                pool.wait_ge(m_read, NEGATED[hn] + 1)
                if hn:
                    pool.wait_ge(shift_in, hn * SHIFT)
                pool.tensor_copy(nm_s[:, 0, :], nm[:, :]).then_inc(shift_step, 1)
                pool.wait_ge(shift_step, hn * 3 + 1)
                pool.tensor_tensor(nr[:, :], nm[:, :], nm_s[:, 0, :], ALU.subtract).then_inc(shift_step, 1)
                pool.wait_ge(shift_step, hn * 3 + 2)
                pool.tensor_copy(nm_s[:, 1, :], nr[:, :]).then_inc(shift_step, 1)
                pool.wait_ge(shift_step, hn * 3 + 3)
                pool.tensor_tensor(nm_s[:, 2, :], nr[:, :], nm_s[:, 1, :], ALU.subtract).then_inc(shift_split, 1)

            for n in range(NBUF):
                quad_v(n)
            split_shift(0)
            for n in range(NQ):
                if 1 <= n and n + 2 < NQ:
                    quad_v(n + 2)
                split_shift(2 * n + 1)
                if n + 1 < NQ:
                    split_shift(2 * n + 2)

        @block.scalar
        def _(act):
            act.dma_start(in_n[:, :, :], in_w.rearrange("(m p) d -> p m d", p=P)).then_inc(s_w_in, 16)
            for at, v in vectors[:5]:
                act.dma_start(vec_n[at:at + v.shape[0], :], v).then_inc(s_vec, 16)

            def root(f, lo, hi):
                act.activation(small[:, f, 1, lo:hi], small[:, f, 0, lo:hi], ACT.Sqrt).then_inc(std_ready, 1)

            def turn_copy(i):
                c = i % NCH
                act.wait_ge(turn_mm, i + 1)
                act.activation(hT[:, c * CH:(c + 1) * CH], bank(i % 2), ACT.Copy).then_inc(turned, 1)

            def ev(k, dst, src, func=ACT.Copy, **kw):
                act.wait_ge(setup_mm, k)
                act.activation(dst, src, func, **kw).then_inc(setup_ev, 1)

            def flat(w):
                return w[:, :, :].rearrange("p m o -> p (m o)")

            act.wait_ge(var_ready, 1)
            act.activation(small[:, 0, 2:4, :], small[:, 0, 0:2, :], ACT.Sqrt).then_inc(std_ready, 1)
            ev(1, vcol[:, :], bank(0)[:, 0:NVEC])
            act.wait_ge(setup_ev, 1)
            ev(2, flat(in_T), bank(1), ACT.Identity, scale=vcol[:, NORM:NORM + 1])
            for b in range(B):
                for q in range(2):
                    turn_copy(TURN_MIX + 2 * b + q)
                for at, (q, m) in enumerate(IN_ORDER):
                    i = WIDE_IN + b * len(IN_ORDER) + at
                    act.wait_ge(wide_mm, i + 1)
                    src, bias = bank(2 + i % 4), vcol[:, IN_B + m:IN_B + m + 1]
                    if m < KC:
                        act.activation(gate[:, b, m, q * CH:(q + 1) * CH], src, ACT.Sigmoid,
                                       bias=bias).then_inc(wide_read, 1)
                    else:
                        act.activation(val[:, b, m - KC, PAD + q * CH:PAD + (q + 1) * CH], src, ACT.Identity,
                                       bias=bias).then_inc(wide_read, 1)

            def causal_out(b):
                for q in range(2):
                    act.wait_ge(u_mm, 2 * b + q + 1)
                    act.activation(u_rows[:, b, q * CH:(q + 1) * CH], bank(6 + q), ACT.Copy).then_inc(u_read, 1)

            def tap(j):
                k, src = KC - 1, val[:, B - 1, KC - 1, j + CH:j + L]
                if j == 0:
                    act.activation(acc[:, B - 1, k, CH:L], src, ACT.Identity, scale=ksym[:, k, 0:1],
                                   bias=vcol[:, SYM_B + k:SYM_B + k + 1]).then_inc(tap_ready, 1)
                else:
                    if j > 4:
                        act.wait_ge(tap_added, j - 4)
                    act.activation(tap_buf(j), src, ACT.Identity, scale=ksym[:, k, j:j + 1]).then_inc(tap_ready, 1)

            def silu(b):
                for k in range(KC):
                    if (b, k) == (B - 1, KC - 1):
                        act.wait_ge(tap_added, KS - 1)
                        act.wait_ge(conv_done, 2 * KC * B - 1)
                    else:
                        act.wait_ge(conv_done, 2 * (KC * b + k + 1))
                    act.activation(acc[:, b, k, :], acc[:, b, k, :], ACT.Silu).then_inc(silu_done, 1)

            act.wait_ge(pads_ready, 5)
            act.wait_ge(s_w_taps, 16 * 3)
            act.wait_ge(wide_read, WIDE_IN + 8 * B)
            causal_out(0)
            ev(3, flat(hh_T), bank(2))
            ev(4, flat(fu_T), bank(3))
            ev(5, ob_T[:, :], bank(4)[:, 0:2 * P + 2 * DS])
            ev(6, flat(att_T), bank(5))
            tap(0)
            tap(1)
            causal_out(1)
            tap(2)
            ev(7, u_T[:, :], bank(6)[0:RANK, :])
            ev(8, flat(wp_T), bank(7))
            silu(0)
            tap(3)
            ev(9, xy[:, :], bank(0)[:, 0:DI + DS])
            ev(10, z_s[:, :], bank(1)[0:RANK, :], ACT.Identity, scale=gate_n[:, 0:1])
            ev(11, v1[:, :], bank(4)[0:DS, 0:1])
            act.wait_ge(setup_ev, 9)
            for t in range(DC):
                ins = act.activation(y1rep[:, 32 * t:32 * t + DS], xy[:, DI:DI + DS], ACT.Copy)
            ins.then_inc(setup_ev, 1)
            ev(12, flat(wb_T), bank(2))
            ev(13, g_T[:, :], bank(3)[:, 0:DI])
            tap(4)
            tap(5)
            tap(6)
            ev(14, fc_T[:, :], bank(6))
            ev(15, v2[:, :], bank(0)[:, 0:KC])
            tap(7)
            ev(16, w1[:, :], bank(1)[:, 0:1], ACT.Identity, bias=vcol[:, HB_B:HB_B + 1])
            ev(17, v3[:, :], bank(7)[:, 0:1], ACT.Identity, bias=vcol[:, HA_B:HA_B + 1])
            tap(8)
            for o in range(KC):
                act.wait_ge(setup_mm, 18)
                act.activation(cb[:, o:o + 1], bank(0)[:, o:o + 1], ACT.Identity,
                               bias=vcol[:, FU_B + o:FU_B + o + 1]).then_inc(setup_ev, 1)
            silu(1)

            def stds(f, c):
                act.wait_ge(var_ready, VAR0[f] + c + 1)
                root(f, TC * c, TC * (c + 1))

            def first_parts(c):
                for w in range(2):
                    i = WIDE_QK + 2 * c + w
                    act.wait_ge(wide_mm, i + 1)
                    if c >= 2:
                        act.wait_ge(scr_done[c % 2], STORED * (c // 2))
                    act.activation(qk_s[c % 2][:, w, 0, :], bank(2 + i % 4), ACT.Identity,
                                   bias=vcol[:, BQ + w:BQ + w + 1]).then_inc(part0_ready, 1)

            def second_parts(c):
                for w in range(2):
                    act.wait_ge(wide_read, WIDE_QK + 2 * c + w + 1)
                    act.activation(qk_s[c % 2][:, w, 1, :], qk_r[:, w, :], ACT.Copy).then_inc(part1_ready, 1)

            def rectify(c, wide0, sq0):
                for m in range(KH):
                    i, n = wide0 + KH * c + m, KH * c + m
                    act.wait_ge(wide_mm, i + 1)
                    if sq0 + n >= NR:
                        act.wait_ge(sq_ready, sq0 + n - NR + 1)
                    act.activation(relu[:, n % NR, :], bank(2 + i % 4), ACT.Relu).then_inc(wide_read, 1)

            stds(1, 0)
            stds(1, 1)
            turn_copy(TURN_F1)
            turn_copy(TURN_F1 + 1)
            stds(1, 2)
            rectify(0, WIDE_F1, 0)
            turn_copy(TURN_F1 + 2)
            stds(1, 3)
            rectify(1, WIDE_F1, 0)
            turn_copy(TURN_F1 + 3)
            stds(2, 0)
            rectify(2, WIDE_F1, 0)
            turn_copy(TURN_QKV)
            stds(2, 1)
            rectify(3, WIDE_F1, 0)
            first_parts(0)
            turn_copy(TURN_QKV + 1)
            second_parts(0)
            stds(2, 2)
            first_parts(1)
            second_parts(1)
            stds(2, 3)
            turn_copy(TURN_QKV + 2)
            first_parts(2)
            turn_copy(TURN_QKV + 3)
            second_parts(2)
            first_parts(3)
            second_parts(3)

            def copy_o(hn, turned_at):
                act.wait_ge(pv_mm, hn * BT + BT)
                if turned_at is not None:
                    act.wait_ge(m_mm, turned_at)
                act.activation(o_sb[:, :], bank(2), ACT.Copy).then_inc(o_copied, 1)

            def quad(n0, trip, first, last):
                n = trip * NBUF + n0
                for s in range(STEPS):
                    if not (first and s < NPB):
                        act.wait_ge(pv_mm, n * STEPS + (s - NPB + 1))
                    for j in range(QH):
                        act.wait_ge(exp_mm, n * (STEPS * QH) + (s * QH + j + 1))
                        act.activation(pexp[s % NPB][:, j, :], bank(exp_bank(n0, s * QH + j, last)[0]), ACT.Exp,
                                       scale=SCALE).then_inc(exp_done, 1)
                        if s == 1 and j == COPY_O_AFTER and not first:
                            copy_o(n * 2 - 1, n * MQ + (M0 - MQ + O_NUMBER[1] + 1))
                        if s == BT + 1 and j == COPY_O_AFTER:
                            copy_o(n * 2, None if first else n * MQ + (M0 + O_NUMBER[0] + 1))

            quad(0, 0, True, False)
            with act.Fori(0, 2) as i:
                for q in range(NBUF):
                    quad(1 + q, i, False, False)
            quad(NQ - 1, 0, False, True)
            copy_o(2 * NQ - 1, M0 + (NQ - 1) * MQ + O_NUMBER_LAST[1] + 1)
            stds(3, 0)
            stds(3, 1)
            turn_copy(TURN_F2)
            stds(3, 2)
            turn_copy(TURN_F2 + 1)
            stds(3, 3)
            for c in range(NCH):
                rectify(c, WIDE_F2, KH * NCH)
                if c + 2 < NCH:
                    turn_copy(TURN_F2 + c + 2)

        @block.vector
        def _(dve):
            steps = [0]

            def settled(ins):
                steps[0] += 1
                ins.then_inc(dve_step, 1)
                dve.wait_ge(dve_step, steps[0])

            def stats(f, lo, hi):
                for i in range(lo, hi):
                    ins = dve.bn_stats(st[:, f, i, :], x[:, i, :])
                    ins.then_inc(dve_step, 1)
                steps[0] += hi - lo
                dve.wait_ge(dve_step, steps[0])
                for i in range(lo, hi):
                    ins = dve.bn_aggr(mv[:, f, i, :], st[:, f, i, :])
                    ins.then_inc(dve_step, 1)
                steps[0] += hi - lo
                dve.wait_ge(dve_step, steps[0])
                dve.tensor_scalar(small[:, f, 0, lo:hi], mv[:, f, lo:hi, 1], EPS_LN, None,
                                  ALU.add).then_inc(var_ready, 1)

            def chunk_stats(f, c):
                stats(f, TC * c, TC * (c + 1))

            def norm(f, c):
                lo, hi = TC * c, TC * (c + 1)
                dve.wait_ge(std_ready, VAR0[f] + c + 1)
                settled(dve.reciprocal(small[:, f, 2, lo:hi], small[:, f, 1, lo:hi]))
                settled(dve.scalar_tensor_tensor(out=small[:, f, 3, lo:hi], in0=mv[:, f, lo:hi, 0], scalar=-1.0,
                                                 in1=small[:, f, 2, lo:hi], op0=ALU.mult, op1=ALU.mult))
                for i in range(lo, hi):
                    ins = dve.tensor_scalar(h[:, i, :], x[:, i, :], small[:, f, 2, i:i + 1],
                                            small[:, f, 3, i:i + 1], ALU.mult, ALU.add)
                    if i == hi - 1:
                        ins.then_inc(xn_ready, 1)

            for c in range(NCH):
                dve.wait_ge(s_x[c], 16)
                for i in range(TC * c, TC * (c + 1)):
                    dve.bn_stats(st[:, 0, i, :], x[:, i, :]).then_inc(dve_step, 1)
            steps[0] += NT
            for i in range(NT):
                dve.wait_ge(dve_step, steps[0] - NT + i + 1)
                dve.bn_aggr(mv[:, 0, i, :], st[:, 0, i, :]).then_inc(dve_step, 1)
            steps[0] += NT
            dve.wait_ge(dve_step, steps[0])
            settled(dve.tensor_scalar(small[:, 0, 0, :], mv[:, 0, :, 1], EPS_LN, None, ALU.add))
            dve.scalar_tensor_tensor(out=small[:, 0, 1, :], in0=small[:, 0, 0, :], scalar=EPS_RMS,
                                     in1=mv[:, 0, :, 1], op0=ALU.mult, op1=ALU.add).then_inc(var_ready, 1)
            dve.wait_ge(std_ready, 1)
            settled(dve.reciprocal(small[:, 0, 4:6, :], small[:, 0, 2:4, :]))
            settled(dve.scalar_tensor_tensor(out=small[:, 0, 7, :], in0=mv[:, 0, :, 0], scalar=-1.0,
                                             in1=small[:, 0, 5, :], op0=ALU.mult, op1=ALU.mult))
            for c in range(NCH):
                for i in range(TC * c, TC * (c + 1)):
                    ins = dve.tensor_scalar(h[:, i, :], x[:, i, :], small[:, 0, 5, i:i + 1],
                                            small[:, 0, 7, i:i + 1], ALU.mult, ALU.add)
                ins.then_inc(xn_ready, 1)
                if c == 1:
                    dve.tensor_scalar(xr_c[:, :], small[:, 0, 4, :], 1.0, None, ALU.add).then_inc(xr_coef, 1)
                    dve.scalar_tensor_tensor(out=small[:, 0, 6, :], in0=mv[:, 0, :, 0], scalar=-1.0,
                                             in1=small[:, 0, 4, :], op0=ALU.mult, op1=ALU.mult).then_inc(xr_coef, 1)

            dve.wait_ge(s_w_taps, 16 * 3)
            dve.wait_ge(pads_ready, 5)
            for k in range(KC):
                for t in range(DC):
                    ins = dve.tensor_scalar(ua[:, k, 32 * t:32 * t + DS], a_n[:, k, :], kdwa[:, k, t:t + 1], None,
                                            ALU.mult)
            ins.then_inc(ua_ready, 1)

            dve.wait_ge(s_w_tern, 16 * 2)
            wfc = wfc_n[:, :, :]
            dve.tensor_reduce(sc[:, 0, 0:KH], wfc, AX.X, ALU.add,
                              apply_absolute_value=True).then_inc(dve_step, 1)
            steps[0] += 1
            settled(dve.tensor_reduce(sc[:, 0, KH:KH + 1], wpr_n[:, :], AX.X, ALU.add, apply_absolute_value=True))
            dve.tensor_scalar(sc[:, 1, 0:KH], sc[:, 0, 0:KH], 1.0 / D, 1e-5, ALU.mult, ALU.max).then_inc(dve_step, 1)
            steps[0] += 1
            settled(dve.tensor_scalar(sc[:, 1, KH:KH + 1], sc[:, 0, KH:KH + 1], 1.0 / HID, 1e-5, ALU.mult, ALU.max))
            dve.tensor_scalar(sc[:, 2, :], sc[:, 1, :], 0.5, None, ALU.mult).then_inc(dve_step, 1)
            dve.tensor_scalar(sc[:, 3, :], sc[:, 1, :], -0.5, None, ALU.mult).then_inc(dve_step, 1)
            steps[0] += 2
            dve.wait_ge(dve_step, steps[0])
            pairs = [(wfc_n[:, m, :], tern_fc[:, m, :], tern_lo[:, m * D:(m + 1) * D], m) for m in range(KH)]
            pairs.append((wpr_n[:, :], tern_pr[:, :], tern_pl[:, :], KH))
            for w, hi, lo, m in pairs:
                dve.tensor_scalar(hi, w, sc[:, 2, m:m + 1], sc[:, 1, m:m + 1], ALU.is_gt,
                                  ALU.mult).then_inc(dve_step, 1)
                dve.tensor_scalar(lo, w, sc[:, 3, m:m + 1], sc[:, 1, m:m + 1], ALU.is_lt,
                                  ALU.mult).then_inc(dve_step, 1)
            steps[0] += 2 * len(pairs)
            dve.wait_ge(dve_step, steps[0])
            dve.tensor_tensor(tern_fc[:, :, :].rearrange("p m d -> p (m d)"),
                              tern_fc[:, :, :].rearrange("p m d -> p (m d)"), tern_lo[:, :],
                              ALU.subtract).then_inc(tern_ready, 1)
            dve.tensor_tensor(tern_pr[:, :], tern_pr[:, :], tern_pl[:, :], ALU.subtract).then_inc(tern_ready, 1)

            def conv(b, streams):
                tap = {}
                for j in range(KS):
                    for k, lo, w in streams:
                        src, dst = val[:, b, k, j + lo:j + lo + w], acc[:, b, k, lo:lo + w]
                        if j == 0:
                            ins = dve.tensor_scalar(dst, src, ksym[:, k, 0:1], vcol[:, SYM_B + k:SYM_B + k + 1],
                                                    ALU.mult, ALU.add)
                        else:
                            dve.wait_ge(dve_step, tap[k, lo])
                            ins = dve.scalar_tensor_tensor(out=dst, in0=src, scalar=ksym[:, k, j:j + 1], in1=dst,
                                                           op0=ALU.mult, op1=ALU.add)
                        if j < KS - 1:
                            steps[0] += 1
                            tap[k, lo] = steps[0]
                            ins.then_inc(dve_step, 1)
                        else:
                            ins.then_inc(conv_done, 2 * w // L)

            def gated(b):
                for q in range(2):
                    for m in range(KC):
                        i = WIDE_Y + (2 * b + q) * KC + m
                        dve.wait_ge(wide_mm, i + 1)
                        dve.scalar_tensor_tensor(out=gate[:, b, m, q * CH:(q + 1) * CH], in0=bank(2 + i % 4),
                                                 scalar=cb[:, m:m + 1], in1=gate[:, b, m, q * CH:(q + 1) * CH],
                                                 op0=ALU.add, op1=ALU.mult).then_inc(wide_read, 1)

            def mixed(c):
                dve.wait_ge(tok_mm, TOK_MIX[c] + 1)
                dve.wait_ge(xr_ready, TC * (c + 1))
                add_tokens(TOK_MIX, c, xr)

            def add_tokens(tok, c, base):
                tiles = slice(TC * c, TC * (c + 1))
                dve.tensor_tensor(x[:, tiles, :].rearrange("p i d -> p (i d)"), bank(6 + tok[c] % 2),
                                  base[:, tiles, :].rearrange("p i d -> p (i d)"), ALU.add).then_inc(tok_read, 1)

            dve.wait_ge(setup_ev, 1)
            dve.wait_ge(wide_read, WIDE_IN + 4)
            conv(0, [(k, 0, L) for k in range(KC)])
            dve.wait_ge(wide_read, WIDE_IN + 8 + 4)
            conv(1, [(0, 0, CH), (0, CH, CH), (1, 0, CH)])
            dve.wait_ge(setup_ev, 20)
            gated(0)
            mixed(0)
            mixed(1)

            def squares(c, wide0, tok):
                for m in range(KH):
                    i = wide0 + KH * c + m
                    dve.wait_ge(wide_read, i + 1)
                    if c >= 2 and m == 0:
                        dve.wait_ge(tok_mm, tok[c - 2] + 1)
                    r = relu[:, (KH * c + m) % NR, :]
                    dve.tensor_tensor(r2_buf[:, c % 2, m, :], r, r, ALU.mult).then_inc(sq_ready, 1)

            def take_tokens(tok, c):
                dve.wait_ge(tok_mm, tok[c] + 1)
                add_tokens(tok, c, x)

            def qkv_out(c):
                tiles = slice(TC * c, TC * (c + 1))
                for w in range(2):
                    i = WIDE_QK + 2 * c + w
                    dve.wait_ge(part0_ready, 2 * c + w + 1)
                    if c:
                        dve.wait_ge(split_ready, 2 * (c - 1) + w + 1)
                    dve.scalar_tensor_tensor(out=qk_r[:, w, :], in0=bank(2 + i % 4),
                                             scalar=vcol[:, BQ + w:BQ + w + 1], in1=qk_s[c % 2][:, w, 0, :],
                                             op0=ALU.add, op1=ALU.subtract).then_inc(wide_read, 1)
                dve.wait_ge(tok_mm, TOK_V[c] + 1)
                dve.tensor_tensor(v_tok[:, tiles, :], bank(6 + TOK_V[c] % 2).rearrange("p (i d) -> p i d", d=D),
                                  bv_bc[:, :].unsqueeze(1).broadcast_to([P, TC, D]), ALU.add).then_inc(tok_read, 1)

            def mix_stats(c):
                dve.wait_ge(tok_read, TOK_MIX[c] + 1)
                chunk_stats(1, c)

            mix_stats(0)
            mix_stats(1)
            norm(1, 0)
            norm(1, 1)
            gated(1)
            mixed(2)
            mix_stats(2)
            norm(1, 2)
            mixed(3)
            mix_stats(3)
            squares(0, WIDE_F1, TOK_F1)
            norm(1, 3)
            for c in range(NCH):
                if c + 1 < NCH:
                    squares(c + 1, WIDE_F1, TOK_F1)
                if c >= 2:
                    qkv_out(c - 2)
                take_tokens(TOK_F1, c)
                dve.wait_ge(tok_read, TOK_F1[c] + 1)
                chunk_stats(2, c)
                norm(2, c)
            qkv_out(2)
            qkv_out(3)

            def unit_max(half, u, i, k):
                dve.wait_ge(m_mm, i + 1)
                dve.tensor_reduce(mx[:, half, u // 2, u % 2:u % 2 + 1], bank(MBANKS[k % 4]), AX.X,
                                  ALU.max).then_inc(m_read, 1)

            def row_max(half, i):
                dve.wait_ge(m_read, i)
                dve.tensor_tensor(mx_row[:, :], mx[:, half, :, 0], mx[:, half, :, 1], ALU.max).then_inc(rows_ready, 1)

            def negate(hn, i, k):
                dve.wait_ge(m_mm, i + 1)
                if not isinstance(hn, int) or hn >= 1:
                    dve.wait_ge(shift_split, hn)
                dve.tensor_scalar(nm[:, :], bank(MBANKS[k % 4])[0:HT, 0:P], -1.0, None,
                                  ALU.mult).then_inc(m_read, 1)

            def norm_o(n, half, i, k):
                dve.wait_ge(m_read, i)
                dve.wait_ge(m_mm, i + 1)
                o = bank(MBANKS[k % 4]).rearrange("p (c j w) -> p c j w", c=TC, j=QH)
                dve.reciprocal(o_rc[:, :, :], o[:, :, :, HD]).then_inc(rc_ready, 1)
                dve.wait_ge(rc_ready, n * 2 + (half + 1))
                quad_out = attn[:, n, :, :] if isinstance(n, int) else attn[:, bass.ds(n, 1), :, :].rearrange(
                    "p a d w -> p (a d) w")
                dst = quad_out.rearrange("p d (j c) -> p c j d", j=QH)[:, TC * half:TC * (half + 1), :, :]
                dve.tensor_tensor(dst, o[:, :, :, 0:HD], o_rc[:, :, :].unsqueeze(3).broadcast_to([P, TC, QH, HD]),
                                  ALU.mult).then_inc(m_read, 1)

            def maxima(hn, half, u, i, k, exist):
                if u == ROW_MAX_AT:
                    row_max(1 - half, i - u if exist else i)
                if u == TURN_MAX_AT:
                    negate(hn - 1, i, k)
                    i, k = i + 1, k + 1
                if exist:
                    unit_max(half, u, i, k)
                    k = k + 1
                return k

            def flatten(c, quads):
                b, q = divmod(c, 2)
                dst = h[:, TC * c:TC * (c + 1), :].rearrange("p d (j g w) -> p g d j w", j=QH, g=GQ)
                for g in quads:
                    src = attn[:, GQ * b + g, TC * q:TC * (q + 1), :].rearrange("p d (j w) -> p d j w", j=QH)
                    dve.tensor_copy(dst[:, g, :, :, :], src).then_inc(attn_flat, 1)

            def projected(c):
                dve.wait_ge(ao_biased, c + 1)
                take_tokens(TOK_AO, c)
                dve.wait_ge(tok_read, TOK_AO[c] + 1)
                chunk_stats(3, c)

            def quad(n, first, last):
                base = n * MQ + M0
                k = 1 if first else 0
                for s in range(STEPS):
                    half = s // BT
                    if s % BT == TURN_O_AT and not (first and half == 0):
                        norm_o(n if half else n - 1, 1 - half, base + k, k)
                        k += 1
                        if last and half:
                            projected(0)
                            projected(1)
                    if last and s == BT:
                        dve.wait_ge(m_read, base + k)
                        for c, quads in ((0, range(GQ)), (1, range(GQ)), (2, range(GQ - 1)), (3, range(GQ - 1))):
                            flatten(c, quads)
                    for m in range(MS):
                        h, u = divmod(NU + LEAD + s * MS + m, NU)
                        if not (last and h > 2):
                            k = maxima(n * 2 + h, h % 2, u, base + k, k, not (last and h == 2))

            for u in range(NU):
                unit_max(0, u, u, u)
            k = NU
            for u in range(LEAD):
                k = maxima(1, 1, u, k, k, True)
            quad(0, True, False)
            with dve.Fori(0, 2) as i:
                for q in range(NBUF):
                    quad(i * NBUF + (1 + q), False, False)
            quad(NQ - 1, False, True)
            norm_o(NQ - 1, 1, O_LAST, O_LAST)

            dve.wait_ge(m_read, O_LAST + 1)
            flatten(2, [GQ - 1])
            flatten(3, [GQ - 1])

            norm(3, 0)
            norm(3, 1)
            projected(2)
            projected(3)
            norm(3, 2)
            squares(0, WIDE_F2, TOK_F2)
            norm(3, 3)
            for c in range(NCH):
                if c + 1 < NCH:
                    squares(c + 1, WIDE_F2, TOK_F2)
                take_tokens(TOK_F2, c)

        @block.tensor
        def _(pe):
            pe.wait_ge(ident_ready, 1)
            pe.wait_ge(s_vec, 16 * 10)
            pe.transpose(bank(0)[:, 0:NVEC], vec_n[:, :], ident[0:NVEC, 0:NVEC]).then_inc(setup_mm, 1)
            pe.wait_ge(s_w_in, 16)
            for m in range(4):
                mm = pe.transpose(bank(1)[:, m * P:(m + 1) * P], in_n[:, m, :], ident[:, :])
            mm.then_inc(setup_mm, 1)
            def turn(i, src):
                if i >= 2:
                    pe.wait_ge(turned, i - 1)
                for t in range(TC):
                    mm = pe.transpose(bank(i % 2)[:, t * P:(t + 1) * P], src(t), ident[:, :])
                mm.then_inc(turn_mm, 1)

            def turn_h(f, i):
                c = i % NCH
                pe.wait_ge(xn_ready, f * NCH + c + 1)
                turn(i, lambda t: h[:, TC * c + t, :])

            def wide(i, pairs):
                if i >= 4:
                    pe.wait_ge(wide_read, i - 3)
                for k, (w, a) in enumerate(pairs):
                    mm = pe.matmul(bank(2 + i % 4), w, a, start=(k == 0), stop=(k == len(pairs) - 1))
                mm.then_inc(wide_mm, 1)

            def tokens(i, pairs):
                if i >= 2:
                    pe.wait_ge(tok_read, i - 1)
                for t in range(TC):
                    group = pairs(t)
                    for k, (a, w) in enumerate(group):
                        mm = pe.matmul(bank(6 + i % 2)[:, t * P:(t + 1) * P], a, w,
                                       start=(k == 0), stop=(k == len(group) - 1))
                mm.then_inc(tok_mm, 1)

            def causal(b):
                for q in range(2):
                    if b:
                        pe.wait_ge(u_read, 2 * (b - 1) + q + 1)
                    for k in range(KC):
                        mm = pe.matmul(bank(6 + q), ua[:, k, :], val[:, b, k, PAD + q * CH:PAD + (q + 1) * CH],
                                       start=(k == 0), stop=(k == KC - 1))
                    mm.then_inc(u_mm, 1)

            def y_mm(b, q, blocks=range(KC)):
                pe.wait_ge(us_in[b], 16 * DC)
                for m in blocks:
                    cols = slice(q * CH, (q + 1) * CH)
                    wide(WIDE_Y + (2 * b + q) * KC + m,
                         [(wb_T[:, k, m * P:(m + 1) * P], acc[:, b, k, cols]) for k in range(KC)]
                         + [(g_T[:, m * P:(m + 1) * P], us[:, b, PAD + q * CH:PAD + (q + 1) * CH])])

            pe.wait_ge(setup_ev, 2)
            for b in range(B):
                for q in range(2):
                    turn_h(0, TURN_MIX + 2 * b + q)
                for at, (q, m) in enumerate(IN_ORDER):
                    c = 2 * b + q
                    pe.wait_ge(turned, TURN_MIX + c + 1)
                    wide(WIDE_IN + b * len(IN_ORDER) + at, [(in_T[:, m, :], hT[:, c * CH:(c + 1) * CH])])
            pe.wait_ge(ua_ready, 1)
            pe.wait_ge(wide_read, WIDE_IN + 8 * B)
            causal(0)

            pe.wait_ge(s_w_mix, 16 * 6)
            for i, src in enumerate((hb_n, ha_n)):
                for k in range(KC):
                    at = (2 * i + k) * P
                    mm = pe.transpose(bank(2)[:, at:at + P], src[:, k * P:(k + 1) * P], ident[:, :])
            mm.then_inc(setup_mm, 1)
            for a in range(2):
                for o in range(KC):
                    at = a * DI + o * P
                    mm = pe.transpose(bank(3)[:, at:at + P], fu_n[:, o, a * P:(a + 1) * P], ident[:, :])
            mm.then_inc(setup_mm, 1)
            for k in range(KC):
                pe.transpose(bank(4)[:, k * P:(k + 1) * P], ow_n[:, k * P:(k + 1) * P], ident[:, :])
                at = 2 * P + k * DS
                mm = pe.transpose(bank(4)[:, at:at + DS], bm_n[:, k * P:(k + 1) * P], ident[0:DS, 0:DS])
            mm.then_inc(setup_mm, 1)
            pe.wait_ge(s_w_att, 16 * 7)
            for w in range(3):
                pe.transpose(bank(5)[:, w * P:(w + 1) * P], qkv_n[:, w, :], ident[:, :])
            pe.transpose(bank(5)[:, 3 * P:4 * P], ao_n[:, :], ident[:, :]).then_inc(setup_mm, 1)
            causal(1)
            pe.wait_ge(u_read, 2 * B)
            pe.wait_ge(s_w_ffn, 16 * 4)
            for m in range(KH):
                mm = pe.transpose(bank(6)[0:RANK, m * P:(m + 1) * P], u_n[:, m, :], ident[:, :])
            mm.then_inc(setup_mm, 1)
            pe.wait_ge(tern_ready, 2)
            for m in range(KH):
                mm = pe.transpose(bank(7)[:, m * P:(m + 1) * P], tern_pr[:, m * P:(m + 1) * P], ident[:, :])
            mm.then_inc(setup_mm, 1)
            pe.wait_ge(setup_ev, 5)
            for k in range(KC):
                pe.matmul(bank(0)[:, 0:DI], hh_T[:, k, :], pw_n[:, k, :], start=(k == 0), stop=(k == KC - 1))
            for k in range(KC):
                mm = pe.matmul(bank(0)[:, DI:DI + DS], hh_T[:, KC + k, :], ob_T[:, DI + k * DS:DI + (k + 1) * DS],
                               start=(k == 0), stop=(k == KC - 1))
            mm.then_inc(setup_mm, 1)
            pe.wait_ge(setup_ev, 7)
            pe.matmul(bank(1)[0:RANK, :], fb_n[:, :], u_T[:, :], start=True, stop=True).then_inc(setup_mm, 1)
            for k in range(KC):
                mm = pe.matmul(bank(4)[0:DS, 0:1], a_n[:, k, :], vcol[:, DWA_B + k:DWA_B + k + 1],
                               start=(k == 0), stop=(k == KC - 1))
            mm.then_inc(setup_mm, 1)
            pe.wait_ge(setup_ev, 9)
            for k in range(KC):
                mm = pe.matmul(bank(2)[:, k * DI:(k + 1) * DI], xy[:, k * P:(k + 1) * P], fu_T[:, 1, :],
                               start=True, stop=True)
            mm.then_inc(setup_mm, 1)
            pe.wait_ge(setup_ev, 12)
            pe.matmul(bank(3)[:, 0:DI], y1rep[:, :], fu_T[:, 0, :], start=True, stop=True).then_inc(setup_mm, 1)
            pe.wait_ge(setup_ev, 14)
            pe.wait_ge(silu_done, KC)
            y_mm(0, 0, [0])
            pe.matmul(bank(6), v_n[:, :], z_s[:, :], start=True, stop=False)
            for m in range(KH):
                mm = pe.matmul(bank(6)[:, m * P:(m + 1) * P], tern_fc[:, m, :], ident[:, :], start=False,
                               stop=(m == KH - 1))
            mm.then_inc(setup_mm, 1)
            y_mm(0, 0, [1])
            for k in range(KC):
                mm = pe.matmul(bank(0)[:, k:k + 1], bm_n[:, k * P:(k + 1) * P], v1[:, :], start=True, stop=True)
            mm.then_inc(setup_mm, 1)
            for k in range(KC):
                mm = pe.matmul(bank(1)[:, 0:1], hh_T[:, k, :], vcol[:, PW_B + k:PW_B + k + 1],
                               start=(k == 0), stop=(k == KC - 1))
            mm.then_inc(setup_mm, 1)
            y_mm(0, 1, [0])
            pe.wait_ge(setup_ev, 16)
            for k in range(KC):
                mm = pe.matmul(bank(7)[:, 0:1], hh_T[:, KC + k, :], v2[:, k:k + 1],
                               start=(k == 0), stop=(k == KC - 1))
            mm.then_inc(setup_mm, 1)
            y_mm(0, 1, [1])
            pe.wait_ge(setup_ev, 18)
            for o in range(KC):
                pe.matmul(bank(0)[:, o:o + 1], fu_T[:, 0, o * P:(o + 1) * P], v3[:, :], start=True, stop=False)
                mm = pe.matmul(bank(0)[:, o:o + 1], fu_T[:, 1, o * P:(o + 1) * P], w1[:, :], start=False, stop=True)
            mm.then_inc(setup_mm, 1)
            pe.wait_ge(setup_ev, 20)

            for b in range(B):
                if b:
                    pe.wait_ge(silu_done, KC * (b + 1))
                    for q in range(2):
                        y_mm(b, q)
                    turn_h(1, TURN_F1)
                    turn_h(1, TURN_F1 + 1)
                for q in range(2):
                    pe.wait_ge(wide_read, WIDE_Y + (2 * b + q + 1) * KC)
                    tokens(TOK_MIX[2 * b + q],
                           lambda t: [(gate[:, b, k, q * CH + t * P:q * CH + (t + 1) * P], ob_T[:, k * P:(k + 1) * P])
                                      for k in range(KC)])

            def fc(c, turn0, wide0):
                pe.wait_ge(turned, turn0 + c + 1)
                for m in range(KH):
                    wide(wide0 + KH * c + m, [(fc_T[:, m * P:(m + 1) * P], hT[:, c * CH:(c + 1) * CH])])

            def proj(c, sq0, tok):
                pe.wait_ge(sq_ready, sq0 + KH * (c + 1))
                tokens(tok[c], lambda t: [(r2_buf[:, c % 2, m, t * P:(t + 1) * P], wp_T[:, m, :])
                                            for m in range(KH)])

            def qk(c):
                pe.wait_ge(turned, TURN_QKV + c + 1)
                for w in range(2):
                    wide(WIDE_QK + 2 * c + w, [(att_T[:, w, :], hT[:, c * CH:(c + 1) * CH])])

            def v(c):
                tokens(TOK_V[c], lambda t: [(hT[:, c * CH + t * P:c * CH + (t + 1) * P], att_T[:, 2, :])])

            fc(0, TURN_F1, WIDE_F1)
            turn_h(1, TURN_F1 + 2)
            fc(1, TURN_F1, WIDE_F1)
            proj(0, 0, TOK_F1)
            turn_h(1, TURN_F1 + 3)
            fc(2, TURN_F1, WIDE_F1)
            proj(1, 0, TOK_F1)
            turn_h(2, TURN_QKV)
            fc(3, TURN_F1, WIDE_F1)
            qk(0)
            v(0)
            turn_h(2, TURN_QKV + 1)
            proj(2, 0, TOK_F1)
            qk(1)
            v(1)
            proj(3, 0, TOK_F1)
            turn_h(2, TURN_QKV + 2)
            qk(2)
            v(2)
            turn_h(2, TURN_QKV + 3)
            qk(3)
            v(3)

            def m_free(i):
                if not isinstance(i, int) or i >= len(MBANKS):
                    pe.wait_ge(m_read, i - (len(MBANKS) - 1))

            def max_mm(r, half, u, i, k):
                (j, c), keys = divmod(u // 2, TC), u % 2
                m_free(i)
                pe.matmul(bank(MBANKS[k % 4]), qt[r][0:QK_ROWS, half, j, c * P:(c + 1) * P],
                          kt[r][0:QK_ROWS, keys, j, :], start=True, stop=True).then_inc(m_mm, 1)

            def turn_max(hn, i, k):
                pe.wait_ge(rows_ready, hn + 1)
                m_free(i)
                pe.transpose(bank(MBANKS[k % 4])[0:HT, 0:P], mx_row[:, :], ident[:, :]).then_inc(m_mm, 1)

            def turn_o(hn, i, k):
                pe.wait_ge(o_copied, hn + 1)
                m_free(i)
                for t in range(TC):
                    mm = pe.transpose(bank(MBANKS[k % 4])[:, t * P:(t + 1) * P], o_sb[:, t * P:(t + 1) * P],
                                      ident[:, :])
                mm.then_inc(m_mm, 1)

            def pv(r, n, s):
                pe.wait_ge(exp_done, n * (STEPS * QH) + QH * (s + 1))
                if s == 0:
                    pe.wait_ge(v4_ready, n + 1)
                hn = n * 2 + s // BT
                if s % BT == 0 and not (isinstance(n, int) and hn == 0):
                    pe.wait_ge(o_copied, hn)
                for j in range(QH):
                    mm = pe.matmul(bank(2)[VW * j:VW * (j + 1), :], v4[r][:, s % BT, j, :], pexp[s % NPB][:, j, :],
                                   start=(s % BT == 0), stop=(s % BT == BT - 1), tile_position=(0, VW * j))
                mm.then_inc(pv_mm, 1)

            def loads(n0, trip):
                return (trip + n0 // NBUF + 1) * (16 * 2 * PARTS) + 16

            def project(c):
                pe.wait_ge(attn_flat, (GQ, 2 * GQ, 4 * GQ - 1, 4 * GQ)[c])
                tokens(TOK_AO[c], lambda t: [(h[:, TC * c + t, :], att_T[:, 3, :])])

            def quad(n0, trip, first, last):
                n = trip * NBUF + n0
                r, nxt, prev = n0 % NBUF, (n0 + 1) % NBUF, (n0 - 1) % NBUF
                base = n * MQ + M0
                k = 1 if first else 0
                for s in range(STEPS):
                    half, tile = divmod(s, BT)
                    j = 0
                    if tile == 0:
                        pe.wait_ge(shift_in, (n * 2 + half) * SHIFT + SHIFT)
                    if tile == TURN_O_AT and not (first and half == 0):
                        turn_o(n * 2 + half - 1, base + k, k)
                        k += 1
                    if last and s * QH == E_MORE:
                        pe.wait_ge(m_read, base + k)
                    if last and s in PROJECT_AT:
                        pe.wait_ge(m_read, base + k)
                        project(PROJECT_AT.index(s))
                    for at, kind in enumerate(ORDER):
                        if kind == "e":
                            e = s * QH + j
                            at_bank, behind = exp_bank(n0, e, last)
                            if not first or e >= behind:
                                pe.wait_ge(exp_done, n * (STEPS * QH) + (e - behind + 1))
                            keys = kt[r][:, tile // TC, j, tile % TC * P:(tile % TC + 1) * P]
                            pe.matmul(bank(at_bank), keys,
                                      qt[r][:, half, j, :], start=True, stop=True).then_inc(exp_mm, 1)
                            j += 1
                        elif kind == "v" and s:
                            pv(r, n, s - 1)
                        elif kind == "v" and not first:
                            pv(prev, n - 1, STEPS - 1)
                        elif kind == "m":
                            h, u = divmod(NU + LEAD + s * MS + ORDER[:at].count("m"), NU)
                            if u == TURN_MAX_AT and not (last and h > 2):
                                turn_max(n * 2 + h - 1, base + k, k)
                                k += 1
                            if last and h >= 2:
                                continue
                            if h == 2 and u == 0:
                                pe.wait_ge(qk_in[nxt], loads(n0 + 1, trip))
                            max_mm(nxt if h >= 2 else r, h % 2, u, base + k, k)
                            k += 1

            pe.wait_ge(turned, TURN_QKV + NCH)
            pe.wait_ge(wide_read, WIDE_QK + 2 * NCH)
            pe.wait_ge(tok_read, TOK_V[-1] + 1)
            pe.wait_ge(qk_in[0], loads(0, 0))
            k = 0
            for u in range(NU + LEAD):
                if u == NU + TURN_MAX_AT:
                    turn_max(0, k, k)
                    k += 1
                max_mm(0, u // NU, u % NU, k, k)
                k += 1
            quad(0, 0, True, False)
            with pe.Fori(0, 2) as i:
                for q in range(NBUF):
                    quad(1 + q, i, False, False)
            quad(NQ - 1, 0, False, True)
            pv((NQ - 1) % NBUF, NQ - 1, STEPS - 1)
            pe.wait_ge(tok_read, TOK_AO[1] + 1)
            turn_o(2 * NQ - 1, O_LAST, O_LAST)

            project(2)
            turn_h(3, TURN_F2)
            project(3)
            turn_h(3, TURN_F2 + 1)
            fc(0, TURN_F2, WIDE_F2)
            for c in range(NCH):
                if c + 2 < NCH:
                    turn_h(3, TURN_F2 + c + 2)
                if c + 1 < NCH:
                    fc(c + 1, TURN_F2, WIDE_F2)
                proj(c, KH * NCH, TOK_F2)


_INS = ['L0_attn_a_x', 'L0_attn_a_norm_w', 'L0_attn_a_in_w', 'L0_attn_a_in_b', 'L0_attn_a_dwa_k', 'L0_attn_a_dwa_b',
        'L0_attn_a_A', 'L0_attn_a_Bm', 'L0_attn_a_sym_k', 'L0_attn_a_sym_b', 'L0_attn_a_pw_w', 'L0_attn_a_pw_b',
        'L0_attn_a_ha_w', 'L0_attn_a_ha_b', 'L0_attn_a_hb_w', 'L0_attn_a_hb_b', 'L0_attn_a_fuse_w',
        'L0_attn_a_fuse_b', 'L0_attn_a_out_w', 'L0_attn_a_out_b', 'L0_attn_b_qkv_w', 'L0_attn_b_qkv_b',
        'L0_attn_b_out_w', 'L0_attn_b_out_b', 'L0_ffn_fast_b', 'L0_ffn_w_fc', 'L0_ffn_w_proj', 'L0_ffn_u',
        'L0_ffn_v', 'L0_ffn_gate']


def kernel(**inputs):
    import numpy as np
    import concourse.bacc as bacc
    from concourse.bass_utils import run_bass_kernel_spmd

    nc = bacc.Bacc("TRN2", target_bir_lowering=False, num_devices=1)
    arrays, args = {}, []
    for name in _INS:
        a = np.ascontiguousarray(inputs[name])
        if a.ndim == 0:
            a = a.reshape(1, 1)
        arrays[f"in_{name}"] = a
        args.append(nc.dram_tensor(f"in_{name}", a.shape, mybir.dt.from_np(a.dtype), kind="ExternalInput").ap())
    out = nc.dram_tensor("out", (B, L, D), F32, kind="ExternalOutput").ap()
    build(nc, args, out)
    r = run_bass_kernel_spmd(nc, [arrays], core_ids=[0])
    return r.results[0]["out"]
```
